# Optimizing a Trainium2 kernel written in Bass

```python
import numpy as np
import jax
import jax.numpy as jnp

def _softmax(x, axis=-1):
    return jax.nn.softmax(x, axis=axis)

def _gelu(x):
    return jax.nn.gelu(x, approximate=True)

def _silu(x):
    return jax.nn.silu(x)

def _sigmoid(x):
    return jax.nn.sigmoid(x)

def _layernorm(x, axis=-1, eps=1e-05):
    m = jnp.mean(x, axis=axis, keepdims=True)
    v = jnp.var(x, axis=axis, keepdims=True)
    return (x - m) / jnp.sqrt(v + eps)

def _scatter_add(tgt, idx, src, axis=0):
    return tgt.at[idx].add(src)

def _segment_sum(src, seg, n):
    return jax.ops.segment_sum(src, seg, n)
kernel_name = 'mk_cond_seq_d2_seqx_r4_c0307a'

def setup_inputs(seed: int=0):
    np.random.seed(seed)
    _w = jnp.asarray

    def _rec_inputs():
        import jax
        import jax.numpy as jnp
        _rk = jax.random.key(seed)
        x = 1.648e-05 + 1 * jax.random.normal(jax.random.fold_in(_rk, 1), (64, 64, 288), jnp.float32)
        _lenS = 64 - jax.random.randint(jax.random.fold_in(_rk, 7), (64,), 0, max(1, 64 // 4) + 1, jnp.int32)
        _lenS2 = 64 - jax.random.randint(jax.random.fold_in(_rk, 8), (64,), 0, max(1, 64 // 4) + 1, jnp.int32)
        cond_1152 = 0.00914911 + 1.00357 * jax.random.normal(jax.random.fold_in(_rk, 11), (64, 288), jnp.float32)
        return (x, cond_1152)
    x, cond_1152 = _rec_inputs()

    def _L0_cond_setup():
        import jax, jax.numpy as jnp
        import numpy as np
        B, N, D = (8, 256, 288)
        H = 16
        HD = D // H
        HID = 4 * D
        EPS = 1e-06

        def _ln(x):
            mu = jnp.mean(x, axis=-1, keepdims=True)
            var = jnp.mean(jnp.square(x - mu), axis=-1, keepdims=True)
            return (x - mu) * jax.lax.rsqrt(var + EPS)

        def _modulate(x, shift, scale):
            return x * (1.0 + scale[:, None, :]) + shift[:, None, :]

        def _attn(x, w_qkv, b_qkv, w_proj, b_proj):
            b, n, d = x.shape
            qkv = (x @ w_qkv + b_qkv).reshape(b, n, 3, H, HD)
            q = qkv[:, :, 0].transpose(0, 2, 1, 3)
            k = qkv[:, :, 1].transpose(0, 2, 1, 3)
            v = qkv[:, :, 2].transpose(0, 2, 1, 3)
            scores = jnp.einsum('bhnd,bhmd->bhnm', q, k) * HD ** (-0.5)
            attn = jax.nn.softmax(scores, axis=-1)
            out = jnp.einsum('bhnm,bhmd->bhnd', attn, v)
            out = out.transpose(0, 2, 1, 3).reshape(b, n, d)
            return out @ w_proj + b_proj
        key = jax.random.key(seed)
        ks = jax.random.split(key, 12)
        s = 0.02
        return {'x': jax.random.normal(ks[0], (B, N, D), jnp.float32), 't_emb': jax.random.normal(ks[1], (B, D), jnp.float32), 'w_qkv': jax.random.normal(ks[2], (D, 3 * D), jnp.float32) * s, 'b_qkv': jax.random.normal(ks[3], (3 * D,), jnp.float32) * s, 'w_proj': jax.random.normal(ks[4], (D, D), jnp.float32) * s, 'b_proj': jax.random.normal(ks[5], (D,), jnp.float32) * s, 'w_fc1': jax.random.normal(ks[6], (D, HID), jnp.float32) * s, 'b_fc1': jax.random.normal(ks[7], (HID,), jnp.float32) * s, 'w_fc2': jax.random.normal(ks[8], (HID, D), jnp.float32) * s, 'b_fc2': jax.random.normal(ks[9], (D,), jnp.float32) * s, 'w_ada': jax.random.normal(ks[10], (D, 6 * D), jnp.float32) * s, 'b_ada': jax.random.normal(ks[11], (6 * D,), jnp.float32) * s}
    _L0_cond_all = _L0_cond_setup()
    _L0_cond_in = {k: v for k, v in _L0_cond_all.items() if k in ('w_qkv', 'b_qkv', 'w_proj', 'b_proj', 'w_fc1', 'b_fc1', 'w_fc2', 'b_fc2', 'w_ada', 'b_ada')}
    del _L0_cond_all

    def _L1_cond_setup():
        import jax, jax.numpy as jnp
        import numpy as np
        NUM_HEADS = 16
        NUM_EXPERTS = 4
        TOP_K = 2
        LN_EPS = 1e-06

        def _ln(h):
            mu = jnp.mean(h, axis=-1, keepdims=True)
            var = jnp.var(h, axis=-1, keepdims=True)
            return (h - mu) * jax.lax.rsqrt(var + LN_EPS)

        def _modulate(h, shift, scale):
            return h * (1.0 + scale[:, None, :]) + shift[:, None, :]
        key = jax.random.key(seed)
        ks = jax.random.split(key, 12)
        B, N, C = (8, 256, 288)
        H = 4 * C
        E = NUM_EXPERTS
        s = 0.02
        return {'x': jax.random.normal(ks[0], (B, N, C), jnp.float32), 'c': jax.random.normal(ks[1], (B, C), jnp.float32), 'w_adaln': jax.random.normal(ks[2], (C, 6 * C), jnp.float32) * s, 'b_adaln': jnp.zeros((6 * C,), jnp.float32), 'w_qkv': jax.random.normal(ks[3], (C, 3 * C), jnp.float32) * s, 'b_qkv': jnp.zeros((3 * C,), jnp.float32), 'w_proj': jax.random.normal(ks[4], (C, C), jnp.float32) * s, 'b_proj': jnp.zeros((C,), jnp.float32), 'w_gate': jax.random.normal(ks[5], (C, E), jnp.float32) * s, 'w1': jax.random.normal(ks[6], (E, C, H), jnp.float32) * s, 'b1': jnp.zeros((E, H), jnp.float32), 'w2': jax.random.normal(ks[7], (E, H, C), jnp.float32) * s, 'b2': jnp.zeros((E, C), jnp.float32)}
    _L1_cond_all = _L1_cond_setup()
    _L1_cond_in = {k: v for k, v in _L1_cond_all.items() if k in ('w_adaln', 'b_adaln', 'w_qkv', 'b_qkv', 'w_proj', 'b_proj', 'w_gate', 'w1', 'b1', 'w2', 'b2')}
    del _L1_cond_all
    return {'x': x, 'cond_1152': cond_1152, 'L0_cond_w_qkv': _L0_cond_in['w_qkv'], 'L0_cond_b_qkv': _L0_cond_in['b_qkv'], 'L0_cond_w_proj': _L0_cond_in['w_proj'], 'L0_cond_b_proj': _L0_cond_in['b_proj'], 'L0_cond_w_fc1': _L0_cond_in['w_fc1'], 'L0_cond_b_fc1': _L0_cond_in['b_fc1'], 'L0_cond_w_fc2': _L0_cond_in['w_fc2'], 'L0_cond_b_fc2': _L0_cond_in['b_fc2'], 'L0_cond_w_ada': _L0_cond_in['w_ada'], 'L0_cond_b_ada': _L0_cond_in['b_ada'], 'L1_cond_w_adaln': _L1_cond_in['w_adaln'], 'L1_cond_b_adaln': _L1_cond_in['b_adaln'], 'L1_cond_w_qkv': _L1_cond_in['w_qkv'], 'L1_cond_b_qkv': _L1_cond_in['b_qkv'], 'L1_cond_w_proj': _L1_cond_in['w_proj'], 'L1_cond_b_proj': _L1_cond_in['b_proj'], 'L1_cond_w_gate': _L1_cond_in['w_gate'], 'L1_cond_w1': _L1_cond_in['w1'], 'L1_cond_b1': _L1_cond_in['b1'], 'L1_cond_w2': _L1_cond_in['w2'], 'L1_cond_b2': _L1_cond_in['b2']}

def reference(x, cond_1152, L0_cond_w_qkv, L0_cond_b_qkv, L0_cond_w_proj, L0_cond_b_proj, L0_cond_w_fc1, L0_cond_b_fc1, L0_cond_w_fc2, L0_cond_b_fc2, L0_cond_w_ada, L0_cond_b_ada, L1_cond_w_adaln, L1_cond_b_adaln, L1_cond_w_qkv, L1_cond_b_qkv, L1_cond_w_proj, L1_cond_b_proj, L1_cond_w_gate, L1_cond_w1, L1_cond_b1, L1_cond_w2, L1_cond_b2):
    import jax
    import jax.numpy as jnp

    def _L0_cond_ref(x, t_emb, w_qkv, b_qkv, w_proj, b_proj, w_fc1, b_fc1, w_fc2, b_fc2, w_ada, b_ada):
        import jax, jax.numpy as jnp
        import numpy as np
        B, N, D = (8, 256, 288)
        H = 16
        HD = D // H
        HID = 4 * D
        EPS = 1e-06

        def _ln(x):
            mu = jnp.mean(x, axis=-1, keepdims=True)
            var = jnp.mean(jnp.square(x - mu), axis=-1, keepdims=True)
            return (x - mu) * jax.lax.rsqrt(var + EPS)

        def _modulate(x, shift, scale):
            return x * (1.0 + scale[:, None, :]) + shift[:, None, :]

        def _attn(x, w_qkv, b_qkv, w_proj, b_proj):
            b, n, d = x.shape
            qkv = (x @ w_qkv + b_qkv).reshape(b, n, 3, H, HD)
            q = qkv[:, :, 0].transpose(0, 2, 1, 3)
            k = qkv[:, :, 1].transpose(0, 2, 1, 3)
            v = qkv[:, :, 2].transpose(0, 2, 1, 3)
            scores = jnp.einsum('bhnd,bhmd->bhnm', q, k) * HD ** (-0.5)
            attn = jax.nn.softmax(scores, axis=-1)
            out = jnp.einsum('bhnm,bhmd->bhnd', attn, v)
            out = out.transpose(0, 2, 1, 3).reshape(b, n, d)
            return out @ w_proj + b_proj
        ada = jax.nn.silu(t_emb) @ w_ada + b_ada
        shift_a, scale_a, gate_a, shift_f, scale_f, gate_f = jnp.split(ada, 6, axis=-1)
        x = x + gate_a[:, None, :] * _attn(_modulate(_ln(x), shift_a, scale_a), w_qkv, b_qkv, w_proj, b_proj)
        h = _modulate(_ln(x), shift_f, scale_f)
        h = jax.nn.gelu(h @ w_fc1 + b_fc1, approximate=True) @ w_fc2 + b_fc2
        return x + gate_f[:, None, :] * h

    def _L1_cond_ref(x, c, w_adaln, b_adaln, w_qkv, b_qkv, w_proj, b_proj, w_gate, w1, b1, w2, b2):
        import jax, jax.numpy as jnp
        import numpy as np
        NUM_HEADS = 16
        NUM_EXPERTS = 4
        TOP_K = 2
        LN_EPS = 1e-06

        def _ln(h):
            mu = jnp.mean(h, axis=-1, keepdims=True)
            var = jnp.var(h, axis=-1, keepdims=True)
            return (h - mu) * jax.lax.rsqrt(var + LN_EPS)

        def _modulate(h, shift, scale):
            return h * (1.0 + scale[:, None, :]) + shift[:, None, :]
        B, N, C = x.shape
        nh = NUM_HEADS
        hd = C // nh
        mod = jax.nn.silu(c) @ w_adaln + b_adaln
        sh_msa, sc_msa, g_msa, sh_mlp, sc_mlp, g_mlp = jnp.split(mod, 6, axis=-1)
        h = _modulate(_ln(x), sh_msa, sc_msa)
        qkv = (h @ w_qkv + b_qkv).reshape(B, N, 3, nh, hd).transpose(2, 0, 3, 1, 4)
        q, k, v = (qkv[0], qkv[1], qkv[2])
        attn = jax.nn.softmax(jnp.einsum('bhqd,bhkd->bhqk', q, k) * hd ** (-0.5), axis=-1)
        o = jnp.einsum('bhqk,bhkd->bhqd', attn, v).transpose(0, 2, 1, 3).reshape(B, N, C)
        o = o @ w_proj + b_proj
        x = x + g_msa[:, None, :] * o
        xn = _modulate(_ln(x), sh_mlp, sc_mlp)
        xf = xn.reshape(-1, C)
        gate_logits = xf @ w_gate
        topk_logits, topk_idx = jax.lax.top_k(gate_logits, TOP_K)
        gates = jax.nn.softmax(topk_logits, axis=-1)
        cw = jnp.sum(jax.nn.one_hot(topk_idx, NUM_EXPERTS, dtype=xf.dtype) * gates[..., None], axis=1)
        hmid = jax.nn.gelu(jnp.einsum('tc,ech->eth', xf, w1) + b1[:, None, :], approximate=True)
        eo = jnp.einsum('eth,ehc->etc', hmid, w2) + b2[:, None, :]
        moe = jnp.einsum('te,etc->tc', cw, eo).reshape(B, N, C)
        return x + g_mlp[:, None, :] * moe
    x = _L0_cond_ref(x, cond_1152, L0_cond_w_qkv, L0_cond_b_qkv, L0_cond_w_proj, L0_cond_b_proj, L0_cond_w_fc1, L0_cond_b_fc1, L0_cond_w_fc2, L0_cond_b_fc2, L0_cond_w_ada, L0_cond_b_ada)
    x = _L1_cond_ref(x, cond_1152, L1_cond_w_adaln, L1_cond_b_adaln, L1_cond_w_qkv, L1_cond_b_qkv, L1_cond_w_proj, L1_cond_b_proj, L1_cond_w_gate, L1_cond_w1, L1_cond_b1, L1_cond_w2, L1_cond_b2)
    return x

_drawn_inputs = setup_inputs


def setup_inputs(seed=0):
    import zlib

    import numpy as np

    out = dict(_drawn_inputs(seed))
    spreads = {'L1_cond_b_adaln': (0.0, 0.437),
     'L1_cond_b_qkv': (0.0, 0.8),
     'L1_cond_b_proj': (0.0, 0.361),
     'L1_cond_b1': (0.0, 0.8),
     'L1_cond_b2': (0.0, 0.501)}
    factors = {'L0_cond_w_qkv': 8.0,
     'L0_cond_b_qkv': 8.0,
     'L0_cond_w_proj': 8.0,
     'L0_cond_b_proj': 8.0,
     'L0_cond_b_fc1': 31.724,
     'L0_cond_b_fc2': 8.0,
     'L0_cond_b_ada': 8.0,
     'L1_cond_w_qkv': 7.82,
     'L1_cond_w_proj': 5.273,
     'L1_cond_w_gate': 2.812,
     'L1_cond_w1': 2.695}
    for name, (base, spread) in spreads.items():
        noise = np.random.default_rng([zlib.crc32(name.encode()), seed]).standard_normal(out[name].shape)
        drawn = base * np.exp(spread * noise) if base else spread * noise
        out[name] = jnp.asarray(drawn.astype(out[name].dtype))
    for name, factor in factors.items():
        out[name] = (out[name] * factor).astype(out[name].dtype)
    return out
```

```python
import concourse.bass as bass
from concourse import mybir
from contextlib import ExitStack

F32 = mybir.dt.float32
F32R = mybir.dt.float32r
ALU = mybir.AluOpType
ACT = mybir.ActivationFunctionType
AX = mybir.AxisListType

P = 128
NSEQ, SEQ, D = 64, 64, 288
HEADS = 16
HD = D // HEADS
HID = 4 * D
EXPERTS = 4
TILES = NSEQ * SEQ // P
BLK = 2 * P
NB = NSEQ * SEQ // BLK
MCH = HID // P
EPS = 1e-6
LAYERS = 2
PASSES_MLP = 1 + EXPERTS
TAIL = D - 2 * P
REP = P // TAIL
XCOLS = 3 * P
GROUPS = [(0, 6), (6, 11), (11, 16)]
PAIRS = [(0, 0, P), (1, 1, P), (0, 2, P), (1, 3, P), (2, 0, P), (3, 1, P), (4, 4, 3 * TAIL)]
VW = HD + 1
ST_LN1, ST_QK, ST_SCORE, ST_PV, ST_PROJ, ST_LN2, ST_GATE = range(7)
DEPTH = ST_GATE


def build(nc, x, cond, w_qkv, b_qkv, w_proj, b_proj, w_up, b_up, w_down, b_down, w_ada, b_ada,
          w_gate, out):
    ctx = ExitStack()
    with ctx:
        def sb(name, shape, dt=F32):
            return ctx.enter_context(nc.sbuf_tensor(name, shape, dt))

        def sem(name):
            return ctx.enter_context(nc.semaphore(name))

        X = sb("X", [P, TILES, D])
        HT = sb("HT", [P, 3, TILES * P])
        hs = [sb(f"hs{i}", [P, 5, BLK], F32R) for i in range(2)]
        ident = sb("ident", [P, P])
        mods = [sb(f"mods{l}", [P, 4, 3, NSEQ]) for l in range(LAYERS)]
        head_mask = sb("head_mask", [P, HEADS])
        mhalf = sb("mhalf", [P, 2])
        gate_bc = [sb(f"gate_bc{i}", [P, 2, D]) for i in range(2)]
        y = [sb(f"y{t}", [P, D]) for t in range(2)]
        bproj_bc = sb("bproj_bc", [P, D])
        bqk = sb("bqk", [P, 6])
        logits = sb("logits", [P, TILES, EXPERTS])
        cw = sb("cw", [P, TILES, EXPERTS])
        wg = sb("wg", [P, 3, EXPERTS])
        stats = [sb(f"stats{k}", [P, 2, 6]) for k in range(2)]
        meanvar = [sb(f"meanvar{k}", [P, 2, 2]) for k in range(2)]
        vareps = [sb(f"vareps{k}", [P, 2]) for k in range(2)]
        rstd = [sb(f"rstd{k}", [P, 2]) for k in range(2)]
        rowmax = [sb(f"rowmax{t}", [P, HEADS]) for t in range(2)]
        rden = [sb(f"rden{t}", [P, HEADS]) for t in range(2)]

        base = nc.sbuf_base
        top = nc.sbuf_usable_end

        class Region:
            def __init__(self, at):
                self.at = at

            def take(self, name, shape, dt=F32):
                n = 4
                for k in shape[1:]:
                    n *= k
                t = nc.alloc_sbuf_tensor_at(name, shape, dt, offset=self.at)
                self.at += (n + 31) // 32 * 32
                assert self.at <= top, (name, self.at, top)
                return t

        r = Region(base)
        raw1 = r.take("raw1", [P, 3 * HID])
        raw2_at = r.at
        raw2 = r.take("raw2", [P, MCH * D])
        shared = r.at
        ctx.enter_context(nc.sbuf_tensor("fence", [P, (top - base) // 4 - 64], F32))

        r = Region(raw2_at)
        prob = [r.take(f"prob{t}", [P, HEADS, SEQ]) for t in range(2)]
        o1 = r.take("o1", [P, XCOLS])
        assert r.at <= shared
        r = Region(base)
        probT = [r.take(f"probT{t}", [P, 8 * P]) for t in range(2)]
        os5 = r.take("os5", [P, 5, BLK], F32R)
        assert r.at <= raw2_at
        r = Region(shared)
        wqkv5 = r.take("wqkv5", [P, 5, 3 * D], F32R)
        wproj5 = r.take("wproj5", [P, 5, D], F32R)
        xn = [[r.take(f"xn{k}{t}", [P, XCOLS]) for t in range(2)] for k in range(2)]
        u = [[r.take(f"u{k}{t}", [P, 3, P]) for t in range(2)] for k in range(2)]
        qT = [r.take(f"qT{i}", [P, 3, BLK]) for i in range(2)]
        kT = r.take("kT", [P, 3, BLK])
        kbd = r.take("kbd", [P, HEADS, BLK])
        vbd = [r.take(f"vbd{i}", [P, 4, HEADS // 2, 2 * VW]) for i in range(2)]
        o = [r.take("o0", [P, XCOLS]), o1]
        oT = [r.take(f"oT{t}", [P, 3, P]) for t in range(2)]

        r = Region(shared)
        wup5 = r.take("wup5", [P, 5, HID], F32R)
        wdn = [r.take(f"wdn{i}", [P, MCH, D], F32R) for i in range(2)]
        gel = [r.take(f"gel{i}", [P, BLK]) for i in range(3)]
        gelu_hi = [r.take(f"gelu_hi{i}", [P, BLK], F32R) for i in range(3)]
        gelu_lo = [r.take(f"gelu_lo{i}", [P, BLK], F32R) for i in range(3)]
        bdown_bc = r.take("bdown_bc", [P, D])
        bup = r.take("bup", [P, MCH])
        rank = r.take("rank", [P, EXPERTS, TILES])
        cmp = r.take("cmp", [P, TILES])
        lmax = r.take("lmax", [P, TILES])
        esel = r.take("esel", [P, TILES, EXPERTS])
        esum = r.take("esum", [P, TILES])

        r = Region(shared)
        wada = r.take("wada", [P, 3, 6 * D])
        wadaC = r.take("wadaC", [P, 4, 4, P])
        bada = r.take("bada", [1, 6 * D])
        ones = r.take("ones", [P, P])
        cnd = r.take("cnd", [NSEQ, D])
        scond = r.take("scond", [NSEQ, D])
        scT = r.take("scT", [P, 3, NSEQ])
        gates_sb = [r.take(f"gates_sb{l}", [NSEQ, 2, D]) for l in range(LAYERS)]
        r = Region(base)
        bvB = r.take("bvB", [P, 3, P])
        bv = r.take("bv", [P, 3])
        bprow = r.take("bprow", [1, D])
        onesr = r.take("onesr", [P, P])

        gates_d = nc.dram_tensor("gates_d", (LAYERS, 2, NSEQ, D), F32).ap()

        scores = ctx.enter_context(nc.psum_tensor("scores", [P, 1024], F32))
        probT_ps = ctx.enter_context(nc.psum_tensor("probT_ps", [P, 1024], F32))
        gemm = [ctx.enter_context(nc.psum_tensor(f"gemm{i}", [P, 512], F32)) for i in range(2)]
        tbank = [ctx.enter_context(nc.psum_tensor(f"tbank{i}", [P, 512], F32)) for i in range(2)]
        up_ps = [scores[:, 0:BLK], scores[:, 512:512 + BLK], probT_ps[:, 0:BLK]]
        down_ps = [[gemm[0], gemm[1]], [tbank[0], tbank[1]]]

        x_in, cond_in, ada_in, wada_in, small_in, gates_out = map(sem, (
            "x_in", "cond_in", "ada_in", "wada_in", "small_in", "gates_out"))
        raw1_in, raw2_in, bias_in, out_done = map(sem, ("raw1_in", "raw2_in", "bias_in", "out_done"))
        gate_in = [sem(f"gate_in{i}") for i in range(2)]
        const_done, setup_pe, setup_act, setup_dve = map(sem, (
            "const_done", "setup_pe", "setup_act", "setup_dve"))
        w_hi, w_lo, bv_done, bv_mm, bp_done, vbd_init = map(sem, (
            "w_hi", "w_lo", "bv_done", "bv_mm", "bp_done", "vbd_init"))
        ln_stats, ln_mv, ln_ve, ln_rstd, ln_xn, ln_T, ln_u, ln_v = (
            [sem(f"{n}{k}") for k in range(2)] for n in (
                "ln_stats", "ln_mv", "ln_ve", "ln_rstd", "ln_xn", "ln_T", "ln_u", "ln_v"))
        h_hi, h_lo, ht_done = map(sem, ("h_hi", "h_lo", "ht_done"))
        qk_mm, qk_sb, v_mm, v_sb, kbd_done, kbd_act = map(sem, (
            "qk_mm", "qk_sb", "v_mm", "v_sb", "kbd_done", "kbd_act"))
        s_mm, s_max, s_sub, s_exp = map(sem, ("s_mm", "s_max", "s_sub", "s_exp"))
        pt_mm, pt_sb, pv_mm, o_rec, o_norm, o_full = map(sem, (
            "pt_mm", "pt_sb", "pv_mm", "o_rec", "o_norm", "o_full"))
        ot_mm, ot_sb, os_hi, os_lo, pj_mm, y_bias, y_gate, x_attn = map(sem, (
            "ot_mm", "ot_sb", "os_hi", "os_lo", "pj_mm", "y_bias", "y_gate", "x_attn"))
        lg_mm, lg_sb = map(sem, ("lg_mm", "lg_sb"))
        m_hi, m_lo, f1_mm, gelu_sb, g_hi, g_lo, f2_mm, z_bias, z_gate, x_mlp, route = map(sem, (
            "m_hi", "m_lo", "f1_mm", "gelu_sb", "g_hi", "g_lo", "f2_mm", "z_bias", "z_gate",
            "x_mlp", "route"))
        route_e, route_step = sem("route_e"), sem("route_step")

        def seven(pe, dst, stationary, moving, w_first):
            for n, (ws, xs, rows) in enumerate(PAIRS):
                a, b = (ws, xs) if w_first else (xs, ws)
                mm = pe.matmul(dst, stationary(a, rows), moving(b, rows),
                               start=(n == 0), stop=(n == len(PAIRS) - 1))
            return mm

        def load_raw1(eng, w, n):
            dst = raw1[:, 0:3 * n].rearrange("p (s n) -> p s n", s=3)
            eng.dma_start(dst[:, 0:2, :], w[0:2 * P, :].rearrange("(s p) n -> p s n", p=P)).then_inc(raw1_in, 16)
            for c in range(3):
                eng.dma_start(dst[c * TAIL:(c + 1) * TAIL, 2, :], w[2 * P:D, :]).then_inc(raw1_in, 16)

        def load_raw2_proj(eng, w):
            dst = raw2[:, 0:3 * D].rearrange("p (s n) -> p s n", s=3)
            eng.dma_start(dst[:, 0:2, :], w[0:2 * P, :].rearrange("(s p) n -> p s n", p=P)).then_inc(raw2_in, 16)
            for c in range(3):
                eng.dma_start(dst[c * TAIL:(c + 1) * TAIL, 2, :], w[2 * P:D, :]).then_inc(raw2_in, 16)

        def load_raw2_down(eng, w):
            eng.dma_start(raw2[:, :].rearrange("p (m n) -> p m n", m=MCH),
                          w.rearrange("(m p) n -> p m n", p=P)).then_inc(raw2_in, 16)

        RAW1_AT = [64 * (n + 1) for n in range(7)]
        RAW2_AT, tot = [], 0
        for n in range(7):
            tot += 64 if n in (0, 2) else 16
            RAW2_AT.append(tot)

        def phase_of_mlp(g):
            return 1 if g == 0 else 2 + g

        def ada_dve(l):
            return 1 + 15 * l

        def ada_pe(l):
            return 1 + 14 * l

        with nc.Block() as block:
            @block.sync
            def _(sp):
                sp.dma_start(cnd[:, :], cond).then_inc(cond_in, 16)
                for l in range(LAYERS):
                    if l:
                        sp.wait_ge(setup_pe, ada_pe(1))
                        sp.wait_ge(setup_dve, ada_dve(1))
                    sp.dma_start(wada[:, 0:2, :], w_ada[l][0:2 * P, :].rearrange("(s p) n -> p s n", p=P)).then_inc(wada_in, 16)
                    sp.dma_start(wada[0:TAIL, 2, :], w_ada[l][2 * P:D, :]).then_inc(wada_in, 16)
                    sp.dma_start(bada[:, :], b_ada[l].unsqueeze(0)).then_inc(wada_in, 16)
                    if l == 0:
                        for q in range(4):
                            sp.dma_start(X[:, 8 * q:8 * q + 8, :],
                                         x[1024 * q:1024 * q + 1024, :].rearrange("(t p) c -> p t c", p=P)).then_inc(x_in, 16)
                        load_raw1(sp, w_qkv[0], 3 * D)
                        load_raw2_proj(sp, w_proj[0])
                sp.dma_start(wg[:, 0:2, :], w_gate[0:2 * P, :].rearrange("(s p) n -> p s n", p=P)).then_inc(small_in, 16)
                sp.dma_start(wg[0:TAIL, 2, :], w_gate[2 * P:D, :]).then_inc(small_in, 16)
                for l in range(LAYERS):
                    sp.wait_ge(setup_dve, ada_dve(l) + 15)
                    sp.dma_start(gates_d[l].rearrange("g b c -> b g c"), gates_sb[l][:, :, :]).then_inc(gates_out, 16)
                sp.wait_ge(gates_out, 16 * LAYERS)
                sp.wait_ge(x_in, 64)
                sp.wait_ge(small_in, 32)

            @block.gpsimd
            def _(pool):
                pool.memset(ident[:, :], 0.0).then_inc(const_done, 1)
                pool.memset(head_mask[:, :], 1.0).then_inc(const_done, 1)
                pool.memset(ones[:, :], 1.0).then_inc(const_done, 1)
                pool.memset(mhalf[:, :], -0.5).then_inc(const_done, 1)
                pool.wait_ge(const_done, 4)
                pool.affine_select(out=ident[:, :], in_=ident[:, :], compare_op=ALU.not_equal, fill=1.0,
                                   base=0, pattern=[[-1, P]], channel_multiplier=1).then_inc(const_done, 1)
                n = 5
                for h0, h1 in GROUPS:
                    part = head_mask[:, h0:h1]
                    pool.affine_select(out=part, in_=part, compare_op=ALU.is_ge, fill=0.0,
                                       base=0, pattern=[[-HD, h1 - h0]], channel_multiplier=1).then_inc(const_done, 1)
                    n += 1
                    pool.wait_ge(const_done, n)
                    pool.affine_select(out=part, in_=part, compare_op=ALU.is_ge, fill=0.0,
                                       base=HD - 1, pattern=[[HD, h1 - h0]], channel_multiplier=-1).then_inc(const_done, 1)
                    n += 1

            @block.scalar
            def _(act):
                act.wait_ge(cond_in, 16)
                act.activation(scond[:, :], cnd[:, :], ACT.Silu).then_inc(setup_act, 1)

            @block.tensor
            def _(pe):
                pe.wait_ge(const_done, 11)
                pe.wait_ge(setup_act, 1)
                for s, (c0, c1) in enumerate(((0, P), (P, 2 * P), (2 * P, D))):
                    mm = pe.transpose(scores[0:c1 - c0, s * NSEQ:(s + 1) * NSEQ], scond[:, c0:c1], ident[0:NSEQ, 0:NSEQ])
                mm.then_inc(setup_pe, 1)
                for l in range(LAYERS):
                    pe.wait_ge(wada_in, 48 * (l + 1))
                    pe.wait_ge(setup_dve, ada_dve(l) + 1)
                    n = 0
                    for v, part in enumerate((0, 1, 3, 4)):
                        for s in range(3):
                            dst = gemm[n % 2][:, 0:NSEQ]
                            if n >= 2:
                                pe.wait_ge(setup_dve, ada_dve(l) + 1 + n - 1)
                            c0 = part * D + s * P
                            for k, rows in enumerate((P, P, TAIL)):
                                w = wada[0:rows, k, c0:c0 + P] if s < 2 else wadaC[0:rows, k, v, :]
                                pe.matmul(dst, w, scT[0:rows, k, :], start=(k == 0), stop=False)
                            w = bada[0:1, c0:c0 + P] if s < 2 else wadaC[0:1, 3, v, :]
                            pe.matmul(dst, w, ones[0:1, 0:NSEQ], start=False, stop=True).then_inc(setup_pe, 1)
                            n += 1
                    for q, part in enumerate((2, 5)):
                        dst = tbank[q][0:NSEQ, 0:D]
                        for k, rows in enumerate((P, P, TAIL)):
                            pe.matmul(dst, scT[0:rows, k, :], wada[0:rows, k, part * D:(part + 1) * D], start=(k == 0), stop=False)
                        pe.matmul(dst, ones[0:1, 0:NSEQ], bada[0:1, part * D:(part + 1) * D], start=False, stop=True).then_inc(setup_pe, 1)

            @block.vector
            def _(dve):
                dve.wait_ge(setup_pe, 1)
                dve.tensor_copy(scT[:, 0:2, :], scores[:, 0:2 * NSEQ].rearrange("p (s b) -> p s b", s=2))
                dve.tensor_copy(scT[0:TAIL, 2, :], scores[0:TAIL, 2 * NSEQ:3 * NSEQ]).then_inc(setup_dve, 1)
                for l in range(LAYERS):
                    dve.wait_ge(wada_in, 48 * (l + 1))
                    if l:
                        dve.wait_ge(setup_pe, ada_pe(1))
                        dve.wait_ge(setup_dve, ada_dve(1))
                    for v, part in enumerate((0, 1, 3, 4)):
                        c0 = part * D + 2 * P
                        for k, rows in enumerate((P, P, TAIL)):
                            dve.tensor_copy(wadaC[0:rows, k, v, :].rearrange("p (r c) -> p r c", r=REP),
                                            wada[0:rows, k, c0:c0 + TAIL].unsqueeze(1).to_broadcast([rows, REP, TAIL]))
                        last = dve.tensor_copy(wadaC[0:1, 3, v, :].rearrange("p (r c) -> p r c", r=REP),
                                               bada[0:1, c0:c0 + TAIL].unsqueeze(1).to_broadcast([1, REP, TAIL]))
                    last.then_inc(setup_dve, 1)
                    for n in range(12):
                        v, s = n // 3, n % 3
                        dve.wait_ge(setup_pe, ada_pe(l) + n + 1)
                        if v % 2:
                            dve.tensor_scalar(mods[l][:, v, s, :], gemm[n % 2][:, 0:NSEQ], 1.0, None, ALU.add).then_inc(setup_dve, 1)
                        else:
                            dve.tensor_copy(mods[l][:, v, s, :], gemm[n % 2][:, 0:NSEQ]).then_inc(setup_dve, 1)
                    for q in range(2):
                        dve.wait_ge(setup_pe, ada_pe(l) + 12 + q + 1)
                        dve.tensor_copy(gates_sb[l][:, q, :], tbank[q][0:NSEQ, 0:D]).then_inc(setup_dve, 1)

        W_AT = [0]
        BIAS_AT = [0]
        for ph in range(7):
            W_AT.append(W_AT[-1] + (4 if ph in (0, 2) else 3))
            BIAS_AT.append(BIAS_AT[-1] + (160 if ph in (0, 2) else 32))

        def ge(eng, s, value):
            if not isinstance(value, int) or value > 0:
                eng.wait_ge(s, value)

        def tile(b, t):
            return X[:, bass.ds(2 * b + t, 1), :].rearrange("p o c -> p (o c)")

        def slots(ap):
            return ap.rearrange("p (s q k) -> p s q k", s=3, q=2)

        def seq_mod(l, v, b, t):
            return mods[l][:, v, :, bass.ds(4 * b + 2 * t, 2)].unsqueeze(3).to_broadcast([P, 3, 2, SEQ])

        def gate_load(sp, l, q, b, parity):
            for half in range(2):
                src = gates_d[l, q].rearrange("(t h) c -> h t c", h=2)[half, bass.ds(2 * b, 2), :]
                sp.dma_start(gate_bc[parity][half * SEQ:(half + 1) * SEQ, :, :],
                             src.unsqueeze(0).to_broadcast([SEQ, 2, D])).then_inc(gate_in[parity], 16)

        def attention(l):
            ph = 2 * l
            L = NB * l
            nstage = ST_GATE + 1
            ORDER = ([(ST_GATE, lg_sb, 0)] if l else []) + [
                (ST_PROJ, ot_sb, 2 * L), (ST_PV, o_norm, 2 * L),
                (ST_PROJ, y_bias, 2 * L), (ST_LN2, ln_u[1], 2 * L)]

            def steps(eng, body):
                for s in range(DEPTH):
                    body(s // 2, s % 2, [0 <= s - k for k in range(nstage)])
                with eng.Fori(DEPTH // 2, NB // 2) as h:
                    for par in range(2):
                        body(h, par, [True] * nstage)
                for s in range(NB, NB + DEPTH):
                    body(s // 2, s % 2, [s - k < NB for k in range(nstage)])

            def blk(h, par, k):
                return 2 * h + (par - k), (par - k) % 2

            def tbank_free(pe, h, par, live, item, t):
                for back in range(4):
                    for j in reversed(range(item if back == 0 else len(ORDER))):
                        k, s, before = ORDER[j]
                        b = 2 * h + par - back - k
                        if isinstance(h, int):
                            if not 0 <= b < NB:
                                continue
                        pe.wait_ge(s, before + 2 * b + t + 1)
                        return

            with nc.Block() as block:
                @block.sync
                def _(sp):
                    for g, (h0, h1) in enumerate(GROUPS):
                        for q in range(2):
                            sp.dma_start(bqk[0:(h1 - h0) * HD, 3 * (1 - q) + g:3 * (1 - q) + g + 1],
                                         b_qkv[l][q * D + h0 * HD:q * D + h1 * HD].unsqueeze(1)).then_inc(bias_in, 16)
                    sp.wait_ge(w_lo, W_AT[ph] + 2)
                    for s in range(3):
                        rows = P if s < 2 else TAIL
                        sp.dma_start(bv[0:rows, s:s + 1], b_qkv[l][2 * D + s * P:2 * D + s * P + rows].unsqueeze(1)).then_inc(bias_in, 16)
                    sp.dma_start(bprow[:, :], b_proj[l].unsqueeze(0)).then_inc(bias_in, 16)
                    gate_load(sp, l, 0, 0, 0)
                    gate_load(sp, l, 0, 1, 1)
                    with sp.Fori(1, NB // 2) as h:
                        for par in range(2):
                            sp.wait_ge(x_attn, 2 * L + 2 * (2 * h + par - 2) + 2)
                            gate_load(sp, l, 0, 2 * h + par, par)

                @block.gpsimd
                def _(pool):
                    for i in range(2):
                        pool.memset(vbd[i][:, :, :, :], 0.0).then_inc(vbd_init, 1)
                    pool.wait_ge(vbd_init, 6 * l + 2)
                    for i in range(2):
                        pool.memset(vbd[i][0:SEQ, :, :, HD:HD + 1], 1.0).then_inc(vbd_init, 1)
                        pool.wait_ge(vbd_init, 6 * l + 3 + 2 * i)
                        pool.memset(vbd[i][SEQ:P, :, :, VW + HD:VW + HD + 1], 1.0).then_inc(vbd_init, 1)
                        pool.wait_ge(vbd_init, 6 * l + 4 + 2 * i)

                    def pow_rstd(k, b):
                        pool.wait_ge(ln_ve[k], L + b + 1)
                        pool.tensor_tensor(rstd[k][:, :], vareps[k][:, :], mhalf[:, :], ALU.pow).then_inc(ln_rstd[k], 1)

                    def shift(k, b):
                        for t in range(2):
                            pool.wait_ge(ln_u[k], 2 * L + 2 * b + t + 1)
                            ut = u[k][t][:, :, :].rearrange("p s (q k) -> p s q k", q=2)
                            pool.tensor_tensor(ut, ut, seq_mod(l, 2 * k, b, t), ALU.add).then_inc(ln_v[k], 1)

                    def body(h, par, live):
                        if live[ST_QK]:
                            shift(0, blk(h, par, ST_QK)[0])
                        if live[ST_LN1]:
                            pow_rstd(0, blk(h, par, ST_LN1)[0])
                        if live[ST_LN2]:
                            pow_rstd(1, blk(h, par, ST_LN2)[0])
                        if live[ST_QK]:
                            b, i = blk(h, par, ST_QK)
                            for t in range(2):
                                ts = slice(t * P, (t + 1) * P)
                                pool.wait_ge(h_hi, 4 * L + 4 * b + 2 * t + 2)
                                pool.tensor_tensor(hs[i][:, 2:4, ts], u[0][t][:, 0:2, :],
                                                   hs[i][:, 0:2, ts].bitcast(F32), ALU.subtract).then_inc(h_lo, 1)
                                pool.wait_ge(h_lo, 4 * L + 4 * b + 2 * t + 1)
                                pool.tensor_tensor(hs[i][TAIL:2 * TAIL, 4, ts], u[0][t][TAIL:2 * TAIL, 2, :],
                                                   hs[i][TAIL:2 * TAIL, 4, ts].bitcast(F32), ALU.subtract).then_inc(h_lo, 1)
                                pool.wait_ge(h_lo, 4 * L + 4 * b + 2 * t + 2)
                        if live[ST_PROJ]:
                            b, _ = blk(h, par, ST_PROJ)
                            for t in range(2):
                                ts = slice(t * P, (t + 1) * P)
                                pool.wait_ge(os_hi, 4 * L + 4 * b + 2 * t + 2)
                                pool.tensor_tensor(os5[:, 2:4, ts], oT[t][:, 0:2, :],
                                                   os5[:, 0:2, ts].bitcast(F32), ALU.subtract).then_inc(os_lo, 1)
                                pool.wait_ge(os_lo, 4 * L + 4 * b + 2 * t + 1)
                                pool.tensor_tensor(os5[TAIL:2 * TAIL, 4, ts], oT[t][TAIL:2 * TAIL, 2, :],
                                                   os5[TAIL:2 * TAIL, 4, ts].bitcast(F32), ALU.subtract).then_inc(os_lo, 1)
                                pool.wait_ge(os_lo, 4 * L + 4 * b + 2 * t + 2)
                            g, i = blk(h, par, ST_PROJ)
                            for t in range(2):
                                if t == 0:
                                    pool.wait_ge(gate_in[i], 256 * ph + 32 * (h + (par - ST_PROJ) // 2) + 32)
                                pool.wait_ge(y_bias, 2 * L + 2 * b + t + 1)
                                pool.tensor_tensor(y[t][:, :], y[t][:, :], gate_bc[i][:, t, :], ALU.mult).then_inc(y_gate, 1)
                                pool.wait_ge(y_gate, 2 * L + 2 * b + t + 1)
                                pool.tensor_tensor(tile(b, t), tile(b, t), y[t][:, :], ALU.add).then_inc(x_attn, 1)
                        if live[ST_LN2]:
                            shift(1, blk(h, par, ST_LN2)[0])
                    steps(pool, body)

                @block.scalar
                def _(act):
                    raw = raw1[:, 0:9 * D].rearrange("p (s n) -> p s n", s=3)
                    act.wait_ge(raw1_in, RAW1_AT[ph])
                    act.activation(wqkv5[:, 0:2, :], raw[:, 0:2, :], ACT.Copy).then_inc(w_hi, 1)
                    act.activation(wqkv5[0:3 * TAIL, 4, :], raw[0:3 * TAIL, 2, :], ACT.Copy).then_inc(w_hi, 1)
                    raw = raw2[:, 0:3 * D].rearrange("p (s n) -> p s n", s=3)
                    act.wait_ge(raw2_in, RAW2_AT[ph])
                    act.activation(wproj5[:, 0:2, :], raw[:, 0:2, :], ACT.Copy).then_inc(w_hi, 1)
                    act.activation(wproj5[0:3 * TAIL, 4, :], raw[0:3 * TAIL, 2, :], ACT.Copy).then_inc(w_hi, 1)
                    act.wait_ge(bias_in, BIAS_AT[ph] + 96)
                    act.wait_ge(vbd_init, 6 * (l + 1))

                    def body(h, par, live):
                        if live[ST_PV]:
                            b, _ = blk(h, par, ST_PV)
                            for t in range(2):
                                ge(act, pv_mm, 2 * L + 2 * (b - 1) + t + 1)
                                for c in range(2):
                                    act.wait_ge(pt_mm, 4 * L + 4 * b + 2 * t + c + 1)
                                    act.activation(probT[t][:, c * 512:(c + 1) * 512], probT_ps[:, c * 512:(c + 1) * 512],
                                                   ACT.Copy).then_inc(pt_sb, 1)
                        if live[ST_QK]:
                            b, i = blk(h, par, ST_QK)
                            ge(act, v_mm, 2 * L + 2 * (b - 2) + 2)
                            for t in range(2):
                                ts = slice(t * P, (t + 1) * P)
                                act.wait_ge(ln_v[0], 2 * L + 2 * b + t + 1)
                                act.activation(hs[i][:, 0:2, ts], u[0][t][:, 0:2, :], ACT.Copy).then_inc(h_hi, 1)
                                act.activation(hs[i][0:3 * TAIL, 4, ts], u[0][t][0:3 * TAIL, 2, :], ACT.Copy).then_inc(h_hi, 1)

                        def exps(t):
                            b, _ = blk(h, par, ST_SCORE)
                            act.wait_ge(s_sub, 2 * L + 2 * b + t + 1)
                            act.activation(prob[t][:, :, :], prob[t][:, :, :], ACT.Exp, scale=float(HD) ** -0.5).then_inc(s_exp, 1)
                        if live[ST_SCORE]:
                            exps(0)
                        if live[ST_PROJ]:
                            b, _ = blk(h, par, ST_PROJ)
                            for t in range(2):
                                ts = slice(t * P, (t + 1) * P)
                                ge(act, pj_mm, 2 * L + 2 * (b - 1) + t + 1)
                                act.wait_ge(ot_sb, 2 * L + 2 * b + t + 1)
                                act.activation(os5[:, 0:2, ts], oT[t][:, 0:2, :], ACT.Copy).then_inc(os_hi, 1)
                                act.activation(os5[0:3 * TAIL, 4, ts], oT[t][0:3 * TAIL, 2, :], ACT.Copy).then_inc(os_hi, 1)
                        if live[ST_GATE]:
                            b, _ = blk(h, par, ST_GATE)
                            for t in range(2):
                                act.wait_ge(ln_v[1], 2 * L + 2 * b + t + 1)
                                act.activation(HT[:, :, bass.ds(b * BLK + t * P, P)], u[1][t][:, :, :], ACT.Copy).then_inc(ht_done, 1)
                        if live[ST_QK]:
                            b, i = blk(h, par, ST_QK)
                            ge(act, s_mm, 2 * L + 2 * (b - 2) + 2)
                            for n in range(6):
                                g = n % 3
                                M = (GROUPS[g][1] - GROUPS[g][0]) * HD
                                if n < 2:
                                    ge(act, kbd_done, 2 * L + 2 * (b - 1) + g + 1)
                                act.wait_ge(qk_mm, 6 * L + 6 * b + n + 1)
                                dst = qT[i][0:M, g, :] if n >= 3 else kT[0:M, g, :]
                                act.activation(dst, gemm[n % 2][0:M, 0:BLK], ACT.Identity, bias=bqk[0:M, n:n + 1]).then_inc(qk_sb, 1)
                            ge(act, pv_mm, 2 * L + 2 * (b - 2) + 2)
                            for t in range(2):
                                act.wait_ge(v_mm, 2 * L + 2 * b + t + 1)
                                vals = gemm[t][:, 0:D].rearrange("p (h o d) -> p h o d", o=2, d=HD)
                                for half in range(2):
                                    for odd in range(2):
                                        act.activation(
                                            vbd[i][odd * SEQ:(odd + 1) * SEQ, 2 * t + half, :, odd * VW:odd * VW + HD],
                                            vals[half * SEQ:(half + 1) * SEQ, :, odd, :], ACT.Copy).then_inc(v_sb, 1)
                        if live[ST_SCORE]:
                            exps(1)
                        if live[ST_QK]:
                            b, _ = blk(h, par, ST_QK)
                            h0, h1 = GROUPS[2]
                            M = (h1 - h0) * HD
                            ge(act, s_mm, 2 * L + 2 * (b - 1) + 2)
                            act.wait_ge(qk_sb, 6 * L + 6 * b + 3)
                            for n in range(h0, h1):
                                act.activation(kbd[0:M, n, :], kT[0:M, 2, :], ACT.Copy,
                                               scale=head_mask[0:M, n:n + 1]).then_inc(kbd_act, 1)
                    steps(act, body)

                @block.vector
                def _(dve):
                    raw = raw1[:, 0:9 * D].rearrange("p (s n) -> p s n", s=3)
                    rawp = raw2[:, 0:3 * D].rearrange("p (s n) -> p s n", s=3)
                    for n, (w5, rw) in enumerate(((wqkv5, raw), (wproj5, rawp))):
                        dve.wait_ge(w_hi, W_AT[ph] + 2 * n + 1)
                        dve.tensor_tensor(w5[:, 2:4, :], rw[:, 0:2, :], w5[:, 0:2, :].bitcast(F32), ALU.subtract).then_inc(w_lo, 1)
                        dve.wait_ge(w_hi, W_AT[ph] + 2 * n + 2)
                        low = w5[2 * TAIL:3 * TAIL, 4, :]
                        dve.tensor_tensor(low, rw[2 * TAIL:3 * TAIL, 2, :], low.bitcast(F32), ALU.subtract).then_inc(w_lo, 1)
                    dve.wait_ge(bias_in, BIAS_AT[ph + 1])
                    dve.wait_ge(w_lo, W_AT[ph] + 4)
                    dve.memset(onesr[:, :], 1.0).then_inc(bv_done, 1)
                    dve.wait_ge(bv_done, 4 * l + 1)
                    for s in range(3):
                        rows = P if s < 2 else TAIL
                        dve.tensor_scalar(bvB[0:rows, s, :], onesr[0:rows, :], bv[0:rows, s:s + 1], None, ALU.mult).then_inc(bv_done, 1)
                    dve.wait_ge(bv_mm, l + 1)
                    dve.tensor_copy(bproj_bc[:, :], tbank[0][:, 0:D]).then_inc(bp_done, 1)

                    def ln_statistics(bs):
                        for k, b in bs.items():
                            for t in range(2):
                                if k:
                                    dve.wait_ge(x_attn, 2 * L + 2 * b + t + 1)
                                if k and t and 0 in bs:
                                    dve.wait_ge(ln_stats[0], 2 * L + 2 * bs[0] + 2)
                                dve.bn_stats(out=stats[k][:, t, :], in_=tile(b, t)).then_inc(ln_stats[k], 1)
                        for k, b in bs.items():
                            if len(bs) == 1:
                                dve.wait_ge(ln_stats[k], 2 * L + 2 * b + 2)
                            for t in range(2):
                                dve.bn_aggr(out=meanvar[k][:, t, :], in_=stats[k][:, t, :]).then_inc(ln_mv[k], 1)
                            if k == 0 and 1 in bs:
                                dve.wait_ge(ln_stats[1], 2 * L + 2 * bs[1] + 2)
                            dve.wait_ge(ln_mv[k], 2 * L + 2 * b + 2)
                            dve.tensor_scalar(vareps[k][:, :], meanvar[k][:, :, 1], EPS, None, ALU.add).then_inc(ln_ve[k], 1)

                    def ln_normalize(k, b):
                        dve.wait_ge(ln_rstd[k], L + b + 1)
                        for t in range(2):
                            ge(dve, ln_T[k], 2 * L + 2 * (b - 1) + t + 1)
                            dve.tensor_scalar(xn[k][t][:, 0:2 * P], X[:, bass.ds(2 * b + t, 1), 0:2 * P].rearrange("p o c -> p (o c)"),
                                              meanvar[k][:, t, 0:1], rstd[k][:, t:t + 1], ALU.subtract, ALU.mult).then_inc(ln_xn[k], 1)
                            dve.tensor_scalar(xn[k][t][:, 2 * P:XCOLS].rearrange("p (r c) -> p r c", r=REP),
                                              X[:, bass.ds(2 * b + t, 1), 2 * P:D].to_broadcast([P, REP, TAIL]),
                                              meanvar[k][:, t, 0:1], rstd[k][:, t:t + 1], ALU.subtract, ALU.mult).then_inc(ln_xn[k], 1)

                    def ln_scale(k, b):
                        for t in range(2):
                            if k == 0:
                                ge(dve, h_lo, 4 * L + 4 * (b - 1) + 2 * t + 2)
                            else:
                                ge(dve, ht_done, 2 * L + 2 * (b - 1) + t + 1)
                                if l:
                                    ge(dve, lg_mm, 2 * (b - 1) + t + 1)
                            dve.wait_ge(ln_T[k], 2 * L + 2 * b + t + 1)
                            dve.tensor_tensor(u[k][t][:, :, :].rearrange("p s (q k) -> p s q k", q=2),
                                              slots((tbank if k else gemm)[t][:, 0:3 * P]),
                                              seq_mod(l, 2 * k + 1, b, t), ALU.mult).then_inc(ln_u[k], 1)

                    def softmax_shift(b, t):
                        dve.wait_ge(s_mm, 2 * L + 2 * b + t + 1)
                        sc = scores[:, :].rearrange("p (h k) -> p h k", k=SEQ)
                        dve.tensor_reduce(out=rowmax[t][:, :], in_=sc, axis=AX.X, op=ALU.max).then_inc(s_max, 1)
                        dve.wait_ge(s_max, 2 * L + 2 * b + t + 1)
                        ge(dve, pt_mm, 4 * L + 4 * (b - 1) + 2 * t + 2)
                        dve.tensor_tensor(prob[t][:, :, :], sc, rowmax[t][:, :].unsqueeze(2).to_broadcast([P, HEADS, SEQ]),
                                          ALU.subtract).then_inc(s_sub, 1)

                    def body(h, par, live):
                        if live[ST_QK]:
                            ln_scale(0, blk(h, par, ST_QK)[0])
                        norms = {k: blk(h, par, st)[0] for k, st in enumerate((ST_LN1, ST_LN2)) if live[st]}
                        if norms:
                            ln_statistics(norms)
                        if live[ST_SCORE]:
                            softmax_shift(blk(h, par, ST_SCORE)[0], 0)
                        if l and live[ST_GATE]:
                            b, _ = blk(h, par, ST_GATE)
                            for t in range(2):
                                dve.wait_ge(lg_mm, 2 * b + t + 1)
                                dve.tensor_copy(logits[:, bass.ds(2 * b + t, 1), :].rearrange("p o e -> p (o e)"),
                                                tbank[t][:, 0:EXPERTS]).then_inc(lg_sb, 1)
                        if live[ST_PROJ]:
                            b, _ = blk(h, par, ST_PROJ)
                            for t in range(2):
                                ge(dve, os_lo, 4 * L + 4 * (b - 1) + 2 * t + 2)
                                dve.wait_ge(ot_mm, 2 * L + 2 * b + t + 1)
                                dve.tensor_copy(oT[t][:, :, :].rearrange("p s k -> p (s k)"), tbank[t][:, 0:3 * P]).then_inc(ot_sb, 1)
                        for k, b in norms.items():
                            ln_normalize(k, b)
                        if live[ST_SCORE]:
                            softmax_shift(blk(h, par, ST_SCORE)[0], 1)
                        if live[ST_PV]:
                            b, _ = blk(h, par, ST_PV)
                            for t in range(2):
                                dve.wait_ge(pv_mm, 2 * L + 2 * b + t + 1)
                                res = tbank[t][:, 0:HEADS * VW].rearrange("p (h d) -> p h d", d=VW)
                                dve.reciprocal(rden[t][:, :], res[:, :, HD]).then_inc(o_rec, 1)
                                dve.wait_ge(o_rec, 2 * L + 2 * b + t + 1)
                                ge(dve, ot_mm, 2 * L + 2 * (b - 1) + t + 1)
                                dve.tensor_tensor(o[t][:, 0:D].rearrange("p (h d) -> p h d", d=HD), res[:, :, 0:HD],
                                                  rden[t][:, :].unsqueeze(2).to_broadcast([P, HEADS, HD]), ALU.mult).then_inc(o_norm, 1)
                                dve.wait_ge(o_norm, 2 * L + 2 * b + t + 1)
                                dve.tensor_copy(o[t][:, D:XCOLS].rearrange("p (r c) -> p r c", r=REP - 1),
                                                o[t][:, 2 * P:D].unsqueeze(1).to_broadcast([P, REP - 1, TAIL])).then_inc(o_full, 1)
                        if live[ST_QK]:
                            b, _ = blk(h, par, ST_QK)
                            for g, (h0, h1) in enumerate(GROUPS[:2]):
                                M, nh = (h1 - h0) * HD, h1 - h0
                                dve.wait_ge(qk_sb, 6 * L + 6 * b + g + 1)
                                ge(dve, s_mm, 2 * L + 2 * (b - 1) + 2)
                                dve.tensor_tensor(kbd[0:M, h0:h1, :], kT[0:M, g, :].unsqueeze(1).to_broadcast([M, nh, BLK]),
                                                  head_mask[0:M, h0:h1].unsqueeze(2).to_broadcast([M, nh, BLK]),
                                                  ALU.mult).then_inc(kbd_done, 1)
                        if live[ST_PROJ]:
                            b, _ = blk(h, par, ST_PROJ)
                            for t in range(2):
                                ge(dve, x_attn, 2 * L + 2 * (b - 1) + t + 1)
                                dve.wait_ge(pj_mm, 2 * L + 2 * b + t + 1)
                                dve.tensor_tensor(y[t][:, :], tbank[t][:, 0:D], bproj_bc[:, :], ALU.add).then_inc(y_bias, 1)
                        if live[ST_LN2]:
                            ln_scale(1, blk(h, par, ST_LN2)[0])
                    steps(dve, body)

                @block.tensor
                def _(pe):
                    pe.wait_ge(bv_done, 4 * l + 4)
                    rawp = raw2[:, 0:3 * D].rearrange("p (s n) -> p s n", s=3)
                    for s, rows in enumerate((P, P, TAIL)):
                        pe.matmul(tbank[0][:, 0:D], bvB[0:rows, s, :], rawp[0:rows, s, :], start=(s == 0), stop=False)
                    pe.matmul(tbank[0][:, 0:D], onesr[0:1, :], bprow[0:1, :], start=False, stop=True).then_inc(bv_mm, 1)
                    pe.wait_ge(bp_done, l + 1)
                    pe.wait_ge(w_lo, W_AT[ph] + 4)
                    G0 = 1 if l else 0

                    def transposes(src, dst):
                        for s in range(3):
                            mm = pe.transpose(dst[:, s * P:(s + 1) * P], src[:, s * P:(s + 1) * P], ident[:, :])
                        return mm

                    def score(h, par, t):
                        b, i = blk(h, par, ST_SCORE)
                        ge(pe, s_sub, 2 * L + 2 * b + t)
                        pe.wait_ge(kbd_done, 2 * L + 2 * b + 2)
                        pe.wait_ge(kbd_act, 5 * L + 5 * b + 5)
                        for g, h0, h1 in ((0, 0, 6), (1, 6, 8), (1, 8, 11), (2, 11, 16)):
                            M = (GROUPS[g][1] - GROUPS[g][0]) * HD
                            for half in range(2):
                                js = slice((2 * t + half) * SEQ, (2 * t + half + 1) * SEQ)
                                mm = pe.matmul(scores[half * SEQ:(half + 1) * SEQ, h0 * SEQ:h1 * SEQ],
                                               qT[i][0:M, g, js], kbd[0:M, h0:h1, js], start=True, stop=True)
                        mm.then_inc(s_mm, 1)

                    def body(h, par, live):
                        if live[ST_SCORE]:
                            score(h, par, 0)
                        if live[ST_PV]:
                            b, _ = blk(h, par, ST_PV)
                            for t in range(2):
                                pe.wait_ge(s_exp, 2 * L + 2 * b + t + 1)
                                pairs = prob[t][:, :, :].rearrange("p h k -> p (h k)")
                                for c in range(2):
                                    ge(pe, pt_sb, 4 * L + 4 * b + 2 * t + c - 1)
                                    for q in range(4):
                                        n = 4 * c + q
                                        mm = pe.transpose(probT_ps[:, n * P:(n + 1) * P], pairs[:, n * P:(n + 1) * P], ident[:, :])
                                    mm.then_inc(pt_mm, 1)
                        if l and live[ST_GATE]:
                            b, _ = blk(h, par, ST_GATE)
                            for t in range(2):
                                pe.wait_ge(ln_v[1], 2 * L + 2 * b + t + 1)
                                tbank_free(pe, h, par, live, 0, t)
                                for s, rows in enumerate((P, P, TAIL)):
                                    mm = pe.matmul(tbank[t][:, 0:EXPERTS], u[1][t][0:rows, s, :], wg[0:rows, s, :],
                                                   start=(s == 0), stop=(s == 2))
                                mm.then_inc(lg_mm, 1)
                        if live[ST_PROJ]:
                            b, _ = blk(h, par, ST_PROJ)
                            for t in range(2):
                                pe.wait_ge(o_full, 2 * L + 2 * b + t + 1)
                                tbank_free(pe, h, par, live, G0, t)
                                transposes(o[t], tbank[t]).then_inc(ot_mm, 1)
                        if live[ST_SCORE]:
                            score(h, par, 1)
                        if live[ST_PV]:
                            b, i = blk(h, par, ST_PV)
                            pe.wait_ge(v_sb, 8 * L + 8 * b + 8)
                            for t in range(2):
                                pe.wait_ge(pt_sb, 4 * L + 4 * b + 2 * t + 2)
                                tbank_free(pe, h, par, live, G0 + 1, t)
                                for n in range(HEADS // 2):
                                    for half in range(2):
                                        mm = pe.matmul(tbank[t][half * SEQ:(half + 1) * SEQ, n * 2 * VW:(n + 1) * 2 * VW],
                                                       probT[t][:, n * P + half * SEQ:n * P + (half + 1) * SEQ],
                                                       vbd[i][:, 2 * t + half, n, :], start=True, stop=True)
                                mm.then_inc(pv_mm, 1)
                        if live[ST_QK]:
                            b, i = blk(h, par, ST_QK)
                            pe.wait_ge(h_lo, 4 * L + 4 * b + 4)
                            for n in range(6):
                                h0, h1 = GROUPS[n % 3]
                                M = (h1 - h0) * HD
                                c0 = (1 - n // 3) * D + h0 * HD
                                if n >= 2:
                                    pe.wait_ge(qk_sb, 6 * L + 6 * b + n - 1)
                                seven(pe, gemm[n % 2][0:M, 0:BLK], lambda s, r: wqkv5[0:r, s, c0:c0 + M],
                                      lambda s, r: hs[i][0:r, s, :], True).then_inc(qk_mm, 1)
                            for t in range(2):
                                pe.wait_ge(qk_sb, 6 * L + 6 * b + 4 + t + 1)
                                ts = slice(t * P, (t + 1) * P)
                                seven(pe, gemm[t][:, 0:D], lambda s, r: hs[i][0:r, s, ts],
                                      lambda s, r: wqkv5[0:r, s, 2 * D:3 * D], False).then_inc(v_mm, 1)
                        if live[ST_PROJ]:
                            b, _ = blk(h, par, ST_PROJ)
                            for t in range(2):
                                ts = slice(t * P, (t + 1) * P)
                                pe.wait_ge(os_lo, 4 * L + 4 * b + 2 * t + 2)
                                tbank_free(pe, h, par, live, G0 + 2, t)
                                seven(pe, tbank[t][:, 0:D], lambda s, r: os5[0:r, s, ts],
                                      lambda s, r: wproj5[0:r, s, :], False).then_inc(pj_mm, 1)
                        if live[ST_LN2]:
                            b, _ = blk(h, par, ST_LN2)
                            for t in range(2):
                                pe.wait_ge(ln_xn[1], 4 * L + 4 * b + 2 * t + 2)
                                tbank_free(pe, h, par, live, G0 + 3, t)
                                transposes(xn[1][t], tbank[t]).then_inc(ln_T[1], 1)
                        if live[ST_LN1]:
                            b, _ = blk(h, par, ST_LN1)
                            for t in range(2):
                                pe.wait_ge(ln_xn[0], 4 * L + 4 * b + 2 * t + 2)
                                if live[ST_QK]:
                                    pe.wait_ge(v_sb, 8 * L + 8 * (b - 1) + 4 * t + 4)
                                transposes(xn[0][t], gemm[t]).then_inc(ln_T[0], 1)
                    steps(pe, body)

        def mlp(g):
            l = min(g, 1)
            ph = phase_of_mlp(g)
            N = NB * g

            def steps(eng, body, tail):
                body(0, 0, True)
                body(1, 1, False)
                body(2, 0, False)
                with eng.Fori(2, NB // 2) as h:
                    body(2 * h - 1, 1, False)
                    body(2 * h, 0, False)
                body(NB - 1, 1, False)
                tail(NB - 1, 1)

            with nc.Block() as block:
                @block.sync
                def _(sp):
                    if g < 2:
                        load_raw1(sp, w_up[g], HID)
                        load_raw2_down(sp, w_down[g])
                    sp.dma_start(bup[:, :], b_up[g].rearrange("(m p) -> p m", p=P),
                                 allow_slow_non_contiguous=True).then_inc(bias_in, 16)
                    sp.dma_start(bdown_bc[:, :], b_down[g].unsqueeze(0).to_broadcast([P, D])).then_inc(bias_in, 16)
                    gate_load(sp, l, 1, 0, 0)
                    gate_load(sp, l, 1, 1, 1)
                    if ph < 6:
                        sp.wait_ge(w_lo, W_AT[ph] + 2)
                        if g == 0:
                            load_raw1(sp, w_qkv[1], 3 * D)
                        else:
                            load_raw1(sp, w_up[g + 1], HID)
                        sp.wait_ge(w_lo, W_AT[ph] + 3)
                        if g == 0:
                            load_raw2_proj(sp, w_proj[1])
                        else:
                            load_raw2_down(sp, w_down[g + 1])

                    def store(b):
                        sp.dma_start(out.rearrange("(t p) c -> p t c", p=P)[:, bass.ds(2 * b, 2), :],
                                     X[:, bass.ds(2 * b, 2), :]).then_inc(out_done, 16)
                    with sp.Fori(1, NB // 2) as h:
                        for par in range(2):
                            b = 2 * h + par
                            sp.wait_ge(x_mlp, 2 * N + 2 * (b - 2) + 2)
                            gate_load(sp, l, 1, b, par)
                            if g == PASSES_MLP - 1:
                                store(b - 2)
                    if g == PASSES_MLP - 1:
                        for b in (NB - 2, NB - 1):
                            sp.wait_ge(x_mlp, 2 * N + 2 * b + 2)
                            store(b)
                        sp.wait_ge(out_done, 16 * NB)

                @block.gpsimd
                def _(pool):
                    with pool.Fori(0, NB // 2) as h:
                        for par in range(2):
                            b = 2 * h + par
                            for t in range(2):
                                pool.wait_ge(z_gate, 2 * N + 2 * b + t + 1)
                                pool.tensor_tensor(tile(b, t), tile(b, t), y[t][:, :], ALU.add).then_inc(x_mlp, 1)

                @block.scalar
                def _(act):
                    raw = raw1[:, :].rearrange("p (s n) -> p s n", s=3)
                    act.wait_ge(raw1_in, RAW1_AT[ph])
                    act.activation(wup5[:, 0:2, :], raw[:, 0:2, :], ACT.Copy).then_inc(w_hi, 1)
                    act.activation(wup5[0:3 * TAIL, 4, :], raw[0:3 * TAIL, 2, :], ACT.Copy).then_inc(w_hi, 1)

                    def split(b, i):
                        ge(act, f1_mm, MCH * N + MCH * (b - 1))
                        cols = bass.ds(b * BLK, BLK)
                        act.activation(hs[i][:, 0:2, :], HT[:, 0:2, cols], ACT.Copy).then_inc(m_hi, 1)
                        act.activation(hs[i][0:3 * TAIL, 4, :], HT[0:3 * TAIL, 2, cols], ACT.Copy).then_inc(m_hi, 1)
                    split(0, 0)
                    act.wait_ge(raw2_in, RAW2_AT[ph])
                    act.activation(wdn[0][:, :, :], raw2[:, :].rearrange("p (m n) -> p m n", m=MCH), ACT.Copy).then_inc(w_hi, 1)
                    act.wait_ge(bias_in, BIAS_AT[ph + 1])
                    if g == 1:
                        act.wait_ge(route, 1)
                        act.activation(esel[:, :, :], esel[:, :, :], ACT.Exp).then_inc(route_e, 1)

                    def body(b, i, first):
                        for m in range(MCH):
                            n = MCH * N + MCH * b + m
                            act.wait_ge(f1_mm, n + 1)
                            ge(act, g_lo, n - 2)
                            act.activation(gel[m % 3][:, :], up_ps[m % 3], ACT.Gelu_apprx_tanh, bias=bup[:, m:m + 1]).then_inc(gelu_sb, 1)
                            if m == 4 and not (isinstance(b, int) and b == NB - 1):
                                split(b + 1, 1 - i)
                    steps(act, body, lambda b, i: None)

                @block.vector
                def _(dve):
                    raw = raw1[:, :].rearrange("p (s n) -> p s n", s=3)
                    dve.wait_ge(w_hi, W_AT[ph] + 1)
                    dve.tensor_tensor(wup5[:, 2:4, :], raw[:, 0:2, :], wup5[:, 0:2, :].bitcast(F32), ALU.subtract).then_inc(w_lo, 1)
                    dve.wait_ge(w_hi, W_AT[ph] + 2)
                    low = wup5[2 * TAIL:3 * TAIL, 4, :]
                    dve.tensor_tensor(low, raw[2 * TAIL:3 * TAIL, 2, :], low.bitcast(F32), ALU.subtract).then_inc(w_lo, 1)

                    def split(b, i):
                        dve.wait_ge(m_hi, 2 * N + 2 * b + 2)
                        cols = bass.ds(b * BLK, BLK)
                        dve.tensor_tensor(hs[i][:, 2:4, :], HT[:, 0:2, cols], hs[i][:, 0:2, :].bitcast(F32), ALU.subtract).then_inc(m_lo, 1)
                        low = hs[i][TAIL:2 * TAIL, 4, :]
                        dve.tensor_tensor(low, HT[TAIL:2 * TAIL, 2, cols], low.bitcast(F32), ALU.subtract).then_inc(m_lo, 1)
                    split(0, 0)
                    dve.wait_ge(w_hi, W_AT[ph] + 3)
                    dve.tensor_tensor(wdn[1][:, :, :], raw2[:, :].rearrange("p (m n) -> p m n", m=MCH),
                                      wdn[0][:, :, :].bitcast(F32), ALU.subtract).then_inc(w_lo, 1)
                    dve.wait_ge(bias_in, BIAS_AT[ph + 1])
                    if g == 1:
                        routing(dve)

                    def evacuate(b, i):
                        for t in range(2):
                            if t == 0:
                                dve.wait_ge(f2_mm, MCH * N + MCH * b + MCH)
                            ge(dve, x_mlp, 2 * N + 2 * (b - 1) + t + 1)
                            dve.tensor_tensor(y[t][:, :], down_ps[i][t][:, 0:D], bdown_bc[:, :], ALU.add).then_inc(z_bias, 1)
                        dve.wait_ge(gate_in[i], 256 * ph + 16 * (b - i) + 32)
                        for t in range(2):
                            dve.wait_ge(z_bias, 2 * N + 2 * b + t + 1)
                            if g == 0:
                                dve.tensor_tensor(y[t][:, :], y[t][:, :], gate_bc[i][:, t, :], ALU.mult).then_inc(z_gate, 1)
                            else:
                                weight = cw[:, bass.ds(2 * b + t, 1), g - 1]
                                dve.scalar_tensor_tensor(out=y[t][:, :], in0=y[t][:, :], scalar=weight,
                                                         in1=gate_bc[i][:, t, :], op0=ALU.mult, op1=ALU.mult).then_inc(z_gate, 1)

                    def body(b, i, first):
                        for m in range(MCH):
                            n = MCH * N + MCH * b + m
                            r = m % 3
                            dve.wait_ge(gelu_sb, n + 1)
                            ge(dve, f2_mm, n - 2)
                            dve.tensor_copy(gelu_hi[r][:, :], gel[r][:, :]).then_inc(g_hi, 1)
                            dve.wait_ge(g_hi, n + 1)
                            dve.tensor_tensor(gelu_lo[r][:, :], gel[r][:, :], gelu_hi[r][:, :].bitcast(F32), ALU.subtract).then_inc(g_lo, 1)
                            if m == 2 and not first:
                                evacuate(b - 1, 1 - i)
                            if m == 5 and not (isinstance(b, int) and b == NB - 1):
                                split(b + 1, 1 - i)
                    steps(dve, body, evacuate)

                @block.tensor
                def _(pe):
                    pe.wait_ge(w_lo, W_AT[ph] + 2)

                    def up(b, i, m):
                        n = MCH * N + MCH * b + m
                        if m == 0:
                            pe.wait_ge(m_lo, 2 * N + 2 * b + 2)
                        ge(pe, gelu_sb, n - 2)
                        seven(pe, up_ps[m % 3], lambda s, r: wup5[0:r, s, m * P:(m + 1) * P],
                              lambda s, r: hs[i][0:r, s, :], True).then_inc(f1_mm, 1)

                    def down(b, i, m):
                        n = MCH * N + MCH * b + m
                        if m == 0:
                            ge(pe, z_bias, 2 * N + 2 * (b - 2) + 2)
                        pe.wait_ge(g_lo, n + 1)
                        for t in range(2):
                            ts = slice(t * P, (t + 1) * P)
                            for q, (a, w) in enumerate(((gelu_hi, 0), (gelu_hi, 1), (gelu_lo, 0))):
                                mm = pe.matmul(down_ps[i][t][:, 0:D], a[m % 3][:, ts], wdn[w][:, m, :],
                                               start=(m == 0 and q == 0), stop=(m == MCH - 1 and q == 2))
                        mm.then_inc(f2_mm, 1)

                    def body(b, i, first):
                        for m in range(MCH):
                            up(b, i, m)
                            if m >= 2:
                                if first and m == 2:
                                    pe.wait_ge(w_lo, W_AT[ph] + 3)
                                down(b, i, m - 2)
                            elif not first:
                                down(b - 1, 1 - i, MCH - 2 + m)

                    def tail(b, i):
                        down(b, i, MCH - 2)
                        down(b, i, MCH - 1)
                    steps(pe, body, tail)

        def routing(dve):
            n = 0

            def link(op):
                nonlocal n
                op.then_inc(route_step, 1)
                n += 1
                dve.wait_ge(route_step, n)

            lg = [logits[:, :, e] for e in range(EXPERTS)]
            link(dve.memset(rank[:, :, :], 0.0))
            for e in range(EXPERTS):
                for j in range(EXPERTS):
                    if j != e:
                        link(dve.tensor_tensor(cmp[:, :], lg[j], lg[e], ALU.is_ge if j < e else ALU.is_gt))
                        link(dve.tensor_tensor(rank[:, e, :], rank[:, e, :], cmp[:, :], ALU.add))
            link(dve.tensor_reduce(out=lmax[:, :], in_=logits[:, :, :], axis=AX.X, op=ALU.max))
            n += 1
            dve.tensor_tensor(esel[:, :, :], logits[:, :, :], lmax[:, :].unsqueeze(2).to_broadcast([P, TILES, EXPERTS]),
                              ALU.subtract).then_inc(route, 1)
            n -= 1
            dve.wait_ge(route_e, 1)
            for e in range(EXPERTS):
                link(dve.tensor_scalar(cmp[:, :], rank[:, e, :], 2.0, None, ALU.is_lt))
                link(dve.tensor_tensor(esel[:, :, e], esel[:, :, e], cmp[:, :], ALU.mult))
            link(dve.tensor_reduce(out=esum[:, :], in_=esel[:, :, :], axis=AX.X, op=ALU.add))
            link(dve.reciprocal(cmp[:, :], esum[:, :]))
            link(dve.tensor_tensor(cw[:, :, :], esel[:, :, :], cmp[:, :].unsqueeze(2).to_broadcast([P, TILES, EXPERTS]), ALU.mult))

        attention(0)
        mlp(0)
        attention(1)
        for g in range(1, PASSES_MLP):
            mlp(g)


def kernel(x, cond_1152, L0_cond_w_qkv, L0_cond_b_qkv, L0_cond_w_proj, L0_cond_b_proj, L0_cond_w_fc1,
           L0_cond_b_fc1, L0_cond_w_fc2, L0_cond_b_fc2, L0_cond_w_ada, L0_cond_b_ada, L1_cond_w_adaln,
           L1_cond_b_adaln, L1_cond_w_qkv, L1_cond_b_qkv, L1_cond_w_proj, L1_cond_b_proj, L1_cond_w_gate,
           L1_cond_w1, L1_cond_b1, L1_cond_w2, L1_cond_b2):
    import numpy as np
    import concourse.bacc as bacc
    from concourse.bass_utils import run_bass_kernel_spmd

    nc = bacc.Bacc("TRN2", target_bir_lowering=False, num_devices=1)
    arrays = {}

    def given(name, a, shape=None):
        a = np.ascontiguousarray(a)
        if shape is not None:
            a = a.reshape(shape)
        arrays[name] = a
        return nc.dram_tensor(name, a.shape, mybir.dt.from_np(a.dtype), kind="ExternalInput").ap()

    tokens = NSEQ * SEQ
    w1 = given("w1", L1_cond_w1)
    b1 = given("b1", L1_cond_b1)
    w2 = given("w2", L1_cond_w2)
    b2 = given("b2", L1_cond_b2)
    result = nc.dram_tensor("result", (tokens, D), F32, kind="ExternalOutput").ap()
    build(
        nc,
        given("tokens", x, (tokens, D)),
        given("cond", cond_1152),
        [given("w_qkv0", L0_cond_w_qkv), given("w_qkv1", L1_cond_w_qkv)],
        [given("b_qkv0", L0_cond_b_qkv), given("b_qkv1", L1_cond_b_qkv)],
        [given("w_proj0", L0_cond_w_proj), given("w_proj1", L1_cond_w_proj)],
        [given("b_proj0", L0_cond_b_proj), given("b_proj1", L1_cond_b_proj)],
        [given("w_fc1", L0_cond_w_fc1)] + [w1[e] for e in range(EXPERTS)],
        [given("b_fc1", L0_cond_b_fc1)] + [b1[e] for e in range(EXPERTS)],
        [given("w_fc2", L0_cond_w_fc2)] + [w2[e] for e in range(EXPERTS)],
        [given("b_fc2", L0_cond_b_fc2)] + [b2[e] for e in range(EXPERTS)],
        [given("w_ada0", L0_cond_w_ada), given("w_ada1", L1_cond_w_adaln)],
        [given("b_ada0", L0_cond_b_ada), given("b_ada1", L1_cond_b_adaln)],
        given("w_gate", L1_cond_w_gate),
        result,
    )
    r = run_bass_kernel_spmd(nc, [arrays], core_ids=[0])
    return r.results[0]["result"].reshape(NSEQ, SEQ, D)
```

```python
import concourse.bass as bass
from concourse import mybir
from contextlib import ExitStack

F32 = mybir.dt.float32
F32R = mybir.dt.float32r
ALU = mybir.AluOpType
ACT = mybir.ActivationFunctionType
AX = mybir.AxisListType

P = 128
NSEQ, SEQ, D = 64, 64, 288
HEADS = 16
HD = D // HEADS
HID = 4 * D
EXPERTS = 4
TILES = NSEQ * SEQ // P
BLK = 2 * P
NB = NSEQ * SEQ // BLK
MCH = HID // P
EPS = 1e-6
LAYERS = 2
PASSES_MLP = 1 + EXPERTS
TAIL = D - 2 * P
REP = P // TAIL
XCOLS = 3 * P
GROUPS = [(0, 6), (6, 11), (11, 16)]
PAIRS = [(0, 0, P), (1, 1, P), (0, 2, P), (1, 3, P), (2, 0, P), (3, 1, P), (4, 4, 3 * TAIL)]
VW = HD + 1
ST_LN1, ST_QK, ST_SCORE, ST_PV, ST_PROJ, ST_LN2, ST_GATE = range(7)
DEPTH = ST_GATE


def build(nc, x, cond, w_qkv, b_qkv, w_proj, b_proj, w_up, b_up, w_down, b_down, w_ada, b_ada,
          w_gate, out):
    ctx = ExitStack()
    with ctx:
        def sb(name, shape, dt=F32):
            return ctx.enter_context(nc.sbuf_tensor(name, shape, dt))

        def sem(name):
            return ctx.enter_context(nc.semaphore(name))

        X = sb("X", [P, TILES, D])
        HT = sb("HT", [P, 3, TILES * P])
        hs = [sb(f"hs{i}", [P, 5, BLK], F32R) for i in range(2)]
        ident = sb("ident", [P, P])
        mods = [sb(f"mods{l}", [P, 4, 3, NSEQ]) for l in range(LAYERS)]
        head_mask = sb("head_mask", [P, HEADS])
        mhalf = sb("mhalf", [P, 2])
        gate_bc = [sb(f"gate_bc{i}", [P, 2, D]) for i in range(2)]
        y = [sb(f"y{t}", [P, D]) for t in range(2)]
        bproj_bc = [sb(f"bproj_bc{l}", [P, D]) for l in range(LAYERS)]
        bqk = [sb(f"bqk{l}", [P, 6]) for l in range(LAYERS)]
        bv = sb("bv", [P, LAYERS, 3])
        bdown_bc = [sb(f"bdown_bc{i}", [P, D]) for i in range(2)]
        bup = [sb(f"bup{i}", [P, MCH]) for i in range(2)]
        logits = sb("logits", [P, TILES, EXPERTS])
        cw = sb("cw", [P, TILES, EXPERTS])
        wg = sb("wg", [P, 3, EXPERTS])
        stats = [sb(f"stats{k}", [P, 2, 6]) for k in range(2)]
        meanvar = [sb(f"meanvar{k}", [P, 2, 2]) for k in range(2)]
        vareps = [sb(f"vareps{k}", [P, 2]) for k in range(2)]
        rstd = [sb(f"rstd{k}", [P, 2]) for k in range(2)]
        rowmax = [sb(f"rowmax{t}", [P, HEADS]) for t in range(2)]
        rden = [sb(f"rden{t}", [P, HEADS]) for t in range(2)]

        base = nc.sbuf_base
        top = nc.sbuf_usable_end

        class Region:
            def __init__(self, at):
                self.at = at

            def take(self, name, shape, dt=F32):
                n = 4
                for k in shape[1:]:
                    n *= k
                t = nc.alloc_sbuf_tensor_at(name, shape, dt, offset=self.at)
                self.at += (n + 31) // 32 * 32
                assert self.at <= top, (name, self.at, top)
                return t

        ctx.enter_context(nc.sbuf_tensor("fence", [P, (top - base) // 4 - 64], F32))
        W1_BYTES, WDN_BYTES = 4 * 5 * HID, 4 * MCH * D
        at_w1b = base + W1_BYTES + 3 * WDN_BYTES
        at_rest = at_w1b + W1_BYTES

        r = Region(base)
        w1b = r.take("w1b", [P, 5, HID], F32R)
        wdn = [r.take(f"wdn{i}", [P, MCH, D], F32R) for i in range(2)]
        wraw = r.take("wraw", [P, MCH, D])
        w1a = r.take("w1a", [P, 5, HID], F32R)
        w1 = [w1a, w1b]
        w1raw = [Region(at_w1b).take("w1a_raw", [P, 5, HID]), Region(base).take("w1b_raw", [P, 5, HID])]
        wrawC = r.take("wrawC", [P, HID])
        gel = [r.take(f"gel{i}", [P, BLK]) for i in range(3)]
        gelu_hi = [r.take(f"gelu_hi{i}", [P, BLK], F32R) for i in range(3)]
        gelu_lo = [r.take(f"gelu_lo{i}", [P, BLK], F32R) for i in range(3)]
        rank = r.take("rank", [P, EXPERTS, TILES])
        cmp = r.take("cmp", [P, TILES])
        lmax = r.take("lmax", [P, TILES])
        esel = r.take("esel", [P, TILES, EXPERTS])
        esum = r.take("esum", [P, TILES])

        r = Region(base)
        kbd = r.take("kbd", [P, HEADS, BLK])
        qT = [r.take(f"qT{i}", [P, 3, BLK]) for i in range(2)]
        assert r.at <= base + W1_BYTES
        r = Region(base + W1_BYTES)
        kT = r.take("kT", [P, 3, BLK])
        vbd = [r.take(f"vbd{i}", [P, 4, HEADS // 2, 2 * VW]) for i in range(2)]
        os5 = r.take("os5", [P, 5, BLK], F32R)
        u00 = r.take("u00", [P, 3, P])
        assert r.at <= base + W1_BYTES + 2 * WDN_BYTES
        r = Region(base + W1_BYTES + 2 * WDN_BYTES)
        prob = [r.take(f"prob{t}", [P, HEADS, SEQ]) for t in range(2)]
        u01 = r.take("u01", [P, 3, P])
        assert r.at <= at_w1b
        r = Region(at_rest)
        probT = [r.take(f"probT{t}", [P, 8 * P]) for t in range(2)]
        u = [[u00, u01], [r.take(f"u1{t}", [P, 3, P]) for t in range(2)]]
        o = [r.take(f"o{t}", [P, XCOLS]) for t in range(2)]
        oT = [r.take(f"oT{t}", [P, 3, P]) for t in range(2)]
        r = Region(r.at - 2 * 4 * 3 * P)
        bvB = r.take("bvB", [P, 3, P])
        onesr = r.take("onesr", [P, P])

        r = Region(base)
        wada = [r.take(f"wada{l}", [P, 3, 6 * D]) for l in range(LAYERS)]
        cnd = r.take("cnd", [NSEQ, D])
        scond = r.take("scond", [NSEQ, D])
        scT = r.take("scT", [P, 3, NSEQ])
        assert r.at <= at_w1b
        ada = [HT[0:NSEQ, 0, 6 * D * l:6 * D * (l + 1)] for l in range(LAYERS)]
        adaC = [HT[0:NSEQ, 1, 4 * P * l:4 * P * (l + 1)].rearrange("b (v r c) -> b v r c", v=4, r=REP)
                for l in range(LAYERS)]
        bada = [HT[0:NSEQ, 2, 6 * D * l:6 * D * (l + 1)] for l in range(LAYERS)]

        gates_d = nc.dram_tensor("gates_d", (LAYERS, 2, NSEQ, D), F32).ap()

        scores = ctx.enter_context(nc.psum_tensor("scores", [P, 1024], F32))
        probT_ps = ctx.enter_context(nc.psum_tensor("probT_ps", [P, 1024], F32))
        gemm = [ctx.enter_context(nc.psum_tensor(f"gemm{i}", [P, 512], F32)) for i in range(2)]
        tbank = [ctx.enter_context(nc.psum_tensor(f"tbank{i}", [P, 512], F32)) for i in range(2)]
        up_ps = [scores[:, 0:BLK], scores[:, 512:512 + BLK], probT_ps[:, 0:BLK]]
        down_ps = [[gemm[0], gemm[1]], [tbank[0], tbank[1]]]

        x_first, x_rest, cond_in, small_in, gates_out = map(sem, (
            "x_first", "x_rest", "cond_in", "small_in", "gates_out"))
        wada_in = [sem(f"wada_in{l}") for l in range(LAYERS)]
        w1_in, wdn_in, bias_in, out_done = map(sem, ("w1_in", "wdn_in", "bias_in", "out_done"))
        gate_in = [sem(f"gate_in{i}") for i in range(2)]
        const_done, silu_done, silu_mm, silu_sb = map(sem, ("const_done", "silu_done", "silu_mm", "silu_sb"))
        ada_mm, ada_sb, adaC_sb, mods_mm, mods_sb = map(sem, ("ada_mm", "ada_sb", "adaC_sb", "mods_mm", "mods_sb"))
        w_hi, w_lo, wd_hi, wd_lo, bv_done, bv_mm, bp_done, vbd_init = map(sem, (
            "w_hi", "w_lo", "wd_hi", "wd_lo", "bv_done", "bv_mm", "bp_done", "vbd_init"))
        ln_stats, ln_mv, ln_ve, ln_rstd, ln_xn, ln_T, ln_u, ln_v = (
            [sem(f"{n}{k}") for k in range(2)] for n in (
                "ln_stats", "ln_mv", "ln_ve", "ln_rstd", "ln_xn", "ln_T", "ln_u", "ln_v"))
        h_hi, h_lo, ht_done = map(sem, ("h_hi", "h_lo", "ht_done"))
        qk_mm, qk_sb, v_mm, v_sb, kbd_done, kbd_act = map(sem, (
            "qk_mm", "qk_sb", "v_mm", "v_sb", "kbd_done", "kbd_act"))
        s_mm, s_max, s_sub, s_exp = map(sem, ("s_mm", "s_max", "s_sub", "s_exp"))
        pt_mm, pt_sb, pv_mm, o_rec, o_norm, o_full = map(sem, (
            "pt_mm", "pt_sb", "pv_mm", "o_rec", "o_norm", "o_full"))
        ot_mm, ot_sb, os_hi, os_lo, pj_mm, y_bias, y_gate, x_attn = map(sem, (
            "ot_mm", "ot_sb", "os_hi", "os_lo", "pj_mm", "y_bias", "y_gate", "x_attn"))
        lg_mm, lg_sb = map(sem, ("lg_mm", "lg_sb"))
        m_hi, m_lo, f1_mm, gelu_sb, g_hi, g_lo, f2_mm, z_bias, z_gate, x_mlp, route = map(sem, (
            "m_hi", "m_lo", "f1_mm", "gelu_sb", "g_hi", "g_lo", "f2_mm", "z_bias", "z_gate",
            "x_mlp", "route"))
        route_e, route_step = map(sem, ("route_e", "route_step"))

        def seven(pe, dst, stationary, moving, w_first):
            for n, (ws, xs, rows) in enumerate(PAIRS):
                a, b = (ws, xs) if w_first else (xs, ws)
                mm = pe.matmul(dst, stationary(a, rows), moving(b, rows),
                               start=(n == 0), stop=(n == len(PAIRS) - 1))
            return mm

        def phase_of_mlp(g):
            return 1 if g == 0 else 2 + g

        WCOLS = {0: ((w_qkv[0], 0), (w_proj[0], 3 * D)), 2: ((w_qkv[1], 0), (w_proj[1], 3 * D))}
        for g in range(PASSES_MLP):
            WCOLS[phase_of_mlp(g)] = ((w_up[g], 0),)
        W1_IN = [0]
        for ph in range(7):
            W1_IN.append(W1_IN[-1] + 64 * len(WCOLS[ph]))

        def load_w1(sp, ph):
            dst = w1raw[ph % 2]
            for w, c0 in WCOLS[ph]:
                n = w.shape[1]
                sp.dma_start(dst[:, 2:4, c0:c0 + n], w[0:2 * P, :].rearrange("(s p) n -> p s n", p=P)).then_inc(w1_in, 16)

        def load_w1C(sp, ph):
            for w, c0 in WCOLS[ph]:
                n = w.shape[1]
                for c in range(3):
                    sp.dma_start(wrawC[c * TAIL:(c + 1) * TAIL, c0:c0 + n], w[2 * P:D, :]).then_inc(w1_in, 16)

        def load_wdn(sp, g):
            sp.dma_start(wraw[:, :, :], w_down[g].rearrange("(m p) n -> p m n", p=P)).then_inc(wdn_in, 16)

        SLICES = 3
        SPLIT = 2 * SLICES
        SCOLS = HID // SLICES

        def split_w1_hi(act, ph, c):
            w5, cs = w1[ph % 2], slice(c * SCOLS, (c + 1) * SCOLS)
            if c == 0:
                act.wait_ge(w1_in, W1_IN[ph + 1])
            act.activation(w5[:, 0:2, cs], w1raw[ph % 2][:, 2:4, cs], ACT.Copy).then_inc(w_hi, 1)
            act.activation(w5[0:3 * TAIL, 4, cs], wrawC[0:3 * TAIL, cs], ACT.Copy).then_inc(w_hi, 1)

        def split_w1_lo(dve, ph, c):
            w5, cs = w1[ph % 2], slice(c * SCOLS, (c + 1) * SCOLS)
            if c == 0:
                dve.wait_ge(w1_in, W1_IN[ph + 1])
            dve.wait_ge(w_hi, SPLIT * ph + 2 * c + 1)
            dve.tensor_tensor(w5[:, 2:4, cs], w1raw[ph % 2][:, 2:4, cs], w5[:, 0:2, cs].bitcast(F32),
                              ALU.subtract).then_inc(w_lo, 1)
            dve.wait_ge(w_hi, SPLIT * ph + 2 * c + 2)
            low = w5[2 * TAIL:3 * TAIL, 4, cs]
            dve.tensor_tensor(low, wrawC[2 * TAIL:3 * TAIL, cs], low.bitcast(F32), ALU.subtract).then_inc(w_lo, 1)

        def load_mlp_bias(sp, g):
            sp.dma_start(bup[g % 2][:, :], b_up[g].rearrange("(m p) -> p m", p=P),
                         allow_slow_non_contiguous=True).then_inc(bias_in, 16)
            sp.dma_start(bdown_bc[g % 2][:, :], b_down[g].unsqueeze(0).to_broadcast([P, D])).then_inc(bias_in, 16)

        NADA = 6 * D // 4
        ada_ps = [gemm[0], gemm[1], tbank[0], tbank[1]]
        SMALL = 2 + LAYERS * (6 + 4 + 1)
        with nc.Block() as block:
            @block.sync
            def _(sp):
                sp.dma_start(cnd[:, :], cond).then_inc(cond_in, 16)
                for l in range(LAYERS):
                    sp.dma_start(wada[l][:, 0:2, :], w_ada[l][0:2 * P, :].rearrange("(s p) n -> p s n", p=P)).then_inc(wada_in[l], 16)
                    sp.dma_start(wada[l][0:TAIL, 2, :], w_ada[l][2 * P:D, :]).then_inc(wada_in[l], 16)
                    sp.dma_start(bada[l], b_ada[l].unsqueeze(0).to_broadcast([NSEQ, 6 * D])).then_inc(wada_in[l], 16)
                load_w1(sp, 0)
                load_w1C(sp, 0)
                for q in range(4):
                    sp.dma_start(X[:, 8 * q:8 * q + 8, :],
                                 x[1024 * q:1024 * q + 1024, :].rearrange("(t p) c -> p t c", p=P)).then_inc(x_rest if q else x_first, 16)
                for l in range(LAYERS):
                    sp.wait_ge(ada_sb, 4 * l + 4)
                    for q in range(2):
                        c0 = (2 + 3 * q) * D
                        sp.dma_start(gates_d[l, q], ada[l][:, c0:c0 + D]).then_inc(gates_out, 16)
                sp.wait_ge(small_in, 16 * SMALL)
                sp.wait_ge(bias_in, 64)

            @block.gpsimd
            def _(pool):
                pool.memset(ident[:, :], 0.0).then_inc(const_done, 1)
                pool.memset(head_mask[:, :], 1.0).then_inc(const_done, 1)
                pool.memset(bv[:, :, :], 0.0).then_inc(const_done, 1)
                pool.memset(mhalf[:, :], -0.5).then_inc(const_done, 1)
                pool.wait_ge(const_done, 4)
                pool.affine_select(out=ident[:, :], in_=ident[:, :], compare_op=ALU.not_equal, fill=1.0,
                                   base=0, pattern=[[-1, P]], channel_multiplier=1).then_inc(const_done, 1)
                n = 5
                for h0, h1 in GROUPS:
                    part = head_mask[:, h0:h1]
                    pool.affine_select(out=part, in_=part, compare_op=ALU.is_ge, fill=0.0,
                                       base=0, pattern=[[-HD, h1 - h0]], channel_multiplier=1).then_inc(const_done, 1)
                    n += 1
                    pool.wait_ge(const_done, n)
                    pool.affine_select(out=part, in_=part, compare_op=ALU.is_ge, fill=0.0,
                                       base=HD - 1, pattern=[[HD, h1 - h0]], channel_multiplier=-1).then_inc(const_done, 1)
                    n += 1

            @block.scalar
            def _(act):
                act.wait_ge(cond_in, 16)
                act.activation(scond[:, :], cnd[:, :], ACT.Silu).then_inc(silu_done, 1)
                act.wait_ge(const_done, 4)
                act.dma_start(wg[:, 0:2, :], w_gate[0:2 * P, :].rearrange("(s p) n -> p s n", p=P)).then_inc(small_in, 16)
                act.dma_start(wg[0:TAIL, 2, :], w_gate[2 * P:D, :]).then_inc(small_in, 16)
                for l in range(LAYERS):
                    for g, (h0, h1) in enumerate(GROUPS):
                        for q in range(2):
                            act.dma_start(bqk[l][0:(h1 - h0) * HD, 3 * (1 - q) + g:3 * (1 - q) + g + 1],
                                           b_qkv[l][q * D + h0 * HD:q * D + h1 * HD].unsqueeze(1)).then_inc(small_in, 16)
                    for s, p0, rows in ((0, 0, P), (1, 0, P), (2, 0, TAIL), (2, 2 * TAIL, TAIL)):
                        c0 = 2 * D + s * P
                        act.dma_start(bv[p0:p0 + rows, l, s:s + 1], b_qkv[l][c0:c0 + rows].unsqueeze(1)).then_inc(small_in, 16)
                    act.dma_start(bproj_bc[l][:, :], b_proj[l].unsqueeze(0).to_broadcast([P, D])).then_inc(small_in, 16)
                load_mlp_bias(act, 0)
                load_mlp_bias(act, 1)
                for c in range(SLICES):
                    split_w1_hi(act, 0, c)

            @block.tensor
            def _(pe):
                pe.wait_ge(const_done, 11)
                pe.wait_ge(silu_done, 1)
                for s, (c0, c1) in enumerate(((0, P), (P, 2 * P), (2 * P, D))):
                    mm = pe.transpose(scores[0:c1 - c0, s * NSEQ:(s + 1) * NSEQ], scond[:, c0:c1], ident[0:NSEQ, 0:NSEQ])
                mm.then_inc(silu_mm, 1)
                pe.wait_ge(silu_sb, 1)
                for l in range(LAYERS):
                    pe.wait_ge(wada_in[l], 48)
                    for j in range(4):
                        if l:
                            pe.wait_ge(ada_sb, j + 1)
                        for k, rows in enumerate((P, P, TAIL)):
                            mm = pe.matmul(ada_ps[j][0:NSEQ, 0:NADA], scT[0:rows, k, :], wada[l][0:rows, k, j * NADA:(j + 1) * NADA],
                                           start=(k == 0), stop=(k == 2))
                        mm.then_inc(ada_mm, 1)
                    pe.wait_ge(adaC_sb, 4 * l + 4)
                    for v, part in enumerate((0, 1, 3, 4)):
                        if l and v % 2 == 0:
                            pe.wait_ge(mods_sb, 2 + v)
                        for s in range(3):
                            c0 = (v // 2) * 512 + (3 * (v % 2) + s) * NSEQ
                            src = (ada[l][:, part * D + s * P:part * D + (s + 1) * P] if s < 2 else
                                   adaC[l][:, v, :, :].rearrange("b r c -> b (r c)"))
                            mm = pe.transpose(scores[:, c0:c0 + NSEQ], src, ident[0:NSEQ, 0:NSEQ])
                        mm.then_inc(mods_mm, 1)

            @block.vector
            def _(dve):
                dve.wait_ge(silu_mm, 1)
                dve.tensor_copy(scT[:, 0:2, :], scores[:, 0:2 * NSEQ].rearrange("p (s b) -> p s b", s=2))
                dve.tensor_copy(scT[0:TAIL, 2, :], scores[0:TAIL, 2 * NSEQ:3 * NSEQ]).then_inc(silu_sb, 1)
                for l in range(LAYERS):
                    dve.wait_ge(wada_in[l], 48)
                    for j in range(4):
                        cs = slice(j * NADA, (j + 1) * NADA)
                        dve.wait_ge(ada_mm, 4 * l + j + 1)
                        dve.tensor_tensor(ada[l][:, cs], ada_ps[j][0:NSEQ, 0:NADA], bada[l][:, cs], ALU.add).then_inc(ada_sb, 1)
                    dve.wait_ge(ada_sb, 4 * l + 4)
                    for v, part in enumerate((0, 1, 3, 4)):
                        c0 = part * D + 2 * P
                        dve.tensor_copy(adaC[l][:, v, :, :], ada[l][:, c0:c0 + TAIL].unsqueeze(1).to_broadcast([NSEQ, REP, TAIL])).then_inc(adaC_sb, 1)
                    for v in range(4):
                        dve.wait_ge(mods_mm, 4 * l + v // 2 * 2 + 2)
                        c0 = (v // 2) * 512 + 3 * (v % 2) * NSEQ
                        src = scores[:, c0:c0 + 3 * NSEQ].rearrange("p (s b) -> p s b", s=3)
                        if v % 2:
                            dve.tensor_scalar(mods[l][:, v, :, :], src, 1.0, None, ALU.add).then_inc(mods_sb, 1)
                        else:
                            dve.tensor_copy(mods[l][:, v, :, :], src).then_inc(mods_sb, 1)
                for c in range(SLICES):
                    split_w1_lo(dve, 0, c)

        def ge(eng, s, value):
            if not isinstance(value, int) or value > 0:
                eng.wait_ge(s, value)

        def tile(b, t):
            return X[:, bass.ds(2 * b + t, 1), :].rearrange("p o c -> p (o c)")

        def slots(ap):
            return ap.rearrange("p (s q k) -> p s q k", s=3, q=2)

        def seq_mod(l, v, b, t):
            return mods[l][:, v, :, bass.ds(4 * b + 2 * t, 2)].unsqueeze(3).to_broadcast([P, 3, 2, SEQ])

        def gate_load(sp, l, q, b, parity):
            for half in range(2):
                src = gates_d[l, q].rearrange("(t h) c -> h t c", h=2)[half, bass.ds(2 * b, 2), :]
                sp.dma_start(gate_bc[parity][half * SEQ:(half + 1) * SEQ, :, :],
                             src.unsqueeze(0).to_broadcast([SEQ, 2, D])).then_inc(gate_in[parity], 16)

        def attention(l):
            ph = 2 * l
            L = NB * l
            nstage = ST_GATE + 1
            ORDER = [(ST_PROJ, ot_sb, 2 * L), (ST_PV, o_norm, 2 * L)] + ([(ST_GATE, lg_sb, 0)] if l else []) + [
                (ST_PROJ, y_bias, 2 * L), (ST_LN2, ln_u[1], 2 * L)]
            OT, PV, GATE, PROJ, LN2 = 0, 1, 2, 2 + l, 3 + l

            def steps(eng, body, after={}):
                for s in range(DEPTH):
                    body(s // 2, s % 2, [0 <= s - k for k in range(nstage)])
                    if s in after:
                        after[s]()
                with eng.Fori(DEPTH // 2, NB // 2) as h:
                    for par in range(2):
                        body(h, par, [True] * nstage)
                for s in range(NB, NB + DEPTH):
                    body(s // 2, s % 2, [s - k < NB for k in range(nstage)])
                    if s in after:
                        after[s]()

            def blk(h, par, k):
                return 2 * h + (par - k), (par - k) % 2

            def tbank_free(pe, h, par, live, item, t):
                for back in range(4):
                    for j in reversed(range(item if back == 0 else len(ORDER))):
                        k, s, before = ORDER[j]
                        b = 2 * h + par - back - k
                        if isinstance(h, int):
                            if not 0 <= b < NB:
                                continue
                        pe.wait_ge(s, before + 2 * b + t + 1)
                        return

            with nc.Block() as block:
                @block.sync
                def _(sp):
                    sp.wait_ge(gates_out, 32 * LAYERS)
                    gate_load(sp, l, 0, 0, 0)
                    gate_load(sp, l, 0, 1, 1)
                    with sp.Fori(1, NB // 2) as h:
                        for par in range(2):
                            sp.wait_ge(x_attn, 2 * L + 2 * (2 * h + par - 2) + 2)
                            gate_load(sp, l, 0, 2 * h + par, par)
                    sp.wait_ge(s_mm, 2 * L + 2 * NB)
                    load_w1(sp, ph + 1)
                    sp.wait_ge(pv_mm, 2 * L + 2 * NB)
                    load_w1C(sp, ph + 1)
                    load_wdn(sp, l)

                @block.gpsimd
                def _(pool):
                    for i in range(2):
                        pool.memset(vbd[i][:, :, :, :], 0.0).then_inc(vbd_init, 1)
                    pool.wait_ge(vbd_init, 6 * l + 2)
                    for i in range(2):
                        pool.memset(vbd[i][0:SEQ, :, :, HD:HD + 1], 1.0).then_inc(vbd_init, 1)
                        pool.wait_ge(vbd_init, 6 * l + 3 + 2 * i)
                        pool.memset(vbd[i][SEQ:P, :, :, VW + HD:VW + HD + 1], 1.0).then_inc(vbd_init, 1)
                        pool.wait_ge(vbd_init, 6 * l + 4 + 2 * i)

                    def pow_rstd(k, b):
                        pool.wait_ge(ln_ve[k], L + b + 1)
                        pool.tensor_tensor(rstd[k][:, :], vareps[k][:, :], mhalf[:, :], ALU.pow).then_inc(ln_rstd[k], 1)

                    def shift(k, b):
                        for t in range(2):
                            pool.wait_ge(ln_u[k], 2 * L + 2 * b + t + 1)
                            ut = u[k][t][:, :, :].rearrange("p s (q k) -> p s q k", q=2)
                            pool.tensor_tensor(ut, ut, seq_mod(l, 2 * k, b, t), ALU.add).then_inc(ln_v[k], 1)

                    def body(h, par, live):
                        if live[ST_QK]:
                            shift(0, blk(h, par, ST_QK)[0])
                        if live[ST_QK]:
                            b, i = blk(h, par, ST_QK)
                            for t in range(2):
                                ts = slice(t * P, (t + 1) * P)
                                pool.wait_ge(h_hi, 4 * L + 4 * b + 2 * t + 2)
                                pool.tensor_tensor(hs[i][:, 2:4, ts], u[0][t][:, 0:2, :],
                                                   hs[i][:, 0:2, ts].bitcast(F32), ALU.subtract).then_inc(h_lo, 1)
                                pool.wait_ge(h_lo, 4 * L + 4 * b + 2 * t + 1)
                                pool.tensor_tensor(hs[i][TAIL:2 * TAIL, 4, ts], u[0][t][TAIL:2 * TAIL, 2, :],
                                                   hs[i][TAIL:2 * TAIL, 4, ts].bitcast(F32), ALU.subtract).then_inc(h_lo, 1)
                                pool.wait_ge(h_lo, 4 * L + 4 * b + 2 * t + 2)
                        if live[ST_LN1]:
                            pow_rstd(0, blk(h, par, ST_LN1)[0])
                        if live[ST_LN2]:
                            pow_rstd(1, blk(h, par, ST_LN2)[0])
                        if live[ST_PROJ]:
                            b, _ = blk(h, par, ST_PROJ)
                            for t in range(2):
                                ts = slice(t * P, (t + 1) * P)
                                pool.wait_ge(os_hi, 4 * L + 4 * b + 2 * t + 2)
                                pool.tensor_tensor(os5[:, 2:4, ts], oT[t][:, 0:2, :],
                                                   os5[:, 0:2, ts].bitcast(F32), ALU.subtract).then_inc(os_lo, 1)
                                pool.wait_ge(os_lo, 4 * L + 4 * b + 2 * t + 1)
                                pool.tensor_tensor(os5[TAIL:2 * TAIL, 4, ts], oT[t][TAIL:2 * TAIL, 2, :],
                                                   os5[TAIL:2 * TAIL, 4, ts].bitcast(F32), ALU.subtract).then_inc(os_lo, 1)
                                pool.wait_ge(os_lo, 4 * L + 4 * b + 2 * t + 2)
                            g, i = blk(h, par, ST_PROJ)
                            for t in range(2):
                                if t == 0:
                                    pool.wait_ge(gate_in[i], 256 * ph + 32 * (h + (par - ST_PROJ) // 2) + 32)
                                pool.wait_ge(y_bias, 2 * L + 2 * b + t + 1)
                                pool.tensor_tensor(y[t][:, :], y[t][:, :], gate_bc[i][:, t, :], ALU.mult).then_inc(y_gate, 1)
                                pool.wait_ge(y_gate, 2 * L + 2 * b + t + 1)
                                pool.tensor_tensor(tile(b, t), tile(b, t), y[t][:, :], ALU.add).then_inc(x_attn, 1)
                        if live[ST_LN2]:
                            shift(1, blk(h, par, ST_LN2)[0])
                    steps(pool, body)

                @block.scalar
                def _(act):
                    act.wait_ge(vbd_init, 6 * (l + 1))

                    def body(h, par, live):
                        if live[ST_PV]:
                            b, _ = blk(h, par, ST_PV)
                            for t in range(2):
                                ge(act, pv_mm, 2 * L + 2 * (b - 1) + t + 1)
                                for c in range(2):
                                    act.wait_ge(pt_mm, 4 * L + 4 * b + 2 * t + c + 1)
                                    act.activation(probT[t][:, c * 512:(c + 1) * 512], probT_ps[:, c * 512:(c + 1) * 512],
                                                   ACT.Copy).then_inc(pt_sb, 1)
                        if live[ST_QK]:
                            b, i = blk(h, par, ST_QK)
                            ge(act, v_mm, 2 * L + 2 * (b - 2) + 2)
                            for t in range(2):
                                ts = slice(t * P, (t + 1) * P)
                                act.wait_ge(ln_v[0], 2 * L + 2 * b + t + 1)
                                act.activation(hs[i][:, 0:2, ts], u[0][t][:, 0:2, :], ACT.Copy).then_inc(h_hi, 1)
                                act.activation(hs[i][0:3 * TAIL, 4, ts], u[0][t][0:3 * TAIL, 2, :], ACT.Copy).then_inc(h_hi, 1)

                        def exps(t):
                            b, _ = blk(h, par, ST_SCORE)
                            act.wait_ge(s_sub, 2 * L + 2 * b + t + 1)
                            act.activation(prob[t][:, :, :], prob[t][:, :, :], ACT.Exp, scale=float(HD) ** -0.5).then_inc(s_exp, 1)

                        def mask_keys(b, first, end):
                            h0, h1 = GROUPS[2]
                            M = (h1 - h0) * HD
                            if first == 0:
                                ge(act, s_mm, 2 * L + 2 * (b - 1) + 2)
                                act.wait_ge(qk_sb, 6 * L + 6 * b + 3)
                            for n in range(h0 + first, h0 + end):
                                act.activation(kbd[0:M, n, :], kT[0:M, 2, :], ACT.Copy,
                                               scale=head_mask[0:M, n:n + 1]).then_inc(kbd_act, 1)
                        if live[ST_SCORE]:
                            exps(0)
                        if live[ST_PROJ]:
                            b, _ = blk(h, par, ST_PROJ)
                            for t in range(2):
                                ts = slice(t * P, (t + 1) * P)
                                ge(act, pj_mm, 2 * L + 2 * (b - 1) + t + 1)
                                act.wait_ge(ot_sb, 2 * L + 2 * b + t + 1)
                                act.activation(os5[:, 0:2, ts], oT[t][:, 0:2, :], ACT.Copy).then_inc(os_hi, 1)
                                act.activation(os5[0:3 * TAIL, 4, ts], oT[t][0:3 * TAIL, 2, :], ACT.Copy).then_inc(os_hi, 1)
                        if live[ST_GATE]:
                            b, _ = blk(h, par, ST_GATE)
                            for t in range(2):
                                act.wait_ge(ln_v[1], 2 * L + 2 * b + t + 1)
                                act.activation(HT[:, :, bass.ds(b * BLK + t * P, P)], u[1][t][:, :, :], ACT.Copy).then_inc(ht_done, 1)
                        if live[ST_QK]:
                            b, i = blk(h, par, ST_QK)
                            ge(act, s_mm, 2 * L + 2 * (b - 2) + 2)
                            for n in range(6):
                                g = n % 3
                                M = (GROUPS[g][1] - GROUPS[g][0]) * HD
                                if n < 2:
                                    ge(act, kbd_done, 2 * L + 2 * (b - 1) + g + 1)
                                act.wait_ge(qk_mm, 6 * L + 6 * b + n + 1)
                                dst = qT[i][0:M, g, :] if n >= 3 else kT[0:M, g, :]
                                act.activation(dst, gemm[n % 2][0:M, 0:BLK], ACT.Identity, bias=bqk[l][0:M, n:n + 1]).then_inc(qk_sb, 1)
                                if n >= 3:
                                    mask_keys(b, n - 3, n - 2)
                            ge(act, pv_mm, 2 * L + 2 * (b - 2) + 2)
                            for t in range(2):
                                act.wait_ge(v_mm, 2 * L + 2 * b + t + 1)
                                vals = gemm[t][:, 0:D].rearrange("p (h o d) -> p h o d", o=2, d=HD)
                                for half in range(2):
                                    for odd in range(2):
                                        act.activation(
                                            vbd[i][odd * SEQ:(odd + 1) * SEQ, 2 * t + half, :, odd * VW:odd * VW + HD],
                                            vals[half * SEQ:(half + 1) * SEQ, :, odd, :], ACT.Copy).then_inc(v_sb, 1)
                        if live[ST_QK]:
                            mask_keys(b, 3, 5)
                        if live[ST_SCORE]:
                            exps(1)

                    def next_weights():
                        for c in range(SLICES):
                            split_w1_hi(act, ph + 1, c)
                    steps(act, body, {NB + ST_PROJ - 1: next_weights})

                @block.vector
                def _(dve):
                    def value_bias():
                        dve.memset(onesr[:, :], 1.0).then_inc(bv_done, 1)
                        dve.wait_ge(bv_done, 4 * l + 1)
                        for s in range(3):
                            rows = P if s < 2 else 3 * TAIL
                            dve.tensor_scalar(bvB[0:rows, s, :], onesr[0:rows, :], bv[0:rows, l, s:s + 1], None, ALU.mult).then_inc(bv_done, 1)

                    def proj_bias():
                        dve.wait_ge(bv_mm, l + 1)
                        dve.tensor_tensor(bproj_bc[l][:, :], bproj_bc[l][:, :], tbank[0][:, 0:D], ALU.add).then_inc(bp_done, 1)

                    def ln_statistics(bs):
                        for k, b in bs.items():
                            for t in range(2):
                                if k:
                                    dve.wait_ge(x_attn, 2 * L + 2 * b + t + 1)
                                if k and t and 0 in bs:
                                    dve.wait_ge(ln_stats[0], 2 * L + 2 * bs[0] + 2)
                                dve.bn_stats(out=stats[k][:, t, :], in_=tile(b, t)).then_inc(ln_stats[k], 1)
                        for k, b in bs.items():
                            if len(bs) == 1:
                                dve.wait_ge(ln_stats[k], 2 * L + 2 * b + 2)
                            for t in range(2):
                                dve.bn_aggr(out=meanvar[k][:, t, :], in_=stats[k][:, t, :]).then_inc(ln_mv[k], 1)
                            if k == 0 and 1 in bs:
                                dve.wait_ge(ln_stats[1], 2 * L + 2 * bs[1] + 2)
                            dve.wait_ge(ln_mv[k], 2 * L + 2 * b + 2)
                            dve.tensor_scalar(vareps[k][:, :], meanvar[k][:, :, 1], EPS, None, ALU.add).then_inc(ln_ve[k], 1)

                    def ln_normalize(k, b):
                        dve.wait_ge(ln_rstd[k], L + b + 1)
                        for t in range(2):
                            if k == 0:
                                ge(dve, h_lo, 4 * L + 4 * (b - 1) + 2 * t + 2)
                            else:
                                ge(dve, ht_done, 2 * L + 2 * (b - 1) + t + 1)
                                if l:
                                    ge(dve, lg_mm, 2 * (b - 1) + t + 1)
                            xn = u[k][t][:, :, :].rearrange("p s k -> p (s k)")
                            dve.tensor_scalar(xn[:, 0:2 * P], X[:, bass.ds(2 * b + t, 1), 0:2 * P].rearrange("p o c -> p (o c)"),
                                              meanvar[k][:, t, 0:1], rstd[k][:, t:t + 1], ALU.subtract, ALU.mult).then_inc(ln_xn[k], 1)
                            dve.tensor_scalar(xn[:, 2 * P:XCOLS].rearrange("p (r c) -> p r c", r=REP),
                                              X[:, bass.ds(2 * b + t, 1), 2 * P:D].to_broadcast([P, REP, TAIL]),
                                              meanvar[k][:, t, 0:1], rstd[k][:, t:t + 1], ALU.subtract, ALU.mult).then_inc(ln_xn[k], 1)

                    def ln_scale(k, b):
                        for t in range(2):
                            dve.wait_ge(ln_T[k], 2 * L + 2 * b + t + 1)
                            dve.tensor_tensor(u[k][t][:, :, :].rearrange("p s (q k) -> p s q k", q=2),
                                              slots((tbank if k else gemm)[t][:, 0:3 * P]),
                                              seq_mod(l, 2 * k + 1, b, t), ALU.mult).then_inc(ln_u[k], 1)

                    def softmax_shift(b, t):
                        dve.wait_ge(s_mm, 2 * L + 2 * b + t + 1)
                        sc = scores[:, :].rearrange("p (h k) -> p h k", k=SEQ)
                        dve.tensor_reduce(out=rowmax[t][:, :], in_=sc, axis=AX.X, op=ALU.max).then_inc(s_max, 1)
                        dve.wait_ge(s_max, 2 * L + 2 * b + t + 1)
                        ge(dve, pt_mm, 4 * L + 4 * (b - 1) + 2 * t + 2)
                        dve.tensor_tensor(prob[t][:, :, :], sc, rowmax[t][:, :].unsqueeze(2).to_broadcast([P, HEADS, SEQ]),
                                          ALU.subtract).then_inc(s_sub, 1)

                    def body(h, par, live):
                        if live[ST_QK]:
                            ln_scale(0, blk(h, par, ST_QK)[0])
                        norms = {k: blk(h, par, st)[0] for k, st in enumerate((ST_LN1, ST_LN2)) if live[st]}
                        if live[ST_SCORE]:
                            softmax_shift(blk(h, par, ST_SCORE)[0], 0)
                        if live[ST_PROJ]:
                            b, _ = blk(h, par, ST_PROJ)
                            for t in range(2):
                                ge(dve, os_lo, 4 * L + 4 * (b - 1) + 2 * t + 2)
                                dve.wait_ge(ot_mm, 2 * L + 2 * b + t + 1)
                                dve.tensor_copy(oT[t][:, :, :].rearrange("p s k -> p (s k)"), tbank[t][:, 0:3 * P]).then_inc(ot_sb, 1)
                        if norms:
                            ln_statistics(norms)
                        if live[ST_SCORE]:
                            softmax_shift(blk(h, par, ST_SCORE)[0], 1)
                        if live[ST_PV]:
                            b, _ = blk(h, par, ST_PV)
                            for t in range(2):
                                dve.wait_ge(pv_mm, 2 * L + 2 * b + t + 1)
                                res = tbank[t][:, 0:HEADS * VW].rearrange("p (h d) -> p h d", d=VW)
                                dve.reciprocal(rden[t][:, :], res[:, :, HD]).then_inc(o_rec, 1)
                                dve.wait_ge(o_rec, 2 * L + 2 * b + t + 1)
                                ge(dve, ot_mm, 2 * L + 2 * (b - 1) + t + 1)
                                dve.tensor_tensor(o[t][:, 0:D].rearrange("p (h d) -> p h d", d=HD), res[:, :, 0:HD],
                                                  rden[t][:, :].unsqueeze(2).to_broadcast([P, HEADS, HD]), ALU.mult).then_inc(o_norm, 1)
                                dve.wait_ge(o_norm, 2 * L + 2 * b + t + 1)
                                dve.tensor_copy(o[t][:, D:XCOLS].rearrange("p (r c) -> p r c", r=REP - 1),
                                                o[t][:, 2 * P:D].unsqueeze(1).to_broadcast([P, REP - 1, TAIL])).then_inc(o_full, 1)
                        if live[ST_QK]:
                            b, _ = blk(h, par, ST_QK)
                            for g, (h0, h1) in enumerate(GROUPS[:2]):
                                M, nh = (h1 - h0) * HD, h1 - h0
                                dve.wait_ge(qk_sb, 6 * L + 6 * b + g + 1)
                                ge(dve, s_mm, 2 * L + 2 * (b - 1) + 2)
                                dve.tensor_tensor(kbd[0:M, h0:h1, :], kT[0:M, g, :].unsqueeze(1).to_broadcast([M, nh, BLK]),
                                                  head_mask[0:M, h0:h1].unsqueeze(2).to_broadcast([M, nh, BLK]),
                                                  ALU.mult).then_inc(kbd_done, 1)
                        if l and live[ST_GATE]:
                            b, _ = blk(h, par, ST_GATE)
                            for t in range(2):
                                dve.wait_ge(lg_mm, 2 * b + t + 1)
                                dve.tensor_copy(logits[:, bass.ds(2 * b + t, 1), :].rearrange("p o e -> p (o e)"),
                                                tbank[t][:, 0:EXPERTS]).then_inc(lg_sb, 1)
                        for k, b in norms.items():
                            ln_normalize(k, b)
                        if live[ST_PROJ]:
                            b, _ = blk(h, par, ST_PROJ)
                            for t in range(2):
                                ge(dve, x_attn, 2 * L + 2 * (b - 1) + t + 1)
                                dve.wait_ge(pj_mm, 2 * L + 2 * b + t + 1)
                                dve.tensor_tensor(y[t][:, :], tbank[t][:, 0:D], bproj_bc[l][:, :], ALU.add).then_inc(y_bias, 1)
                        if live[ST_LN2]:
                            ln_scale(1, blk(h, par, ST_LN2)[0])

                    def rest_of_x():
                        if l == 0:
                            dve.wait_ge(x_rest, 48)

                    def next_weights():
                        for c in range(SLICES):
                            split_w1_lo(dve, ph + 1, c)
                    if l == 0:
                        dve.wait_ge(x_first, 16)
                    steps(dve, body, {0: value_bias, 1: proj_bias, 3: rest_of_x, NB + ST_PROJ - 1: next_weights})

                @block.tensor
                def _(pe):
                    w5 = w1[0]

                    def proj_bias():
                        pe.wait_ge(bv_done, 4 * l + 4)
                        for n, (s, ws, rows) in enumerate(((0, 0, P), (0, 2, P), (1, 1, P), (1, 3, P), (2, 4, 3 * TAIL))):
                            mm = pe.matmul(tbank[0][:, 0:D], bvB[0:rows, s, :], w5[0:rows, ws, 3 * D:HID].bitcast(F32),
                                           start=(n == 0), stop=(n == 4))
                        mm.then_inc(bv_mm, 1)

                    def proj_bias_read():
                        pe.wait_ge(bp_done, l + 1)

                    def transposes(src, dst):
                        for s in range(3):
                            mm = pe.transpose(dst[:, s * P:(s + 1) * P], src[:, s * P:(s + 1) * P], ident[:, :])
                        return mm

                    def score(h, par, t):
                        b, i = blk(h, par, ST_SCORE)
                        ge(pe, s_sub, 2 * L + 2 * b + t)
                        pe.wait_ge(kbd_done, 2 * L + 2 * b + 2)
                        pe.wait_ge(kbd_act, 5 * L + 5 * b + 5)
                        for g, h0, h1 in ((0, 0, 6), (1, 6, 8), (1, 8, 11), (2, 11, 16)):
                            M = (GROUPS[g][1] - GROUPS[g][0]) * HD
                            for half in range(2):
                                js = slice((2 * t + half) * SEQ, (2 * t + half + 1) * SEQ)
                                mm = pe.matmul(scores[half * SEQ:(half + 1) * SEQ, h0 * SEQ:h1 * SEQ],
                                               qT[i][0:M, g, js], kbd[0:M, h0:h1, js], start=True, stop=True)
                        mm.then_inc(s_mm, 1)

                    def prob_transposes(h, par, t):
                        b, _ = blk(h, par, ST_PV)
                        pe.wait_ge(s_exp, 2 * L + 2 * b + t + 1)
                        pairs = prob[t][:, :, :].rearrange("p h k -> p (h k)")
                        for c in range(2):
                            ge(pe, pt_sb, 4 * L + 4 * b + 2 * t + c - 1)
                            for q in range(4):
                                n = 4 * c + q
                                mm = pe.transpose(probT_ps[:, n * P:(n + 1) * P], pairs[:, n * P:(n + 1) * P], ident[:, :])
                            mm.then_inc(pt_mm, 1)

                    def body(h, par, live):
                        if live[ST_SCORE]:
                            score(h, par, 0)
                        if live[ST_PV]:
                            prob_transposes(h, par, 0)
                        if live[ST_PROJ]:
                            b, _ = blk(h, par, ST_PROJ)
                            for t in range(2):
                                pe.wait_ge(o_full, 2 * L + 2 * b + t + 1)
                                tbank_free(pe, h, par, live, OT, t)
                                transposes(o[t], tbank[t]).then_inc(ot_mm, 1)
                        if live[ST_PV]:
                            prob_transposes(h, par, 1)
                        if live[ST_SCORE]:
                            score(h, par, 1)
                        if live[ST_PV]:
                            b, i = blk(h, par, ST_PV)
                            pe.wait_ge(v_sb, 8 * L + 8 * b + 8)
                            for t in range(2):
                                pe.wait_ge(pt_sb, 4 * L + 4 * b + 2 * t + 2)
                                tbank_free(pe, h, par, live, PV, t)
                                for n in range(HEADS // 2):
                                    for half in range(2):
                                        mm = pe.matmul(tbank[t][half * SEQ:(half + 1) * SEQ, n * 2 * VW:(n + 1) * 2 * VW],
                                                       probT[t][:, n * P + half * SEQ:n * P + (half + 1) * SEQ],
                                                       vbd[i][:, 2 * t + half, n, :], start=True, stop=True)
                                mm.then_inc(pv_mm, 1)
                        if live[ST_QK]:
                            b, i = blk(h, par, ST_QK)
                            pe.wait_ge(h_lo, 4 * L + 4 * b + 4)
                            for n in range(6):
                                h0, h1 = GROUPS[n % 3]
                                M = (h1 - h0) * HD
                                c0 = (1 - n // 3) * D + h0 * HD
                                if n >= 2:
                                    pe.wait_ge(qk_sb, 6 * L + 6 * b + n - 1)
                                seven(pe, gemm[n % 2][0:M, 0:BLK], lambda s, r: w5[0:r, s, c0:c0 + M],
                                      lambda s, r: hs[i][0:r, s, :], True).then_inc(qk_mm, 1)
                        if l and live[ST_GATE]:
                            b, _ = blk(h, par, ST_GATE)
                            for t in range(2):
                                pe.wait_ge(ln_v[1], 2 * L + 2 * b + t + 1)
                                tbank_free(pe, h, par, live, GATE, t)
                                for s, rows in enumerate((P, P, TAIL)):
                                    mm = pe.matmul(tbank[t][:, 0:EXPERTS], u[1][t][0:rows, s, :], wg[0:rows, s, :],
                                                   start=(s == 0), stop=(s == 2))
                                mm.then_inc(lg_mm, 1)
                        if live[ST_QK]:
                            b, i = blk(h, par, ST_QK)
                            for t in range(2):
                                pe.wait_ge(qk_sb, 6 * L + 6 * b + 4 + t + 1)
                                ts = slice(t * P, (t + 1) * P)
                                seven(pe, gemm[t][:, 0:D], lambda s, r: hs[i][0:r, s, ts],
                                      lambda s, r: w5[0:r, s, 2 * D:3 * D], False).then_inc(v_mm, 1)
                        if live[ST_PROJ]:
                            b, _ = blk(h, par, ST_PROJ)
                            for t in range(2):
                                ts = slice(t * P, (t + 1) * P)
                                pe.wait_ge(os_lo, 4 * L + 4 * b + 2 * t + 2)
                                tbank_free(pe, h, par, live, PROJ, t)
                                seven(pe, tbank[t][:, 0:D], lambda s, r: os5[0:r, s, ts],
                                      lambda s, r: w5[0:r, s, 3 * D:HID], False).then_inc(pj_mm, 1)
                        if live[ST_LN1]:
                            b, _ = blk(h, par, ST_LN1)
                            for t in range(2):
                                pe.wait_ge(ln_xn[0], 4 * L + 4 * b + 2 * t + 2)
                                if live[ST_QK]:
                                    pe.wait_ge(v_sb, 8 * L + 8 * (b - 1) + 4 * t + 4)
                                transposes(u[0][t][:, :, :].rearrange("p s k -> p (s k)"), gemm[t]).then_inc(ln_T[0], 1)
                        if live[ST_LN2]:
                            b, _ = blk(h, par, ST_LN2)
                            for t in range(2):
                                pe.wait_ge(ln_xn[1], 4 * L + 4 * b + 2 * t + 2)
                                tbank_free(pe, h, par, live, LN2, t)
                                transposes(u[1][t][:, :, :].rearrange("p s k -> p (s k)"), tbank[t]).then_inc(ln_T[1], 1)
                    steps(pe, body, {1: proj_bias, 2: proj_bias_read})

        def mlp(passes):
            l = min(passes[0], 1)

            def steps(eng, body):
                for g in passes:
                    body(g, 0, 0)
                    body(g, 1, 1)
                    body(g, 2, 0)
                    with eng.Fori(2, NB // 2) as h:
                        body(g, 2 * h - 1, 1)
                        body(g, 2 * h, 0)
                    body(g, NB - 1, 1)

            def before(g, b):
                if isinstance(b, int) and b == 0:
                    return (g - 1, NB - 1) if g - 1 in passes else None
                return g, b - 1

            def behind(g, b):
                if isinstance(b, int) and b == NB - 1:
                    return (g + 1, 0) if g + 1 in passes else None
                return g, b + 1

            def splits_next(g, b, m):
                return isinstance(b, int) and b == 2 and m % SLICES == 0 and g < PASSES_MLP - 1

            with nc.Block() as block:
                @block.sync
                def _(sp):
                    for g in passes:
                        ph, N = phase_of_mlp(g), NB * g

                        def gates(b, par):
                            if not (isinstance(b, int) and b < 2 and g == passes[0]):
                                sp.wait_ge(x_mlp, 2 * N + 2 * (b - 2) + 2)
                            gate_load(sp, l, 1, b, par)
                        gates(0, 0)
                        if ph < 6:
                            if g > 1:
                                sp.wait_ge(f1_mm, MCH * N)
                            sp.wait_ge(w_lo, SPLIT * (ph + 1))
                            load_w1(sp, ph + 1)
                            load_w1C(sp, ph + 1)
                        gates(1, 1)
                        if 0 < g < PASSES_MLP - 1:
                            sp.wait_ge(gelu_sb, MCH * N)
                            sp.wait_ge(z_bias, 2 * N)
                            load_mlp_bias(sp, g + 1)
                            sp.wait_ge(wd_lo, MCH * (g + 1))
                            load_wdn(sp, g + 1)

                        def store(b):
                            sp.dma_start(out.rearrange("(t p) c -> p t c", p=P)[:, bass.ds(2 * b, 2), :],
                                         X[:, bass.ds(2 * b, 2), :]).then_inc(out_done, 16)
                        with sp.Fori(1, NB // 2) as h:
                            for par in range(2):
                                gates(2 * h + par, par)
                                if g == PASSES_MLP - 1:
                                    store(2 * h + par - 2)
                        if g == PASSES_MLP - 1:
                            for b in (NB - 2, NB - 1):
                                sp.wait_ge(x_mlp, 2 * N + 2 * b + 2)
                                store(b)
                            sp.wait_ge(out_done, 16 * NB)

                @block.gpsimd
                def _(pool):
                    for g in passes:
                        N = NB * g
                        with pool.Fori(0, NB // 2) as h:
                            for par in range(2):
                                b = 2 * h + par
                                for t in range(2):
                                    pool.wait_ge(z_gate, 2 * N + 2 * b + t + 1)
                                    pool.tensor_tensor(tile(b, t), tile(b, t), y[t][:, :], ALU.add).then_inc(x_mlp, 1)

                @block.scalar
                def _(act):
                    def split(g, b, i):
                        N = NB * g
                        ge(act, f1_mm, MCH * N + MCH * (b - 1))
                        cols = bass.ds(b * BLK, BLK)
                        act.activation(hs[i][:, 0:2, :], HT[:, 0:2, cols], ACT.Copy).then_inc(m_hi, 1)
                        act.activation(hs[i][0:3 * TAIL, 4, :], HT[0:3 * TAIL, 2, cols], ACT.Copy).then_inc(m_hi, 1)
                    split(passes[0], 0, 0)

                    def body(g, b, i):
                        first = isinstance(b, int) and b == 0
                        if first:
                            act.wait_ge(bias_in, 32 * (g + 1))
                            act.wait_ge(wdn_in, 16 * (g + 1))
                        for m in range(MCH):
                            n = MCH * NB * g + MCH * b + m
                            act.wait_ge(f1_mm, n + 1)
                            ge(act, g_lo, n - 2)
                            act.activation(gel[m % 3][:, :], up_ps[m % 3], ACT.Gelu_apprx_tanh, bias=bup[g % 2][:, m:m + 1]).then_inc(gelu_sb, 1)
                            if first:
                                ge(act, f2_mm, MCH * (NB * g - 1) + m + 1)
                                act.activation(wdn[0][:, m, :], wraw[:, m, :], ACT.Copy).then_inc(wd_hi, 1)
                            if splits_next(g, b, m):
                                split_w1_hi(act, phase_of_mlp(g) + 1, m // SLICES)
                            if m == 4 and behind(g, b):
                                split(*behind(g, b), 1 - i)
                            if m == 3 and g == 1 and first:
                                act.wait_ge(route, 1)
                                act.activation(esel[:, :, :], esel[:, :, :], ACT.Exp).then_inc(route_e, 1)
                    steps(act, body)

                @block.vector
                def _(dve):
                    def split(g, b, i):
                        N = NB * g
                        dve.wait_ge(m_hi, 2 * N + 2 * b + 2)
                        cols = bass.ds(b * BLK, BLK)
                        dve.tensor_tensor(hs[i][:, 2:4, :], HT[:, 0:2, cols], hs[i][:, 0:2, :].bitcast(F32), ALU.subtract).then_inc(m_lo, 1)
                        low = hs[i][TAIL:2 * TAIL, 4, :]
                        dve.tensor_tensor(low, HT[TAIL:2 * TAIL, 2, cols], low.bitcast(F32), ALU.subtract).then_inc(m_lo, 1)
                    split(passes[0], 0, 0)

                    def evacuate(g, b, i):
                        N, ph = NB * g, phase_of_mlp(g)
                        for t in range(2):
                            if t == 0:
                                dve.wait_ge(f2_mm, MCH * N + MCH * b + MCH)
                            ge(dve, x_mlp, 2 * N + 2 * (b - 1) + t + 1)
                            dve.tensor_tensor(y[t][:, :], down_ps[i][t][:, 0:D], bdown_bc[g % 2][:, :], ALU.add).then_inc(z_bias, 1)
                        dve.wait_ge(gate_in[i], 256 * ph + 16 * (b - i) + 32)
                        for t in range(2):
                            dve.wait_ge(z_bias, 2 * N + 2 * b + t + 1)
                            if g == 0:
                                dve.tensor_tensor(y[t][:, :], y[t][:, :], gate_bc[i][:, t, :], ALU.mult).then_inc(z_gate, 1)
                            else:
                                weight = cw[:, bass.ds(2 * b + t, 1), g - 1]
                                dve.scalar_tensor_tensor(out=y[t][:, :], in0=y[t][:, :], scalar=weight,
                                                         in1=gate_bc[i][:, t, :], op0=ALU.mult, op1=ALU.mult).then_inc(z_gate, 1)

                    def body(g, b, i):
                        first = isinstance(b, int) and b == 0
                        for m in range(MCH):
                            n = MCH * NB * g + MCH * b + m
                            r = m % 3
                            dve.wait_ge(gelu_sb, n + 1)
                            ge(dve, f2_mm, n - 2)
                            dve.tensor_copy(gelu_hi[r][:, :], gel[r][:, :]).then_inc(g_hi, 1)
                            dve.wait_ge(g_hi, n + 1)
                            dve.tensor_tensor(gelu_lo[r][:, :], gel[r][:, :], gelu_hi[r][:, :].bitcast(F32), ALU.subtract).then_inc(g_lo, 1)
                            if first:
                                dve.wait_ge(wd_hi, MCH * g + m + 1)
                                dve.tensor_tensor(wdn[1][:, m, :], wraw[:, m, :], wdn[0][:, m, :].bitcast(F32), ALU.subtract).then_inc(wd_lo, 1)
                            if g == 1 and first:
                                routing(dve, m)
                            if splits_next(g, b, m):
                                split_w1_lo(dve, phase_of_mlp(g) + 1, m // SLICES)
                            if m == 2:
                                if isinstance(b, int) and b == 1:
                                    dve.wait_ge(bias_in, 32 * (g + 1))
                                if before(g, b):
                                    evacuate(*before(g, b), 1 - i)
                            if m == 5 and behind(g, b):
                                split(*behind(g, b), 1 - i)
                    steps(dve, body)
                    evacuate(passes[-1], NB - 1, 1)

                @block.tensor
                def _(pe):
                    def up(g, b, i, m):
                        N, ph = NB * g, phase_of_mlp(g)
                        n = MCH * N + MCH * b + m
                        if m == 0:
                            pe.wait_ge(m_lo, 2 * N + 2 * b + 2)
                        ge(pe, gelu_sb, n - 2)
                        seven(pe, up_ps[m % 3], lambda s, r: w1[ph % 2][0:r, s, m * P:(m + 1) * P],
                              lambda s, r: hs[i][0:r, s, :], True).then_inc(f1_mm, 1)

                    def down(g, b, i, m):
                        N = NB * g
                        n = MCH * N + MCH * b + m
                        if m == 0:
                            ge(pe, z_bias, 2 * N + 2 * (b - 2) + 2)
                        pe.wait_ge(g_lo, n + 1)
                        if isinstance(b, int) and b == 0:
                            pe.wait_ge(wd_lo, MCH * g + m + 1)
                        for t in range(2):
                            ts = slice(t * P, (t + 1) * P)
                            for q, (a, w) in enumerate(((gelu_hi, 0), (gelu_hi, 1), (gelu_lo, 0))):
                                mm = pe.matmul(down_ps[i][t][:, 0:D], a[m % 3][:, ts], wdn[w][:, m, :],
                                               start=(m == 0 and q == 0), stop=(m == MCH - 1 and q == 2))
                        mm.then_inc(f2_mm, 1)

                    def body(g, b, i):
                        if isinstance(b, int) and b == 0:
                            pe.wait_ge(w_lo, SPLIT * (phase_of_mlp(g) + 1))
                        for m in range(MCH):
                            up(g, b, i, m)
                            if m >= 2:
                                down(g, b, i, m - 2)
                            elif before(g, b):
                                down(*before(g, b), 1 - i, MCH - 2 + m)
                    steps(pe, body)
                    down(passes[-1], NB - 1, 1, MCH - 2)
                    down(passes[-1], NB - 1, 1, MCH - 1)

        route_steps = [0]

        def routing(dve, m):
            def link(op):
                op.then_inc(route_step, 1)
                route_steps[0] += 1
                dve.wait_ge(route_step, route_steps[0])

            lg = [logits[:, :, e] for e in range(EXPERTS)]
            if m == 0:
                link(dve.tensor_reduce(out=lmax[:, :], in_=logits[:, :, :], axis=AX.X, op=ALU.max))
                dve.tensor_tensor(esel[:, :, :], logits[:, :, :], lmax[:, :].unsqueeze(2).to_broadcast([P, TILES, EXPERTS]),
                                  ALU.subtract).then_inc(route, 1)
                link(dve.memset(rank[:, :, :], 0.0))
            elif m <= EXPERTS:
                e = m - 1
                for j in range(EXPERTS):
                    if j != e:
                        link(dve.tensor_tensor(cmp[:, :], lg[j], lg[e], ALU.is_ge if j < e else ALU.is_gt))
                        link(dve.tensor_tensor(rank[:, e, :], rank[:, e, :], cmp[:, :], ALU.add))
            elif m in (6, 7):
                dve.wait_ge(route_e, 1)
                for e in (2 * (m - 6), 2 * (m - 6) + 1):
                    link(dve.tensor_scalar(cmp[:, :], rank[:, e, :], 2.0, None, ALU.is_lt))
                    link(dve.tensor_tensor(esel[:, :, e], esel[:, :, e], cmp[:, :], ALU.mult))
            elif m == 8:
                link(dve.tensor_reduce(out=esum[:, :], in_=esel[:, :, :], axis=AX.X, op=ALU.add))
                link(dve.reciprocal(cmp[:, :], esum[:, :]))
                link(dve.tensor_tensor(cw[:, :, :], esel[:, :, :], cmp[:, :].unsqueeze(2).to_broadcast([P, TILES, EXPERTS]), ALU.mult))

        attention(0)
        mlp([0])
        attention(1)
        mlp(list(range(1, PASSES_MLP)))


def kernel(x, cond_1152, L0_cond_w_qkv, L0_cond_b_qkv, L0_cond_w_proj, L0_cond_b_proj, L0_cond_w_fc1,
           L0_cond_b_fc1, L0_cond_w_fc2, L0_cond_b_fc2, L0_cond_w_ada, L0_cond_b_ada, L1_cond_w_adaln,
           L1_cond_b_adaln, L1_cond_w_qkv, L1_cond_b_qkv, L1_cond_w_proj, L1_cond_b_proj, L1_cond_w_gate,
           L1_cond_w1, L1_cond_b1, L1_cond_w2, L1_cond_b2):
    import numpy as np
    import concourse.bacc as bacc
    from concourse.bass_utils import run_bass_kernel_spmd

    nc = bacc.Bacc("TRN2", target_bir_lowering=False, num_devices=1)
    arrays = {}

    def given(name, a, shape=None):
        a = np.ascontiguousarray(a)
        if shape is not None:
            a = a.reshape(shape)
        arrays[name] = a
        return nc.dram_tensor(name, a.shape, mybir.dt.from_np(a.dtype), kind="ExternalInput").ap()

    tokens = NSEQ * SEQ
    w1 = given("w1", L1_cond_w1)
    b1 = given("b1", L1_cond_b1)
    w2 = given("w2", L1_cond_w2)
    b2 = given("b2", L1_cond_b2)
    result = nc.dram_tensor("result", (tokens, D), F32, kind="ExternalOutput").ap()
    build(
        nc,
        given("tokens", x, (tokens, D)),
        given("cond", cond_1152),
        [given("w_qkv0", L0_cond_w_qkv), given("w_qkv1", L1_cond_w_qkv)],
        [given("b_qkv0", L0_cond_b_qkv), given("b_qkv1", L1_cond_b_qkv)],
        [given("w_proj0", L0_cond_w_proj), given("w_proj1", L1_cond_w_proj)],
        [given("b_proj0", L0_cond_b_proj), given("b_proj1", L1_cond_b_proj)],
        [given("w_fc1", L0_cond_w_fc1)] + [w1[e] for e in range(EXPERTS)],
        [given("b_fc1", L0_cond_b_fc1)] + [b1[e] for e in range(EXPERTS)],
        [given("w_fc2", L0_cond_w_fc2)] + [w2[e] for e in range(EXPERTS)],
        [given("b_fc2", L0_cond_b_fc2)] + [b2[e] for e in range(EXPERTS)],
        [given("w_ada0", L0_cond_w_ada), given("w_ada1", L1_cond_w_adaln)],
        [given("b_ada0", L0_cond_b_ada), given("b_ada1", L1_cond_b_adaln)],
        given("w_gate", L1_cond_w_gate),
        result,
    )
    r = run_bass_kernel_spmd(nc, [arrays], core_ids=[0])
    return r.results[0]["result"].reshape(NSEQ, SEQ, D)
```

```python
import concourse.bass as bass
from concourse import mybir
from contextlib import ExitStack

F32 = mybir.dt.float32
F32R = mybir.dt.float32r
ALU = mybir.AluOpType
ACT = mybir.ActivationFunctionType
AX = mybir.AxisListType

P = 128
NSEQ, SEQ, D = 64, 64, 288
HEADS = 16
HD = D // HEADS
HID = 4 * D
EXPERTS = 4
TILES = NSEQ * SEQ // P
BLK = 2 * P
NB = NSEQ * SEQ // BLK
MCH = HID // P
EPS = 1e-6
LAYERS = 2
PASSES_MLP = 1 + EXPERTS
TAIL = D - 2 * P
REP = P // TAIL
XCOLS = 3 * P
GROUPS = [(0, 7), (7, 14), (14, 16)]
KEYS2 = 64
M2 = KEYS2 + (GROUPS[2][1] - GROUPS[2][0]) * HD
K_, Q_ = 1, 0
QK_ITEMS = [[(K_, 0, 0)], [(K_, 1, 0)], [(Q_, 0, 0)], [(Q_, 1, 0)], [(K_, 2, KEYS2), (Q_, 2, 0)]]
QK_SB = [0, 1, 2, 3, 4, 6]
BANK_HEADS = 512 // SEQ
SCORE_PARTS = [[(0, 0, 7), (1, 7, 8)], [(1, 8, 14), (2, 14, 16)]]
KBD_DVE = (0, 6)
KBD_POOL = (7, 12)
KBD_ACT = [6] + list(range(12, HEADS))
PAIRS = [(0, 0, P), (1, 1, P), (0, 2, P), (1, 3, P), (2, 0, P), (3, 1, P), (4, 4, 3 * TAIL)]
VW = HD + 1
ST_LN1, ST_QK, ST_SCORE, ST_PV, ST_PROJ, ST_LN2, ST_GATE = range(7)
DEPTH = ST_GATE


def build(nc, x, cond, w_qkv, b_qkv, w_proj, b_proj, w_up, b_up, w_down, b_down, w_ada, b_ada,
          w_gate, out):
    ctx = ExitStack()
    with ctx:
        def sb(name, shape, dt=F32):
            return ctx.enter_context(nc.sbuf_tensor(name, shape, dt))

        def sem(name):
            return ctx.enter_context(nc.semaphore(name))

        X = sb("X", [P, TILES, D])
        HT = sb("HT", [P, 3, TILES * P])
        hs = [sb(f"hs{i}", [P, 5, BLK], F32R) for i in range(2)]
        ident = sb("ident", [P, P])
        mods = [sb(f"mods{l}", [P, 4, 3, NSEQ]) for l in range(LAYERS)]
        head_mask = sb("head_mask", [P, HEADS])
        mhalf = sb("mhalf", [P, 2])
        warm = sb("warm", [P, 2])
        gate_bc = [sb(f"gate_bc{i}", [P, 2, D]) for i in range(2)]
        y = [sb(f"y{t}", [P, D]) for t in range(2)]
        bproj_bc = [sb(f"bproj_bc{l}", [P, D]) for l in range(LAYERS)]
        bqk = [sb(f"bqk{l}", [P, 6]) for l in range(LAYERS)]
        bv = sb("bv", [P, LAYERS, 3])
        bdown_bc = [sb(f"bdown_bc{i}", [P, D]) for i in range(2)]
        bup = [sb(f"bup{i}", [P, MCH]) for i in range(2)]
        logits = sb("logits", [P, TILES, EXPERTS])
        cw = sb("cw", [P, TILES, EXPERTS])
        wg = sb("wg", [P, 3, EXPERTS])
        stats = [sb(f"stats{k}", [P, 2, 6]) for k in range(2)]
        meanvar = [sb(f"meanvar{k}", [P, 2, 2]) for k in range(2)]
        vareps = [sb(f"vareps{k}", [P, 2]) for k in range(2)]
        rstd = [sb(f"rstd{k}", [P, 2]) for k in range(2)]
        rowmax = [sb(f"rowmax{t}", [P, HEADS]) for t in range(2)]
        rden = [sb(f"rden{t}", [P, HEADS]) for t in range(2)]

        base = nc.sbuf_base
        top = nc.sbuf_usable_end

        class Region:
            def __init__(self, at):
                self.at = at

            def take(self, name, shape, dt=F32):
                n = 4
                for k in shape[1:]:
                    n *= k
                t = nc.alloc_sbuf_tensor_at(name, shape, dt, offset=self.at)
                self.at += (n + 31) // 32 * 32
                assert self.at <= top, (name, self.at, top)
                return t

        ctx.enter_context(nc.sbuf_tensor("fence", [P, (top - base) // 4 - 64], F32))
        W1_BYTES, WDN_BYTES = 4 * 5 * HID, 4 * MCH * D
        at_w1b = base + W1_BYTES + 3 * WDN_BYTES
        at_rest = at_w1b + W1_BYTES

        r = Region(base)
        w1b = r.take("w1b", [P, 5, HID], F32R)
        wdn = [r.take(f"wdn{i}", [P, MCH, D], F32R) for i in range(2)]
        wraw = r.take("wraw", [P, MCH, D])
        w1a = r.take("w1a", [P, 5, HID], F32R)
        w1 = [w1a, w1b]
        w1raw = [Region(at_w1b).take("w1a_raw", [P, 5, HID]), Region(base).take("w1b_raw", [P, 5, HID])]
        wrawC = r.take("wrawC", [P, HID])
        gel = [r.take(f"gel{i}", [P, BLK]) for i in range(3)]
        gelu_hi = [r.take(f"gelu_hi{i}", [P, BLK], F32R) for i in range(3)]
        gelu_lo = [r.take(f"gelu_lo{i}", [P, BLK], F32R) for i in range(3)]
        rank = r.take("rank", [P, TILES, EXPERTS])
        cmp = r.take("cmp", [P, TILES, EXPERTS])
        ncmp = r.take("ncmp", [P, TILES])
        lmax = r.take("lmax", [P, TILES])
        esel = r.take("esel", [P, TILES, EXPERTS])
        esum = r.take("esum", [P, TILES])

        r = Region(base)
        kbd = r.take("kbd", [P, HEADS, BLK])
        qT = [r.take(f"qT{i}", [P, 3, BLK]) for i in range(2)]
        assert r.at <= base + W1_BYTES
        r = Region(base + W1_BYTES)
        kT = r.take("kT", [P, 3, BLK])
        vbd = [r.take(f"vbd{i}", [P, 4, HEADS // 2, 2 * VW]) for i in range(2)]
        os5 = r.take("os5", [P, 5, BLK], F32R)
        wqk2 = r.take("wqk2", [P, 5, M2], F32R)
        assert r.at <= base + W1_BYTES + 2 * WDN_BYTES
        r = Region(base + W1_BYTES + 2 * WDN_BYTES)
        prob = [r.take(f"prob{t}", [P, HEADS, SEQ]) for t in range(2)]
        u01 = r.take("u01", [P, 3, P])
        assert r.at <= at_w1b
        r = Region(at_rest)
        probT = [r.take(f"probT{t}", [P, 8 * P]) for t in range(2)]
        u = [[r.take("u00", [P, 3, P]), u01], [r.take(f"u1{t}", [P, 3, P]) for t in range(2)]]
        o = [r.take(f"o{t}", [P, XCOLS]) for t in range(2)]
        oT = [r.take(f"oT{t}", [P, 3, P]) for t in range(2)]
        r = Region(r.at - 2 * 4 * 3 * P)
        bvB = r.take("bvB", [P, 3, P])
        onesr = r.take("onesr", [P, P])

        r = Region(base)
        wada0 = r.take("wada0", [P, 3, 6 * D])
        cnd = r.take("cnd", [NSEQ, D])
        scond = r.take("scond", [NSEQ, D])
        scT = r.take("scT", [P, 3, NSEQ])
        assert r.at <= at_w1b
        free = HT[:, :, :].rearrange("p s n -> p (s n)")
        wada = [wada0, free[:, 0:3 * 6 * D].rearrange("p (s n) -> p s n", s=3)]
        ada = [free[0:NSEQ, (18 + 6 * l) * D:(24 + 6 * l) * D] for l in range(LAYERS)]
        adaC = [free[0:NSEQ, 30 * D + 4 * P * l:30 * D + 4 * P * (l + 1)].rearrange("b (v r c) -> b v r c", v=4, r=REP)
                for l in range(LAYERS)]

        gates_d = nc.dram_tensor("gates_d", (LAYERS, 2, NSEQ, D), F32).ap()

        scores = ctx.enter_context(nc.psum_tensor("scores", [P, 1024], F32))
        probT_ps = ctx.enter_context(nc.psum_tensor("probT_ps", [P, 1024], F32))
        gemm = [ctx.enter_context(nc.psum_tensor(f"gemm{i}", [P, 512], F32)) for i in range(2)]
        tbank = [ctx.enter_context(nc.psum_tensor(f"tbank{i}", [P, 512], F32)) for i in range(2)]
        up_ps = [scores[:, 0:BLK], scores[:, 512:512 + BLK], probT_ps[:, 0:BLK]]
        down_ps = [[gemm[0], gemm[1]], [tbank[0], tbank[1]]]

        x_first, x_rest, cond_in = map(sem, ("x_first", "x_rest", "cond_in"))
        small_in = [sem(f"small_in{l}") for l in range(LAYERS)]
        bias_in = [sem(f"bias_in{i}") for i in range(2)]
        gates_out = [sem(f"gates_out{l}") for l in range(LAYERS)]
        wada_in = [sem(f"wada_in{l}") for l in range(LAYERS)]
        w1_in, wdn_in, out_done = map(sem, ("w1_in", "wdn_in", "out_done"))
        gate_in = [sem(f"gate_in{i}") for i in range(2)]
        const_done, silu_done, silu_mm, silu_sb = map(sem, ("const_done", "silu_done", "silu_mm", "silu_sb"))
        ada_mm, ada_sb, adaC_sb, mods_mm, mods_sb = map(sem, ("ada_mm", "ada_sb", "adaC_sb", "mods_mm", "mods_sb"))
        w_hi, w_lo, wd_hi, wd_lo, w2_done, bv_done, bv_mm, bp_done, vbd_init = map(sem, (
            "w_hi", "w_lo", "wd_hi", "wd_lo", "w2_done", "bv_done", "bv_mm", "bp_done", "vbd_init"))
        ln_stats, ln_mv, ln_ve, ln_rstd, ln_xn, ln_T, ln_u, ln_v = (
            [sem(f"{n}{k}") for k in range(2)] for n in (
                "ln_stats", "ln_mv", "ln_ve", "ln_rstd", "ln_xn", "ln_T", "ln_u", "ln_v"))
        h_hi, h_lo, ht_done = map(sem, ("h_hi", "h_lo", "ht_done"))
        qk_mm, qk_sb, v_mm, v_sb, kbd_done, kbd_act, kbd_pool = map(sem, (
            "qk_mm", "qk_sb", "v_mm", "v_sb", "kbd_done", "kbd_act", "kbd_pool"))
        s_mm, s_max, s_sub, s_exp = map(sem, ("s_mm", "s_max", "s_sub", "s_exp"))
        pt_mm, pt_sb, pv_mm, o_rec, o_norm, o_full = map(sem, (
            "pt_mm", "pt_sb", "pv_mm", "o_rec", "o_norm", "o_full"))
        ot_mm, ot_sb, os_hi, os_lo, pj_mm, y_bias, y_gate, x_attn = map(sem, (
            "ot_mm", "ot_sb", "os_hi", "os_lo", "pj_mm", "y_bias", "y_gate", "x_attn"))
        lg_mm, lg_sb = map(sem, ("lg_mm", "lg_sb"))
        m_hi, m_lo, f1_mm, gelu_sb, g_hi, g_lo, f2_mm, z_bias, z_gate, x_mlp, route = map(sem, (
            "m_hi", "m_lo", "f1_mm", "gelu_sb", "g_hi", "g_lo", "f2_mm", "z_bias", "z_gate",
            "x_mlp", "route"))
        route_e, route_step = map(sem, ("route_e", "route_step"))

        def seven(pe, dst, stationary, moving, w_first):
            for n, (ws, xs, rows) in enumerate(PAIRS):
                a, b = (ws, xs) if w_first else (xs, ws)
                mm = pe.matmul(dst, stationary(a, rows), moving(b, rows),
                               start=(n == 0), stop=(n == len(PAIRS) - 1))
            return mm

        def phase_of_mlp(g):
            return 1 if g == 0 else 2 + g

        WCOLS = {0: ((w_qkv[0], 0), (w_proj[0], 3 * D)), 2: ((w_qkv[1], 0), (w_proj[1], 3 * D))}
        for g in range(PASSES_MLP):
            WCOLS[phase_of_mlp(g)] = ((w_up[g], 0),)
        W1_IN = [0]
        for ph in range(7):
            W1_IN.append(W1_IN[-1] + 64 * len(WCOLS[ph]))

        def load_w1(sp, ph):
            dst = w1raw[ph % 2]
            for w, c0 in WCOLS[ph]:
                n = w.shape[1]
                sp.dma_start(dst[:, 2:4, c0:c0 + n], w[0:2 * P, :].rearrange("(s p) n -> p s n", p=P)).then_inc(w1_in, 16)

        def load_w1C(sp, ph):
            for w, c0 in WCOLS[ph]:
                n = w.shape[1]
                for c in range(3):
                    sp.dma_start(wrawC[c * TAIL:(c + 1) * TAIL, c0:c0 + n], w[2 * P:D, :]).then_inc(w1_in, 16)

        def load_wdn(sp, g):
            sp.dma_start(wraw[:, :, :], w_down[g].rearrange("(m p) n -> p m n", p=P)).then_inc(wdn_in, 16)

        SLICES = 3
        SPLIT = 2 * SLICES
        SCOLS = HID // SLICES

        def split_w1_hi(act, ph, c):
            w5, cs = w1[ph % 2], slice(c * SCOLS, (c + 1) * SCOLS)
            if c == 0:
                act.wait_ge(w1_in, W1_IN[ph + 1])
            act.activation(w5[:, 0:2, cs], w1raw[ph % 2][:, 2:4, cs], ACT.Copy).then_inc(w_hi, 1)
            act.activation(w5[0:3 * TAIL, 4, cs], wrawC[0:3 * TAIL, cs], ACT.Copy).then_inc(w_hi, 1)

        def split_w1_lo(dve, ph, c):
            w5, cs = w1[ph % 2], slice(c * SCOLS, (c + 1) * SCOLS)
            if c == 0:
                dve.wait_ge(w1_in, W1_IN[ph + 1])
            dve.wait_ge(w_hi, SPLIT * ph + 2 * c + 1)
            dve.tensor_tensor(w5[:, 2:4, cs], w1raw[ph % 2][:, 2:4, cs], w5[:, 0:2, cs].bitcast(F32),
                              ALU.subtract).then_inc(w_lo, 1)
            dve.wait_ge(w_hi, SPLIT * ph + 2 * c + 2)
            low = w5[2 * TAIL:3 * TAIL, 4, cs]
            dve.tensor_tensor(low, wrawC[2 * TAIL:3 * TAIL, cs], low.bitcast(F32), ALU.subtract).then_inc(w_lo, 1)

        def load_mlp_bias(sp, g):
            sp.dma_start(bup[g % 2][:, :], b_up[g].rearrange("(m p) -> p m", p=P),
                         allow_slow_non_contiguous=True).then_inc(bias_in[g % 2], 16)
            sp.dma_start(bdown_bc[g % 2][:, :], b_down[g].unsqueeze(0).to_broadcast([P, D])).then_inc(bias_in[g % 2], 16)

        NADA = 6 * D // 4
        ada_ps = [[gemm[0], gemm[1], tbank[0], tbank[1]],
                  [probT_ps[:, 0:512], probT_ps[:, 512:1024], scores[:, 512:1024], scores[:, 0:512]]]
        mods_ps = [gemm, tbank]
        SMALL = 6 + 4 + 1

        def load_ada(sp, l):
            sp.dma_start(wada[l][:, 0:2, :], w_ada[l][0:2 * P, :].rearrange("(s p) n -> p s n", p=P)).then_inc(wada_in[l], 16)
            sp.dma_start(wada[l][0:TAIL, 2, :], w_ada[l][2 * P:D, :]).then_inc(wada_in[l], 16)
            sp.dma_start(ada[l], b_ada[l].unsqueeze(0).to_broadcast([NSEQ, 6 * D])).then_inc(wada_in[l], 16)

        def load_small(eng, l):
            for g, (h0, h1) in enumerate(GROUPS):
                for q in range(2):
                    p0 = KEYS2 if q == K_ and g == 2 else 0
                    eng.dma_start(bqk[l][p0:p0 + (h1 - h0) * HD, 3 * q + g:3 * q + g + 1],
                                  b_qkv[l][q * D + h0 * HD:q * D + h1 * HD].unsqueeze(1)).then_inc(small_in[l], 16)
            for s, p0, rows in ((0, 0, P), (1, 0, P), (2, 0, TAIL), (2, 2 * TAIL, TAIL)):
                c0 = 2 * D + s * P
                eng.dma_start(bv[p0:p0 + rows, l, s:s + 1], b_qkv[l][c0:c0 + rows].unsqueeze(1)).then_inc(small_in[l], 16)
            eng.dma_start(bproj_bc[l][:, :], b_proj[l].unsqueeze(0).to_broadcast([P, D])).then_inc(small_in[l], 16)
            if l:
                eng.dma_start(wg[:, 0:2, :], w_gate[0:2 * P, :].rearrange("(s p) n -> p s n", p=P)).then_inc(small_in[l], 16)
                eng.dma_start(wg[0:TAIL, 2, :], w_gate[2 * P:D, :]).then_inc(small_in[l], 16)

        def init_vbd(pool, l):
            for i in range(2):
                pool.memset(vbd[i][:, :, :, :], 0.0).then_inc(vbd_init, 1)
            pool.wait_ge(vbd_init, 6 * l + 2)
            for i in range(2):
                pool.memset(vbd[i][0:SEQ, :, :, HD:HD + 1], 1.0).then_inc(vbd_init, 1)
                pool.wait_ge(vbd_init, 6 * l + 3 + 2 * i)
                pool.memset(vbd[i][SEQ:P, :, :, VW + HD:VW + HD + 1], 1.0).then_inc(vbd_init, 1)
                pool.wait_ge(vbd_init, 6 * l + 4 + 2 * i)

        def load_x(sp, q, done):
            sp.dma_start(X[:, 8 * q:8 * q + 8, :],
                         x[1024 * q:1024 * q + 1024, :].rearrange("(t p) c -> p t c", p=P)).then_inc(done, 16)

        def store_gates(sp, l):
            sp.wait_ge(ada_sb, 4 * l + 4)
            for q in range(2):
                c0 = (2 + 3 * q) * D
                sp.dma_start(gates_d[l, q], ada[l][:, c0:c0 + D]).then_inc(gates_out[l], 16)

        def ada_product(pe, l, j):
            if j == 0:
                pe.wait_ge(wada_in[l], 48)
            for k, rows in enumerate((P, P, TAIL)):
                mm = pe.matmul(ada_ps[l][j][0:NSEQ, 0:NADA], scT[0:rows, k, :], wada[l][0:rows, k, j * NADA:(j + 1) * NADA],
                               start=(k == 0), stop=(k == 2))
            mm.then_inc(ada_mm, 1)

        def ada_bias(dve, l, j):
            cs = slice(j * NADA, (j + 1) * NADA)
            if j == 0:
                dve.wait_ge(wada_in[l], 48)
            dve.wait_ge(ada_mm, 4 * l + j + 1)
            dve.tensor_tensor(ada[l][:, cs], ada_ps[l][j][0:NSEQ, 0:NADA], ada[l][:, cs], ALU.add).then_inc(ada_sb, 1)

        def repeat_tails(dve, l):
            dve.wait_ge(ada_sb, 4 * l + 4)
            for v, part in enumerate((0, 1, 3, 4)):
                c0 = part * D + 2 * P
                dve.tensor_copy(adaC[l][:, v, :, :], ada[l][:, c0:c0 + TAIL].unsqueeze(1).to_broadcast([NSEQ, REP, TAIL])).then_inc(adaC_sb, 1)

        def mods_transposes(pe, l):
            pe.wait_ge(ada_sb, 4 * l + 4)
            pe.wait_ge(adaC_sb, 4 * l + 4)
            for v, part in enumerate((0, 1, 3, 4)):
                for s in range(3):
                    c0 = (3 * (v % 2) + s) * NSEQ
                    src = (ada[l][:, part * D + s * P:part * D + (s + 1) * P] if s < 2 else
                           adaC[l][:, v, :, :].rearrange("b r c -> b (r c)"))
                    mm = pe.transpose(mods_ps[l][v // 2][:, c0:c0 + NSEQ], src, ident[0:NSEQ, 0:NSEQ])
                mm.then_inc(mods_mm, 1)

        def mods_copy(dve, l):
            for v in range(4):
                dve.wait_ge(mods_mm, 4 * l + v // 2 * 2 + 2)
                c0 = 3 * (v % 2) * NSEQ
                src = mods_ps[l][v // 2][:, c0:c0 + 3 * NSEQ].rearrange("p (s b) -> p s b", s=3)
                if v % 2:
                    dve.tensor_scalar(mods[l][:, v, :, :], src, 1.0, None, ALU.add).then_inc(mods_sb, 1)
                else:
                    dve.tensor_copy(mods[l][:, v, :, :], src).then_inc(mods_sb, 1)

        with nc.Block() as block:
            @block.sync
            def _(sp):
                sp.dma_start(cnd[:, :], cond).then_inc(cond_in, 16)
                load_ada(sp, 0)
                load_ada(sp, 1)
                load_w1(sp, 0)
                load_w1C(sp, 0)
                load_x(sp, 0, x_first)
                for q in range(1, 4):
                    load_x(sp, q, x_rest)
                for l in range(LAYERS):
                    store_gates(sp, l)

            @block.gpsimd
            def _(pool):
                pool.memset(ident[:, :], 0.0).then_inc(const_done, 1)
                pool.memset(head_mask[:, :], 1.0).then_inc(const_done, 1)
                pool.memset(bv[:, :, :], 0.0).then_inc(const_done, 1)
                pool.memset(mhalf[:, :], -0.5).then_inc(const_done, 1)
                pool.wait_ge(const_done, 4)
                pool.affine_select(out=ident[:, :], in_=ident[:, :], compare_op=ALU.not_equal, fill=1.0,
                                   base=0, pattern=[[-1, P]], channel_multiplier=1).then_inc(const_done, 1)
                n = 5
                for h0, h1 in GROUPS:
                    part = head_mask[:, h0:h1]
                    pool.affine_select(out=part, in_=part, compare_op=ALU.is_ge, fill=0.0,
                                       base=0, pattern=[[-HD, h1 - h0]], channel_multiplier=1).then_inc(const_done, 1)
                    n += 1
                    pool.wait_ge(const_done, n)
                    pool.affine_select(out=part, in_=part, compare_op=ALU.is_ge, fill=0.0,
                                       base=HD - 1, pattern=[[HD, h1 - h0]], channel_multiplier=-1).then_inc(const_done, 1)
                    n += 1
                init_vbd(pool, 0)

            @block.scalar
            def _(act):
                act.wait_ge(cond_in, 16)
                act.activation(scond[:, :], cnd[:, :], ACT.Silu).then_inc(silu_done, 1)
                act.wait_ge(const_done, 4)
                load_small(act, 0)
                for c in range(SLICES):
                    split_w1_hi(act, 0, c)

            @block.tensor
            def _(pe):
                pe.wait_ge(const_done, 11)
                pe.wait_ge(silu_done, 1)
                for s, (c0, c1) in enumerate(((0, P), (P, 2 * P), (2 * P, D))):
                    mm = pe.transpose(scores[0:c1 - c0, s * NSEQ:(s + 1) * NSEQ], scond[:, c0:c1], ident[0:NSEQ, 0:NSEQ])
                mm.then_inc(silu_mm, 1)
                pe.wait_ge(silu_sb, 1)
                for l in range(LAYERS):
                    for j in range(4):
                        ada_product(pe, l, j)
                for l in range(LAYERS):
                    mods_transposes(pe, l)

            @block.vector
            def _(dve):
                dve.wait_ge(silu_mm, 1)
                dve.tensor_copy(scT[:, 0:2, :], scores[:, 0:2 * NSEQ].rearrange("p (s b) -> p s b", s=2))
                dve.tensor_copy(scT[0:TAIL, 2, :], scores[0:TAIL, 2 * NSEQ:3 * NSEQ]).then_inc(silu_sb, 1)
                for l in range(LAYERS):
                    for j in range(4):
                        ada_bias(dve, l, j)
                        if l and j < SLICES:
                            split_w1_lo(dve, 0, j)
                    repeat_tails(dve, l)
                for l in range(LAYERS):
                    mods_copy(dve, l)

        def ge(eng, s, value):
            if not isinstance(value, int) or value > 0:
                eng.wait_ge(s, value)

        def group_of(head):
            return next(g for g, (h0, h1) in enumerate(GROUPS) if h0 <= head < h1)

        def mask_heads(eng, h0, h1):
            g = group_of(h0)
            M, nh = (GROUPS[g][1] - GROUPS[g][0]) * HD, h1 - h0
            return eng.tensor_tensor(kbd[0:M, h0:h1, :], kT[0:M, g, :].unsqueeze(1).to_broadcast([M, nh, BLK]),
                                     head_mask[0:M, h0:h1].unsqueeze(2).to_broadcast([M, nh, BLK]), ALU.mult)

        def tile(b, t):
            return X[:, bass.ds(2 * b + t, 1), :].rearrange("p o c -> p (o c)")

        def slots(ap):
            return ap.rearrange("p (s q k) -> p s q k", s=3, q=2)

        def seq_mod(l, v, b, t):
            return mods[l][:, v, :, bass.ds(4 * b + 2 * t, 2)].unsqueeze(3).to_broadcast([P, 3, 2, SEQ])

        def gate_load(sp, l, q, b, parity):
            for half in range(2):
                src = gates_d[l, q].rearrange("(t h) c -> h t c", h=2)[half, bass.ds(2 * b, 2), :]
                sp.dma_start(gate_bc[parity][half * SEQ:(half + 1) * SEQ, :, :],
                             src.unsqueeze(0).to_broadcast([SEQ, 2, D])).then_inc(gate_in[parity], 16)

        def attention(l):
            ph = 2 * l
            L = NB * l
            nstage = ST_GATE + 1
            ORDER = [(ST_PROJ, ot_sb, 2 * L), (ST_PV, o_norm, 2 * L)] + ([(ST_GATE, lg_sb, 0)] if l else []) + [
                (ST_PROJ, y_bias, 2 * L), (ST_LN2, ln_u[1], 2 * L)]
            OT, PV, GATE, PROJ, LN2 = 0, 1, 2, 2 + l, 3 + l

            def steps(eng, body, after={}):
                for s in range(DEPTH):
                    body(s // 2, s % 2, [0 <= s - k for k in range(nstage)])
                    if s in after:
                        after[s]()
                with eng.Fori(DEPTH // 2, NB // 2) as h:
                    for par in range(2):
                        body(h, par, [True] * nstage)
                for s in range(NB, NB + DEPTH):
                    body(s // 2, s % 2, [s - k < NB for k in range(nstage)])
                    if s in after:
                        after[s]()

            def blk(h, par, k):
                return 2 * h + (par - k), (par - k) % 2

            def tbank_free(pe, h, par, live, item, t):
                for back in range(4):
                    for j in reversed(range(item if back == 0 else len(ORDER))):
                        k, s, before = ORDER[j]
                        b = 2 * h + par - back - k
                        if isinstance(h, int):
                            if not 0 <= b < NB:
                                continue
                        pe.wait_ge(s, before + 2 * b + t + 1)
                        return

            with nc.Block() as block:
                @block.sync
                def _(sp):
                    sp.wait_ge(gates_out[l], 32)
                    gate_load(sp, l, 0, 0, 0)
                    gate_load(sp, l, 0, 1, 1)
                    if l == 0:
                        load_small(sp, 1)
                        load_mlp_bias(sp, 0)
                        load_mlp_bias(sp, 1)
                    with sp.Fori(1, NB // 2) as h:
                        for par in range(2):
                            sp.wait_ge(x_attn, 2 * L + 2 * (2 * h + par - 2) + 2)
                            gate_load(sp, l, 0, 2 * h + par, par)
                    sp.wait_ge(s_mm, 4 * L + 4 * NB)
                    load_w1(sp, ph + 1)
                    sp.wait_ge(pv_mm, 2 * L + 2 * NB)
                    load_w1C(sp, ph + 1)
                    load_wdn(sp, l)

                @block.gpsimd
                def _(pool):
                    if l:
                        init_vbd(pool, l)

                    def pow_rstd(k, b):
                        pool.wait_ge(ln_ve[k], L + b + 1)
                        pool.tensor_tensor(rstd[k][:, :], vareps[k][:, :], mhalf[:, :], ALU.pow).then_inc(ln_rstd[k], 1)

                    def shift(k, b):
                        for t in range(2):
                            pool.wait_ge(ln_u[k], 2 * L + 2 * b + t + 1)
                            ut = u[k][t][:, :, :].rearrange("p s (q k) -> p s q k", q=2)
                            pool.tensor_tensor(ut, ut, seq_mod(l, 2 * k, b, t), ALU.add).then_inc(ln_v[k], 1)

                    def body(h, par, live):
                        if live[ST_QK]:
                            b, i = blk(h, par, ST_QK)
                            shift(0, b)
                            for t in range(2):
                                ts = slice(t * P, (t + 1) * P)
                                pool.wait_ge(h_hi, 4 * L + 4 * b + 2 * t + 2)
                                pool.tensor_tensor(hs[i][:, 2:4, ts], u[0][t][:, 0:2, :],
                                                   hs[i][:, 0:2, ts].bitcast(F32), ALU.subtract).then_inc(h_lo, 1)
                                pool.wait_ge(h_lo, 4 * L + 4 * b + 2 * t + 1)
                                pool.tensor_tensor(hs[i][TAIL:2 * TAIL, 4, ts], u[0][t][TAIL:2 * TAIL, 2, :],
                                                   hs[i][TAIL:2 * TAIL, 4, ts].bitcast(F32), ALU.subtract).then_inc(h_lo, 1)
                                pool.wait_ge(h_lo, 4 * L + 4 * b + 2 * t + 2)
                        if live[ST_LN1]:
                            pow_rstd(0, blk(h, par, ST_LN1)[0])
                        if live[ST_LN2]:
                            pow_rstd(1, blk(h, par, ST_LN2)[0])
                        if live[ST_PROJ]:
                            b, _ = blk(h, par, ST_PROJ)
                            for t in range(2):
                                ts = slice(t * P, (t + 1) * P)
                                pool.wait_ge(os_hi, 4 * L + 4 * b + 2 * t + 2)
                                pool.tensor_tensor(os5[:, 2:4, ts], oT[t][:, 0:2, :],
                                                   os5[:, 0:2, ts].bitcast(F32), ALU.subtract).then_inc(os_lo, 1)
                                pool.wait_ge(os_lo, 4 * L + 4 * b + 2 * t + 1)
                                pool.tensor_tensor(os5[TAIL:2 * TAIL, 4, ts], oT[t][TAIL:2 * TAIL, 2, :],
                                                   os5[TAIL:2 * TAIL, 4, ts].bitcast(F32), ALU.subtract).then_inc(os_lo, 1)
                                pool.wait_ge(os_lo, 4 * L + 4 * b + 2 * t + 2)
                        if live[ST_QK]:
                            b, _ = blk(h, par, ST_QK)
                            pool.wait_ge(qk_sb, 6 * L + 6 * b + QK_SB[2])
                            ge(pool, s_mm, 4 * L + 4 * (b - 1) + 4)
                            mask_heads(pool, *KBD_POOL).then_inc(kbd_pool, 1)
                        if live[ST_PROJ]:
                            b, i = blk(h, par, ST_PROJ)
                            for t in range(2):
                                if t == 0:
                                    pool.wait_ge(gate_in[i], 256 * ph + 32 * (h + (par - ST_PROJ) // 2) + 32)
                                pool.wait_ge(y_bias, 2 * L + 2 * b + t + 1)
                                pool.tensor_tensor(y[t][:, :], y[t][:, :], gate_bc[i][:, t, :], ALU.mult).then_inc(y_gate, 1)
                                pool.wait_ge(y_gate, 2 * L + 2 * b + t + 1)
                                pool.tensor_tensor(tile(b, t), tile(b, t), y[t][:, :], ALU.add).then_inc(x_attn, 1)
                        if live[ST_LN2]:
                            shift(1, blk(h, par, ST_LN2)[0])
                    steps(pool, body)

                @block.scalar
                def _(act):
                    act.activation(warm[:, 0:1], mhalf[:, 0:1], ACT.Exp)
                    c0 = GROUPS[2][0] * HD
                    for part, rows in ((slice(0, 4), P), (slice(4, 5), 3 * TAIL)):
                        act.activation(wqk2[0:rows, part, 0:KEYS2], w1[0][0:rows, part, c0:c0 + KEYS2].bitcast(F32), ACT.Copy).then_inc(w2_done, 1)
                        act.activation(wqk2[0:rows, part, KEYS2:M2], w1[0][0:rows, part, D + c0:2 * D].bitcast(F32), ACT.Copy).then_inc(w2_done, 1)
                    act.wait_ge(small_in[l], 16 * SMALL + 32 * l)
                    act.wait_ge(vbd_init, 6 * (l + 1))

                    def body(h, par, live):
                        if live[ST_PV]:
                            b, _ = blk(h, par, ST_PV)
                            for t in range(2):
                                ge(act, pv_mm, 2 * L + 2 * (b - 1) + t + 1)
                                for c in range(2):
                                    act.wait_ge(pt_mm, 4 * L + 4 * b + 2 * t + c + 1)
                                    act.activation(probT[t][:, c * 512:(c + 1) * 512], probT_ps[:, c * 512:(c + 1) * 512],
                                                   ACT.Copy).then_inc(pt_sb, 1)
                        if live[ST_QK]:
                            b, i = blk(h, par, ST_QK)
                            ge(act, v_mm, 2 * L + 2 * (b - 2) + 2)
                            for t in range(2):
                                ts = slice(t * P, (t + 1) * P)
                                act.wait_ge(ln_v[0], 2 * L + 2 * b + t + 1)
                                act.activation(hs[i][:, 0:2, ts], u[0][t][:, 0:2, :], ACT.Copy).then_inc(h_hi, 1)
                                act.activation(hs[i][0:3 * TAIL, 4, ts], u[0][t][0:3 * TAIL, 2, :], ACT.Copy).then_inc(h_hi, 1)

                        def exps(t):
                            b, _ = blk(h, par, ST_SCORE)
                            act.wait_ge(s_sub, 4 * L + 4 * b + 2 * t + 2)
                            act.activation(prob[t][:, :, :], prob[t][:, :, :], ACT.Exp, scale=float(HD) ** -0.5).then_inc(s_exp, 1)

                        def mask_keys(b, first, end):
                            if first == 0:
                                ge(act, s_mm, 4 * L + 4 * (b - 1) + 4)
                                act.wait_ge(qk_sb, 6 * L + 6 * b + QK_SB[2])
                            if first == 3:
                                act.wait_ge(qk_sb, 6 * L + 6 * b + QK_SB[5])
                            for n in KBD_ACT[first:end]:
                                g = group_of(n)
                                M = (GROUPS[g][1] - GROUPS[g][0]) * HD
                                act.activation(kbd[0:M, n, :], kT[0:M, g, :], ACT.Copy,
                                               scale=head_mask[0:M, n:n + 1]).then_inc(kbd_act, 1)
                        if live[ST_SCORE]:
                            exps(0)
                        if live[ST_PROJ]:
                            b, _ = blk(h, par, ST_PROJ)
                            for t in range(2):
                                ts = slice(t * P, (t + 1) * P)
                                ge(act, pj_mm, 2 * L + 2 * (b - 1) + t + 1)
                                act.wait_ge(ot_sb, 2 * L + 2 * b + t + 1)
                                act.activation(os5[:, 0:2, ts], oT[t][:, 0:2, :], ACT.Copy).then_inc(os_hi, 1)
                                act.activation(os5[0:3 * TAIL, 4, ts], oT[t][0:3 * TAIL, 2, :], ACT.Copy).then_inc(os_hi, 1)
                        if live[ST_GATE]:
                            b, _ = blk(h, par, ST_GATE)
                            for t in range(2):
                                act.wait_ge(ln_v[1], 2 * L + 2 * b + t + 1)
                                act.activation(HT[:, :, bass.ds(b * BLK + t * P, P)], u[1][t][:, :, :], ACT.Copy).then_inc(ht_done, 1)
                        if live[ST_QK]:
                            b, i = blk(h, par, ST_QK)
                            ge(act, s_mm, 4 * L + 4 * (b - 2) + 4)
                            ge(act, kbd_done, L + b)
                            ge(act, kbd_pool, L + b)
                            for n, item in enumerate(QK_ITEMS):
                                act.wait_ge(qk_mm, 5 * L + 5 * b + n + 1)
                                for q, g, p0 in item:
                                    M = (GROUPS[g][1] - GROUPS[g][0]) * HD
                                    dst = (qT[i] if q == Q_ else kT)[0:M, g, :]
                                    act.activation(dst, gemm[(n + 1) % 2][p0:p0 + M, 0:BLK], ACT.Identity,
                                                   bias=bqk[l][p0:p0 + M, 3 * q + g:3 * q + g + 1]).then_inc(qk_sb, 1)
                                if n in (2, 3):
                                    mask_keys(b, n - 2, n - 1)
                            ge(act, pv_mm, 2 * L + 2 * (b - 2) + 2)
                            for t in range(2):
                                act.wait_ge(v_mm, 2 * L + 2 * b + t + 1)
                                vals = gemm[t][:, 0:D].rearrange("p (h o d) -> p h o d", o=2, d=HD)
                                for half in range(2):
                                    for odd in range(2):
                                        act.activation(
                                            vbd[i][odd * SEQ:(odd + 1) * SEQ, 2 * t + half, :, odd * VW:odd * VW + HD],
                                            vals[half * SEQ:(half + 1) * SEQ, :, odd, :], ACT.Copy).then_inc(v_sb, 1)
                            mask_keys(b, 2, 3)
                            mask_keys(b, 3, len(KBD_ACT))
                        if live[ST_SCORE]:
                            exps(1)

                    def next_weights():
                        for c in range(SLICES):
                            split_w1_hi(act, ph + 1, c)

                    def ada_out_of_HT():
                        if l == 0:
                            act.wait_ge(gates_out[0], 32)
                            act.wait_ge(gates_out[1], 32)
                    steps(act, body, {DEPTH - 1: ada_out_of_HT, NB + ST_PROJ - 1: next_weights})

                @block.vector
                def _(dve):
                    def value_bias():
                        dve.wait_ge(small_in[l], 16 * SMALL + 32 * l)
                        dve.memset(onesr[:, :], 1.0).then_inc(bv_done, 1)
                        dve.wait_ge(bv_done, 4 * l + 1)
                        for s in range(3):
                            rows = P if s < 2 else 3 * TAIL
                            dve.tensor_scalar(bvB[0:rows, s, :], onesr[0:rows, :], bv[0:rows, l, s:s + 1], None, ALU.mult).then_inc(bv_done, 1)

                    def proj_bias():
                        dve.wait_ge(bv_mm, l + 1)
                        dve.tensor_tensor(bproj_bc[l][:, :], bproj_bc[l][:, :], tbank[0][:, 0:D], ALU.add).then_inc(bp_done, 1)

                    def ln_statistics(bs):
                        for k, b in bs.items():
                            for t in range(2):
                                if k:
                                    dve.wait_ge(x_attn, 2 * L + 2 * b + t + 1)
                                if k and t and 0 in bs:
                                    dve.wait_ge(ln_stats[0], 2 * L + 2 * bs[0] + 2)
                                dve.bn_stats(out=stats[k][:, t, :], in_=tile(b, t)).then_inc(ln_stats[k], 1)
                        for k, b in bs.items():
                            if len(bs) == 1:
                                dve.wait_ge(ln_stats[k], 2 * L + 2 * b + 2)
                            for t in range(2):
                                dve.bn_aggr(out=meanvar[k][:, t, :], in_=stats[k][:, t, :]).then_inc(ln_mv[k], 1)
                            if k == 0 and 1 in bs:
                                dve.wait_ge(ln_stats[1], 2 * L + 2 * bs[1] + 2)
                            dve.wait_ge(ln_mv[k], 2 * L + 2 * b + 2)
                            dve.tensor_scalar(vareps[k][:, :], meanvar[k][:, :, 1], EPS, None, ALU.add).then_inc(ln_ve[k], 1)

                    def ln_normalize(k, b):
                        dve.wait_ge(ln_rstd[k], L + b + 1)
                        for t in range(2):
                            if k == 0:
                                ge(dve, h_lo, 4 * L + 4 * (b - 1) + 2 * t + 2)
                            else:
                                ge(dve, ht_done, 2 * L + 2 * (b - 1) + t + 1)
                                if l:
                                    ge(dve, lg_mm, 2 * (b - 1) + t + 1)
                            xn = u[k][t][:, :, :].rearrange("p s k -> p (s k)")
                            dve.tensor_scalar(xn[:, 0:2 * P], X[:, bass.ds(2 * b + t, 1), 0:2 * P].rearrange("p o c -> p (o c)"),
                                              meanvar[k][:, t, 0:1], rstd[k][:, t:t + 1], ALU.subtract, ALU.mult).then_inc(ln_xn[k], 1)
                            dve.tensor_scalar(xn[:, 2 * P:XCOLS].rearrange("p (r c) -> p r c", r=REP),
                                              X[:, bass.ds(2 * b + t, 1), 2 * P:D].to_broadcast([P, REP, TAIL]),
                                              meanvar[k][:, t, 0:1], rstd[k][:, t:t + 1], ALU.subtract, ALU.mult).then_inc(ln_xn[k], 1)

                    def ln_scale(k, b):
                        for t in range(2):
                            dve.wait_ge(ln_T[k], 2 * L + 2 * b + t + 1)
                            dve.tensor_tensor(u[k][t][:, :, :].rearrange("p s (q k) -> p s q k", q=2),
                                              slots((tbank if k else gemm)[t][:, 0:3 * P]),
                                              seq_mod(l, 2 * k + 1, b, t), ALU.mult).then_inc(ln_u[k], 1)

                    def softmax_shift(b, t):
                        for c in range(2):
                            heads = slice(c * BANK_HEADS, (c + 1) * BANK_HEADS)
                            sc = scores[:, c * 512:(c + 1) * 512].rearrange("p (h k) -> p h k", k=SEQ)
                            dve.wait_ge(s_mm, 4 * L + 4 * b + 2 * t + c + 1)
                            dve.tensor_reduce(out=rowmax[t][:, heads], in_=sc, axis=AX.X, op=ALU.max).then_inc(s_max, 1)
                            dve.wait_ge(s_max, 4 * L + 4 * b + 2 * t + c + 1)
                            ge(dve, pt_mm, 4 * L + 4 * (b - 1) + 2 * t + c + 1)
                            dve.tensor_tensor(prob[t][:, heads, :], sc,
                                              rowmax[t][:, heads].unsqueeze(2).to_broadcast([P, BANK_HEADS, SEQ]),
                                              ALU.subtract).then_inc(s_sub, 1)

                    def body(h, par, live):
                        if live[ST_QK]:
                            ln_scale(0, blk(h, par, ST_QK)[0])
                        norms = {k: blk(h, par, st)[0] for k, st in enumerate((ST_LN1, ST_LN2)) if live[st]}
                        if live[ST_SCORE]:
                            softmax_shift(blk(h, par, ST_SCORE)[0], 0)
                        if live[ST_PROJ]:
                            b, _ = blk(h, par, ST_PROJ)
                            for t in range(2):
                                ge(dve, os_lo, 4 * L + 4 * (b - 1) + 2 * t + 2)
                                dve.wait_ge(ot_mm, 2 * L + 2 * b + t + 1)
                                dve.tensor_copy(oT[t][:, :, :].rearrange("p s k -> p (s k)"), tbank[t][:, 0:3 * P]).then_inc(ot_sb, 1)
                        if norms:
                            ln_statistics(norms)
                        if live[ST_SCORE]:
                            softmax_shift(blk(h, par, ST_SCORE)[0], 1)
                        if live[ST_PV]:
                            b, _ = blk(h, par, ST_PV)
                            for t in range(2):
                                dve.wait_ge(pv_mm, 2 * L + 2 * b + t + 1)
                                res = tbank[t][:, 0:HEADS * VW].rearrange("p (h d) -> p h d", d=VW)
                                dve.reciprocal(rden[t][:, :], res[:, :, HD]).then_inc(o_rec, 1)
                                dve.wait_ge(o_rec, 2 * L + 2 * b + t + 1)
                                ge(dve, ot_mm, 2 * L + 2 * (b - 1) + t + 1)
                                dve.tensor_tensor(o[t][:, 0:D].rearrange("p (h d) -> p h d", d=HD), res[:, :, 0:HD],
                                                  rden[t][:, :].unsqueeze(2).to_broadcast([P, HEADS, HD]), ALU.mult).then_inc(o_norm, 1)
                                dve.wait_ge(o_norm, 2 * L + 2 * b + t + 1)
                                dve.tensor_copy(o[t][:, D:XCOLS].rearrange("p (r c) -> p r c", r=REP - 1),
                                                o[t][:, 2 * P:D].unsqueeze(1).to_broadcast([P, REP - 1, TAIL])).then_inc(o_full, 1)
                        if live[ST_QK]:
                            b, _ = blk(h, par, ST_QK)
                            dve.wait_ge(qk_sb, 6 * L + 6 * b + QK_SB[1])
                            ge(dve, s_mm, 4 * L + 4 * (b - 1) + 4)
                            mask_heads(dve, *KBD_DVE).then_inc(kbd_done, 1)
                        if l and live[ST_GATE]:
                            b, _ = blk(h, par, ST_GATE)
                            for t in range(2):
                                dve.wait_ge(lg_mm, 2 * b + t + 1)
                                dve.tensor_copy(logits[:, bass.ds(2 * b + t, 1), :].rearrange("p o e -> p (o e)"),
                                                tbank[t][:, 0:EXPERTS]).then_inc(lg_sb, 1)

                        def projection(t):
                            b, _ = blk(h, par, ST_PROJ)
                            ge(dve, x_attn, 2 * L + 2 * (b - 1) + t + 1)
                            dve.wait_ge(pj_mm, 2 * L + 2 * b + t + 1)
                            dve.tensor_tensor(y[t][:, :], tbank[t][:, 0:D], bproj_bc[l][:, :], ALU.add).then_inc(y_bias, 1)
                        if 0 in norms:
                            ln_normalize(0, norms[0])
                        if live[ST_PROJ]:
                            projection(0)
                        if 1 in norms:
                            ln_normalize(1, norms[1])
                        if live[ST_PROJ]:
                            projection(1)
                        if live[ST_LN2]:
                            ln_scale(1, blk(h, par, ST_LN2)[0])

                    def rest_of_x():
                        if l == 0:
                            dve.wait_ge(x_rest, 48)

                    def next_weights(c):
                        return lambda: split_w1_lo(dve, ph + 1, c)
                    if l == 0:
                        dve.wait_ge(x_first, 16)
                    value_bias()
                    after = {1: proj_bias, 3: rest_of_x}
                    for c in range(SLICES):
                        after[NB + ST_PROJ - 1 + c] = next_weights(c)
                    steps(dve, body, after)

                @block.tensor
                def _(pe):
                    w5 = w1[0]
                    pe.wait_ge(w2_done, 4 * (l + 1))

                    def proj_bias():
                        pe.wait_ge(bv_done, 4 * l + 4)
                        for n, (s, ws, rows) in enumerate(((0, 0, P), (0, 2, P), (1, 1, P), (1, 3, P), (2, 4, 3 * TAIL))):
                            mm = pe.matmul(tbank[0][:, 0:D], bvB[0:rows, s, :], w5[0:rows, ws, 3 * D:HID].bitcast(F32),
                                           start=(n == 0), stop=(n == 4))
                        mm.then_inc(bv_mm, 1)

                    def proj_bias_read():
                        pe.wait_ge(bp_done, l + 1)

                    def transposes(src, dst):
                        for s in range(3):
                            mm = pe.transpose(dst[:, s * P:(s + 1) * P], src[:, s * P:(s + 1) * P], ident[:, :])
                        return mm

                    def score(h, par, t):
                        b, i = blk(h, par, ST_SCORE)
                        pe.wait_ge(kbd_done, L + b + 1)
                        pe.wait_ge(kbd_act, len(KBD_ACT) * (L + b + 1))
                        pe.wait_ge(kbd_pool, L + b + 1)
                        for c, parts in enumerate(SCORE_PARTS):
                            ge(pe, s_sub, 4 * L + 4 * b + 2 * t + c - 1)
                            for g, h0, h1 in parts:
                                M = (GROUPS[g][1] - GROUPS[g][0]) * HD
                                for half in range(2):
                                    js = slice((2 * t + half) * SEQ, (2 * t + half + 1) * SEQ)
                                    mm = pe.matmul(scores[half * SEQ:(half + 1) * SEQ, h0 * SEQ:h1 * SEQ],
                                                   qT[i][0:M, g, js], kbd[0:M, h0:h1, js], start=True, stop=True)
                            mm.then_inc(s_mm, 1)

                    def prob_transposes(h, par, t):
                        b, _ = blk(h, par, ST_PV)
                        pe.wait_ge(s_exp, 2 * L + 2 * b + t + 1)
                        pairs = prob[t][:, :, :].rearrange("p h k -> p (h k)")
                        for c in range(2):
                            ge(pe, pt_sb, 4 * L + 4 * b + 2 * t + c - 1)
                            for q in range(4):
                                n = 4 * c + q
                                mm = pe.transpose(probT_ps[:, n * P:(n + 1) * P], pairs[:, n * P:(n + 1) * P], ident[:, :])
                            mm.then_inc(pt_mm, 1)

                    def body(h, par, live):
                        if live[ST_SCORE]:
                            score(h, par, 0)
                        if live[ST_PV]:
                            prob_transposes(h, par, 0)
                        if live[ST_PROJ]:
                            b, _ = blk(h, par, ST_PROJ)
                            for t in range(2):
                                pe.wait_ge(o_full, 2 * L + 2 * b + t + 1)
                                tbank_free(pe, h, par, live, OT, t)
                                transposes(o[t], tbank[t]).then_inc(ot_mm, 1)
                        if live[ST_PV]:
                            prob_transposes(h, par, 1)
                        if live[ST_SCORE]:
                            score(h, par, 1)
                        if live[ST_PV]:
                            b, i = blk(h, par, ST_PV)
                            pe.wait_ge(v_sb, 8 * L + 8 * b + 8)
                            for t in range(2):
                                pe.wait_ge(pt_sb, 4 * L + 4 * b + 2 * t + 2)
                                tbank_free(pe, h, par, live, PV, t)
                                for n in range(HEADS // 2):
                                    for half in range(2):
                                        mm = pe.matmul(tbank[t][half * SEQ:(half + 1) * SEQ, n * 2 * VW:(n + 1) * 2 * VW],
                                                       probT[t][:, n * P + half * SEQ:n * P + (half + 1) * SEQ],
                                                       vbd[i][:, 2 * t + half, n, :], start=True, stop=True)
                                mm.then_inc(pv_mm, 1)
                        if live[ST_QK]:
                            b, i = blk(h, par, ST_QK)
                            pe.wait_ge(h_lo, 4 * L + 4 * b + 4)
                            for n, item in enumerate(QK_ITEMS):
                                if n >= 2:
                                    pe.wait_ge(qk_sb, 6 * L + 6 * b + QK_SB[n - 1])
                                q, g, _ = item[0]
                                h0, h1 = GROUPS[g]
                                M, c0 = (h1 - h0) * HD, q * D + h0 * HD
                                if len(item) == 1:
                                    mm = seven(pe, gemm[(n + 1) % 2][0:M, 0:BLK], lambda s, r: w5[0:r, s, c0:c0 + M],
                                               lambda s, r: hs[i][0:r, s, :], True)
                                else:
                                    mm = seven(pe, gemm[(n + 1) % 2][0:M2, 0:BLK], lambda s, r: wqk2[0:r, s, :],
                                               lambda s, r: hs[i][0:r, s, :], True)
                                mm.then_inc(qk_mm, 1)
                        if l and live[ST_GATE]:
                            b, _ = blk(h, par, ST_GATE)
                            for t in range(2):
                                pe.wait_ge(ln_v[1], 2 * L + 2 * b + t + 1)
                                tbank_free(pe, h, par, live, GATE, t)
                                for s, rows in enumerate((P, P, TAIL)):
                                    mm = pe.matmul(tbank[t][:, 0:EXPERTS], u[1][t][0:rows, s, :], wg[0:rows, s, :],
                                                   start=(s == 0), stop=(s == 2))
                                mm.then_inc(lg_mm, 1)
                        for t in range(2):
                            ts = slice(t * P, (t + 1) * P)
                            if live[ST_QK]:
                                b, i = blk(h, par, ST_QK)
                                pe.wait_ge(qk_sb, 6 * L + 6 * b + QK_SB[4 + t])
                                seven(pe, gemm[t][:, 0:D], lambda s, r: hs[i][0:r, s, ts],
                                      lambda s, r: w5[0:r, s, 2 * D:3 * D], False).then_inc(v_mm, 1)
                            if live[ST_PROJ]:
                                b, _ = blk(h, par, ST_PROJ)
                                pe.wait_ge(os_lo, 4 * L + 4 * b + 2 * t + 2)
                                tbank_free(pe, h, par, live, PROJ, t)
                                seven(pe, tbank[t][:, 0:D], lambda s, r: os5[0:r, s, ts],
                                      lambda s, r: w5[0:r, s, 3 * D:HID], False).then_inc(pj_mm, 1)
                        if live[ST_LN1]:
                            b, _ = blk(h, par, ST_LN1)
                            for t in range(2):
                                pe.wait_ge(ln_xn[0], 4 * L + 4 * b + 2 * t + 2)
                                if live[ST_QK]:
                                    pe.wait_ge(v_sb, 8 * L + 8 * (b - 1) + 4 * t + 4)
                                transposes(u[0][t][:, :, :].rearrange("p s k -> p (s k)"), gemm[t]).then_inc(ln_T[0], 1)
                        if live[ST_LN2]:
                            b, _ = blk(h, par, ST_LN2)
                            for t in range(2):
                                pe.wait_ge(ln_xn[1], 4 * L + 4 * b + 2 * t + 2)
                                tbank_free(pe, h, par, live, LN2, t)
                                transposes(u[1][t][:, :, :].rearrange("p s k -> p (s k)"), tbank[t]).then_inc(ln_T[1], 1)
                    steps(pe, body, {0: proj_bias, 2: proj_bias_read})

        def mlp(passes):
            l = min(passes[0], 1)

            def steps(eng, body):
                for g in passes:
                    body(g, 0, 0)
                    body(g, 1, 1)
                    body(g, 2, 0)
                    with eng.Fori(2, NB // 2) as h:
                        body(g, 2 * h - 1, 1)
                        body(g, 2 * h, 0)
                    body(g, NB - 1, 1)

            def before(g, b):
                if isinstance(b, int) and b == 0:
                    return (g - 1, NB - 1) if g - 1 in passes else None
                return g, b - 1

            def behind(g, b):
                if isinstance(b, int) and b == NB - 1:
                    return (g + 1, 0) if g + 1 in passes else None
                return g, b + 1

            def splits_next(g, b, m):
                return isinstance(b, int) and b == 2 and m % SLICES == 0 and g < PASSES_MLP - 1

            with nc.Block() as block:
                @block.sync
                def _(sp):
                    for g in passes:
                        ph, N = phase_of_mlp(g), NB * g

                        def gates(b, par):
                            if not (isinstance(b, int) and b < 2 and g == passes[0]):
                                sp.wait_ge(x_mlp, 2 * N + 2 * (b - 2) + 2)
                            gate_load(sp, l, 1, b, par)
                        gates(0, 0)
                        if ph < 6:
                            if g > 1:
                                sp.wait_ge(f1_mm, MCH * N)
                            sp.wait_ge(w_lo, SPLIT * (ph + 1))
                            load_w1(sp, ph + 1)
                            load_w1C(sp, ph + 1)
                        gates(1, 1)
                        if 0 < g < PASSES_MLP - 1:
                            sp.wait_ge(gelu_sb, MCH * N)
                            sp.wait_ge(z_bias, 2 * N)
                            load_mlp_bias(sp, g + 1)
                            sp.wait_ge(wd_lo, MCH * (g + 1))
                            load_wdn(sp, g + 1)

                        def store(b):
                            sp.dma_start(out.rearrange("(t p) c -> p t c", p=P)[:, bass.ds(2 * b, 2), :],
                                         X[:, bass.ds(2 * b, 2), :]).then_inc(out_done, 16)
                        with sp.Fori(1, NB // 2) as h:
                            for par in range(2):
                                gates(2 * h + par, par)
                                if g == PASSES_MLP - 1:
                                    store(2 * h + par - 2)
                        if g == PASSES_MLP - 1:
                            for b in (NB - 2, NB - 1):
                                sp.wait_ge(x_mlp, 2 * N + 2 * b + 2)
                                store(b)
                            sp.wait_ge(out_done, 16 * NB)

                @block.gpsimd
                def _(pool):
                    for g in passes:
                        N = NB * g
                        with pool.Fori(0, NB // 2) as h:
                            for par in range(2):
                                b = 2 * h + par
                                for t in range(2):
                                    pool.wait_ge(z_gate, 2 * N + 2 * b + t + 1)
                                    pool.tensor_tensor(tile(b, t), tile(b, t), y[t][:, :], ALU.add).then_inc(x_mlp, 1)

                @block.scalar
                def _(act):
                    def split(g, b, i):
                        N = NB * g
                        ge(act, f1_mm, MCH * N + MCH * (b - 1))
                        cols = bass.ds(b * BLK, BLK)
                        act.activation(hs[i][:, 0:2, :], HT[:, 0:2, cols], ACT.Copy).then_inc(m_hi, 1)
                        act.activation(hs[i][0:3 * TAIL, 4, :], HT[0:3 * TAIL, 2, cols], ACT.Copy).then_inc(m_hi, 1)
                    split(passes[0], 0, 0)
                    act.activation(warm[:, 1:2], mhalf[:, 1:2], ACT.Gelu_apprx_tanh)

                    def body(g, b, i):
                        first = isinstance(b, int) and b == 0
                        if first:
                            act.wait_ge(bias_in[g % 2], 32 * (g // 2 + 1))
                            act.wait_ge(wdn_in, 16 * (g + 1))
                        for m in range(MCH):
                            n = MCH * NB * g + MCH * b + m
                            act.wait_ge(f1_mm, n + 1)
                            ge(act, g_lo, n - 2)
                            act.activation(gel[m % 3][:, :], up_ps[m % 3], ACT.Gelu_apprx_tanh, bias=bup[g % 2][:, m:m + 1]).then_inc(gelu_sb, 1)
                            if first:
                                ge(act, f2_mm, MCH * (NB * g - 1) + m + 1)
                                act.activation(wdn[0][:, m, :], wraw[:, m, :], ACT.Copy).then_inc(wd_hi, 1)
                            if splits_next(g, b, m):
                                split_w1_hi(act, phase_of_mlp(g) + 1, m // SLICES)
                            if m == 4 and behind(g, b):
                                split(*behind(g, b), 1 - i)
                            if m == 3 and g == 1 and first:
                                act.wait_ge(route, 1)
                                act.activation(esel[:, :, :], esel[:, :, :], ACT.Exp).then_inc(route_e, 1)
                    steps(act, body)

                @block.vector
                def _(dve):
                    def split(g, b, i):
                        N = NB * g
                        dve.wait_ge(m_hi, 2 * N + 2 * b + 2)
                        cols = bass.ds(b * BLK, BLK)
                        dve.tensor_tensor(hs[i][:, 2:4, :], HT[:, 0:2, cols], hs[i][:, 0:2, :].bitcast(F32), ALU.subtract).then_inc(m_lo, 1)
                        low = hs[i][TAIL:2 * TAIL, 4, :]
                        dve.tensor_tensor(low, HT[TAIL:2 * TAIL, 2, cols], low.bitcast(F32), ALU.subtract).then_inc(m_lo, 1)
                    split(passes[0], 0, 0)

                    def evacuate(g, b, i):
                        N, ph = NB * g, phase_of_mlp(g)
                        for t in range(2):
                            if t == 0:
                                dve.wait_ge(f2_mm, MCH * N + MCH * b + MCH)
                            ge(dve, x_mlp, 2 * N + 2 * (b - 1) + t + 1)
                            dve.tensor_tensor(y[t][:, :], down_ps[i][t][:, 0:D], bdown_bc[g % 2][:, :], ALU.add).then_inc(z_bias, 1)
                        dve.wait_ge(gate_in[i], 256 * ph + 16 * (b - i) + 32)
                        for t in range(2):
                            dve.wait_ge(z_bias, 2 * N + 2 * b + t + 1)
                            if g == 0:
                                dve.tensor_tensor(y[t][:, :], y[t][:, :], gate_bc[i][:, t, :], ALU.mult).then_inc(z_gate, 1)
                            else:
                                weight = cw[:, bass.ds(2 * b + t, 1), g - 1]
                                dve.scalar_tensor_tensor(out=y[t][:, :], in0=y[t][:, :], scalar=weight,
                                                         in1=gate_bc[i][:, t, :], op0=ALU.mult, op1=ALU.mult).then_inc(z_gate, 1)

                    def body(g, b, i):
                        first = isinstance(b, int) and b == 0
                        for m in range(MCH):
                            n = MCH * NB * g + MCH * b + m
                            r = m % 3
                            dve.wait_ge(gelu_sb, n + 1)
                            ge(dve, f2_mm, n - 2)
                            dve.tensor_copy(gelu_hi[r][:, :], gel[r][:, :]).then_inc(g_hi, 1)
                            dve.wait_ge(g_hi, n + 1)
                            dve.tensor_tensor(gelu_lo[r][:, :], gel[r][:, :], gelu_hi[r][:, :].bitcast(F32), ALU.subtract).then_inc(g_lo, 1)
                            if first:
                                dve.wait_ge(wd_hi, MCH * g + m + 1)
                                dve.tensor_tensor(wdn[1][:, m, :], wraw[:, m, :], wdn[0][:, m, :].bitcast(F32), ALU.subtract).then_inc(wd_lo, 1)
                            if g == 1 and first:
                                routing(dve, m)
                            if splits_next(g, b, m):
                                split_w1_lo(dve, phase_of_mlp(g) + 1, m // SLICES)
                            if m == 2:
                                if isinstance(b, int) and b == 1:
                                    dve.wait_ge(bias_in[g % 2], 32 * (g // 2 + 1))
                                if before(g, b):
                                    evacuate(*before(g, b), 1 - i)
                            if m == 5 and behind(g, b):
                                split(*behind(g, b), 1 - i)
                    steps(dve, body)
                    evacuate(passes[-1], NB - 1, 1)

                @block.tensor
                def _(pe):
                    def up(g, b, i, m):
                        N, ph = NB * g, phase_of_mlp(g)
                        n = MCH * N + MCH * b + m
                        if m == 0:
                            pe.wait_ge(m_lo, 2 * N + 2 * b + 2)
                        ge(pe, gelu_sb, n - 2)
                        seven(pe, up_ps[m % 3], lambda s, r: w1[ph % 2][0:r, s, m * P:(m + 1) * P],
                              lambda s, r: hs[i][0:r, s, :], True).then_inc(f1_mm, 1)

                    def down(g, b, i, m):
                        N = NB * g
                        n = MCH * N + MCH * b + m
                        if m == 0:
                            ge(pe, z_bias, 2 * N + 2 * (b - 2) + 2)
                        pe.wait_ge(g_lo, n + 1)
                        if isinstance(b, int) and b == 0:
                            pe.wait_ge(wd_lo, MCH * g + m + 1)
                        for t in range(2):
                            ts = slice(t * P, (t + 1) * P)
                            for q, (a, w) in enumerate(((gelu_hi, 0), (gelu_hi, 1), (gelu_lo, 0))):
                                mm = pe.matmul(down_ps[i][t][:, 0:D], a[m % 3][:, ts], wdn[w][:, m, :],
                                               start=(m == 0 and q == 0), stop=(m == MCH - 1 and q == 2))
                        mm.then_inc(f2_mm, 1)

                    def body(g, b, i):
                        if isinstance(b, int) and b == 0:
                            pe.wait_ge(w_lo, SPLIT * (phase_of_mlp(g) + 1))
                        for m in range(MCH):
                            up(g, b, i, m)
                            if m >= 2:
                                down(g, b, i, m - 2)
                            elif before(g, b):
                                down(*before(g, b), 1 - i, MCH - 2 + m)
                    steps(pe, body)
                    down(passes[-1], NB - 1, 1, MCH - 2)
                    down(passes[-1], NB - 1, 1, MCH - 1)

        route_steps = [0]

        def routing(dve, m):
            def link(op):
                op.then_inc(route_step, 1)
                route_steps[0] += 1
                dve.wait_ge(route_step, route_steps[0])

            if m == 0:
                link(dve.tensor_reduce(out=lmax[:, :], in_=logits[:, :, :], axis=AX.X, op=ALU.max))
                dve.tensor_tensor(esel[:, :, :], logits[:, :, :], lmax[:, :].unsqueeze(2).to_broadcast([P, TILES, EXPERTS]),
                                  ALU.subtract).then_inc(route, 1)
                link(dve.memset(rank[:, :, :], 0.0))
            elif m < EXPERTS:
                j = m - 1
                n = EXPERTS - 1 - j
                wins = cmp[:, :, 0:n]
                link(dve.tensor_tensor(wins, logits[:, :, j:j + 1].to_broadcast([P, TILES, n]), logits[:, :, j + 1:EXPERTS], ALU.is_ge))
                link(dve.tensor_tensor(rank[:, :, j + 1:EXPERTS], rank[:, :, j + 1:EXPERTS], wins, ALU.add))
                link(dve.tensor_reduce(out=ncmp[:, :], in_=wins, axis=AX.X, op=ALU.add))
                link(dve.tensor_tensor(rank[:, :, j], rank[:, :, j], ncmp[:, :], ALU.subtract))
            elif m in (5, 6):
                dve.wait_ge(route_e, 1)
                for e in (2 * (m - 5), 2 * (m - 5) + 1):
                    link(dve.tensor_scalar(ncmp[:, :], rank[:, :, e], 2.0 - (EXPERTS - 1 - e), None, ALU.is_lt))
                    link(dve.tensor_tensor(esel[:, :, e], esel[:, :, e], ncmp[:, :], ALU.mult))
            elif m == 8:
                link(dve.tensor_reduce(out=esum[:, :], in_=esel[:, :, :], axis=AX.X, op=ALU.add))
                link(dve.reciprocal(lmax[:, :], esum[:, :]))
                link(dve.tensor_tensor(cw[:, :, :], esel[:, :, :], lmax[:, :].unsqueeze(2).to_broadcast([P, TILES, EXPERTS]), ALU.mult))

        attention(0)
        mlp([0])
        attention(1)
        mlp(list(range(1, PASSES_MLP)))


def kernel(x, cond_1152, L0_cond_w_qkv, L0_cond_b_qkv, L0_cond_w_proj, L0_cond_b_proj, L0_cond_w_fc1,
           L0_cond_b_fc1, L0_cond_w_fc2, L0_cond_b_fc2, L0_cond_w_ada, L0_cond_b_ada, L1_cond_w_adaln,
           L1_cond_b_adaln, L1_cond_w_qkv, L1_cond_b_qkv, L1_cond_w_proj, L1_cond_b_proj, L1_cond_w_gate,
           L1_cond_w1, L1_cond_b1, L1_cond_w2, L1_cond_b2):
    import numpy as np
    import concourse.bacc as bacc
    from concourse.bass_utils import run_bass_kernel_spmd

    nc = bacc.Bacc("TRN2", target_bir_lowering=False, num_devices=1)
    arrays = {}

    def given(name, a, shape=None):
        a = np.ascontiguousarray(a)
        if shape is not None:
            a = a.reshape(shape)
        arrays[name] = a
        return nc.dram_tensor(name, a.shape, mybir.dt.from_np(a.dtype), kind="ExternalInput").ap()

    tokens = NSEQ * SEQ
    w1 = given("w1", L1_cond_w1)
    b1 = given("b1", L1_cond_b1)
    w2 = given("w2", L1_cond_w2)
    b2 = given("b2", L1_cond_b2)
    result = nc.dram_tensor("result", (tokens, D), F32, kind="ExternalOutput").ap()
    build(
        nc,
        given("tokens", x, (tokens, D)),
        given("cond", cond_1152),
        [given("w_qkv0", L0_cond_w_qkv), given("w_qkv1", L1_cond_w_qkv)],
        [given("b_qkv0", L0_cond_b_qkv), given("b_qkv1", L1_cond_b_qkv)],
        [given("w_proj0", L0_cond_w_proj), given("w_proj1", L1_cond_w_proj)],
        [given("b_proj0", L0_cond_b_proj), given("b_proj1", L1_cond_b_proj)],
        [given("w_fc1", L0_cond_w_fc1)] + [w1[e] for e in range(EXPERTS)],
        [given("b_fc1", L0_cond_b_fc1)] + [b1[e] for e in range(EXPERTS)],
        [given("w_fc2", L0_cond_w_fc2)] + [w2[e] for e in range(EXPERTS)],
        [given("b_fc2", L0_cond_b_fc2)] + [b2[e] for e in range(EXPERTS)],
        [given("w_ada0", L0_cond_w_ada), given("w_ada1", L1_cond_w_adaln)],
        [given("b_ada0", L0_cond_b_ada), given("b_ada1", L1_cond_b_adaln)],
        given("w_gate", L1_cond_w_gate),
        result,
    )
    r = run_bass_kernel_spmd(nc, [arrays], core_ids=[0])
    return r.results[0]["result"].reshape(NSEQ, SEQ, D)
```
